# Optimizing a Trainium2 kernel written in Bass

```python
import numpy as np
import jax
import jax.numpy as jnp

def _softmax(x, axis=-1):
    return jax.nn.softmax(x, axis=axis)

def _gelu(x):
    return jax.nn.gelu(x, approximate=True)

def _silu(x):
    return jax.nn.silu(x)

def _sigmoid(x):
    return jax.nn.sigmoid(x)

def _layernorm(x, axis=-1, eps=1e-05):
    m = jnp.mean(x, axis=axis, keepdims=True)
    v = jnp.var(x, axis=axis, keepdims=True)
    return (x - m) / jnp.sqrt(v + eps)

def _scatter_add(tgt, idx, src, axis=0):
    return tgt.at[idx].add(src)

def _segment_sum(src, seg, n):
    return jax.ops.segment_sum(src, seg, n)
kernel_name = 'mk_flamingo_gated_d2_seqx_r8_92273a'

def setup_inputs(seed: int=0):
    np.random.seed(seed)
    _w = jnp.asarray

    def _rec_inputs():
        import jax
        import jax.numpy as jnp
        _rk = jax.random.key(seed)
        x = -0.0002928 + 1 * jax.random.normal(jax.random.fold_in(_rk, 1), (128, 64, 128), jnp.float32)
        _lenS = 64 - jax.random.randint(jax.random.fold_in(_rk, 7), (128,), 0, max(1, 64 // 4) + 1, jnp.int32)
        _lenS2 = 64 - jax.random.randint(jax.random.fold_in(_rk, 8), (128,), 0, max(1, 64 // 4) + 1, jnp.int32)
        _ctx_1024P = jax.random.normal(jax.random.fold_in(_rk, 11), (128, 16, 128), jnp.float32)
        _ctx_1024c = jax.random.dirichlet(jax.random.fold_in(_rk, 511), 0.3 * jnp.ones((16,), jnp.float32), (128, 64))
        _ctx_1024t = jnp.einsum('bsk,bkd->bsd', _ctx_1024c, _ctx_1024P)
        _ctx_1024t = _ctx_1024t * jax.lax.rsqrt(jnp.mean(jnp.square(_ctx_1024t)) + 1e-12) * 0.953939
        ctx_1024 = -1.39393e-06 + 0.999914 * (_ctx_1024t + 0.3 * jax.random.normal(jax.random.fold_in(_rk, 611), (128, 64, 128), jnp.float32))
        fside_1xSxS2_0 = 0.000675642 + 1.00031 * jax.random.normal(jax.random.fold_in(_rk, 12), (1, 64, 64), jnp.float32)
        _g = jax.random.normal(jax.random.fold_in(_rk, 9001), (2, 2), jnp.float32)
        _g = jnp.sign(_g) * jnp.maximum(jnp.abs(_g), 1.0) + (_g == 0) * 1.0
        g_xattn = _g[0]
        g_ffn = _g[1]
        return (x, ctx_1024, fside_1xSxS2_0, g_xattn, g_ffn)
    x, ctx_1024, fside_1xSxS2_0, g_xattn, g_ffn = _rec_inputs()

    def _L0_xattn_setup():
        import jax, jax.numpy as jnp
        import numpy as np
        B, S, E, NH = (2, 256, 128, 4)
        HD = E // NH

        def _mlstm_head(q, k, v, ig, fg, eps=1e-06):
            s, dh = q.shape
            log_f = jax.nn.log_sigmoid(fg)
            cs = jnp.concatenate([jnp.zeros((1, 1), log_f.dtype), jnp.cumsum(log_f, axis=0)], axis=0)
            neg = jnp.asarray(-0.7 * jnp.finfo(cs.dtype).max, cs.dtype)
            log_d = jnp.where(jnp.tri(s, dtype=bool), (cs - cs.T)[1:, 1:] + ig.T, neg)
            m = jnp.max(log_d, axis=-1, keepdims=True)
            d = jnp.exp(log_d - m)
            c = q @ (k.T / jnp.sqrt(dh)) * d
            n = jnp.maximum(jnp.sum(c, axis=-1, keepdims=True), jnp.exp(-m))
            return c / (n + eps) @ v
        key = jax.random.key(seed)
        ks = jax.random.split(key, 8)
        return {'q': jax.random.normal(ks[0], (B, S, E), jnp.float32), 'k': jax.random.normal(ks[1], (B, S, E), jnp.float32), 'v': jax.random.normal(ks[2], (B, S, E), jnp.float32), 'igate_kernel': jax.random.normal(ks[3], (3 * E, NH), jnp.float32) * 0.02, 'igate_bias': jax.random.normal(ks[4], (NH,), jnp.float32) * 0.1, 'fgate_kernel': jax.random.normal(ks[5], (3 * E, NH), jnp.float32) * 0.02, 'fgate_bias': jnp.linspace(3.0, 6.0, NH, dtype=jnp.float32), 'rms_scale': jax.random.normal(ks[6], (HD,), jnp.float32) * 0.02}
    _L0_xattn_all = _L0_xattn_setup()
    _L0_xattn_in = {k: v for k, v in _L0_xattn_all.items() if k in ('igate_kernel', 'igate_bias', 'fgate_kernel', 'fgate_bias', 'rms_scale')}
    del _L0_xattn_all

    def _L0_ffn_setup():
        import jax, jax.numpy as jnp
        import numpy as np
        key = jax.random.key(seed)
        ks = jax.random.split(key, 4)
        B, T, M, E, F = (4, 256, 128, 8, 512)
        hidden_states = jax.random.normal(ks[0], (B, T, M), dtype=jnp.float32)
        wg = jax.random.normal(ks[1], (M, E), dtype=jnp.float32) * (1.0 / np.sqrt(M))
        w1 = jax.random.normal(ks[2], (E, M, F), dtype=jnp.float32) * (1.0 / np.sqrt(M))
        b1 = jnp.zeros((E, F), dtype=jnp.float32)
        w2 = jax.random.normal(ks[3], (E, F, M), dtype=jnp.float32) * (1.0 / np.sqrt(F))
        b2 = jnp.zeros((E, M), dtype=jnp.float32)
        return {'hidden_states': hidden_states, 'wg': wg, 'w1': w1, 'b1': b1, 'w2': w2, 'b2': b2}
    _L0_ffn_all = _L0_ffn_setup()
    _L0_ffn_in = {k: v for k, v in _L0_ffn_all.items() if k in ('wg', 'w1', 'b1', 'w2', 'b2')}
    del _L0_ffn_all

    def _L1_xattn_setup():
        import jax, jax.numpy as jnp
        import numpy as np
        import math
        D = 128
        B, S = (8, 256)

        def _proj(x, W1, b1, W2, b2):
            h = jnp.einsum('bsd,od->bso', x, W1) + b1
            return jnp.einsum('bsd,od->bso', h, W2) + b2
        key = jax.random.key(seed)
        ks = jax.random.split(key, 8)
        q = jax.random.normal(ks[0], (B, S, D), dtype=jnp.float32)
        k = jax.random.normal(ks[1], (B, S, D), dtype=jnp.float32)
        v1 = jax.random.normal(ks[2], (B, S, D), dtype=jnp.float32)
        mask = jax.random.normal(ks[3], (1, S, S), dtype=jnp.float32)
        lim = 1.0 / math.sqrt(D)
        W1 = jax.random.uniform(ks[4], (D, D), jnp.float32, -lim, lim)
        b1 = jax.random.uniform(ks[5], (D,), jnp.float32, -lim, lim)
        W2 = jax.random.uniform(ks[6], (D, D), jnp.float32, -lim, lim)
        b2 = jax.random.uniform(ks[7], (D,), jnp.float32, -lim, lim)
        return {'q': q, 'k': k, 'v1': v1, 'mask': mask, 'W1': W1, 'b1': b1, 'W2': W2, 'b2': b2}
    _L1_xattn_all = _L1_xattn_setup()
    _L1_xattn_in = {k: v for k, v in _L1_xattn_all.items() if k in ('W1', 'b1', 'W2', 'b2')}
    del _L1_xattn_all

    def _L1_ffn_setup():
        import jax, jax.numpy as jnp
        import numpy as np
        B, S, K, N = (8, 1024, 128, 128)
        key = jax.random.key(seed)
        k1, k2, k3, k4 = jax.random.split(key, 4)
        x = jax.random.normal(k1, (B, S, K), dtype=jnp.float32)
        CB = jnp.clip(jnp.round(jax.random.normal(k2, (N, K), dtype=jnp.float32) * 42.0), -127.0, 127.0)
        SCB = jax.random.uniform(k3, (N,), dtype=jnp.float32, minval=0.5, maxval=2.0)
        bias = jax.random.normal(k4, (N,), dtype=jnp.float32) * 0.02
        return {'x': x, 'CB': CB, 'SCB': SCB, 'bias': bias}
    _L1_ffn_all = _L1_ffn_setup()
    _L1_ffn_in = {k: v for k, v in _L1_ffn_all.items() if k in ('CB', 'SCB', 'bias')}
    del _L1_ffn_all
    return {'x': x, 'ctx_1024': ctx_1024, 'fside_1xSxS2_0': fside_1xSxS2_0, 'g_xattn': g_xattn, 'g_ffn': g_ffn, 'L0_xattn_igate_kernel': _L0_xattn_in['igate_kernel'], 'L0_xattn_igate_bias': _L0_xattn_in['igate_bias'], 'L0_xattn_fgate_kernel': _L0_xattn_in['fgate_kernel'], 'L0_xattn_fgate_bias': _L0_xattn_in['fgate_bias'], 'L0_xattn_rms_scale': _L0_xattn_in['rms_scale'], 'L0_ffn_wg': _L0_ffn_in['wg'], 'L0_ffn_w1': _L0_ffn_in['w1'], 'L0_ffn_b1': _L0_ffn_in['b1'], 'L0_ffn_w2': _L0_ffn_in['w2'], 'L0_ffn_b2': _L0_ffn_in['b2'], 'L1_xattn_W1': _L1_xattn_in['W1'], 'L1_xattn_b1': _L1_xattn_in['b1'], 'L1_xattn_W2': _L1_xattn_in['W2'], 'L1_xattn_b2': _L1_xattn_in['b2'], 'L1_ffn_CB': _L1_ffn_in['CB'], 'L1_ffn_SCB': _L1_ffn_in['SCB'], 'L1_ffn_bias': _L1_ffn_in['bias']}

def reference(x, ctx_1024, fside_1xSxS2_0, g_xattn, g_ffn, L0_xattn_igate_kernel, L0_xattn_igate_bias, L0_xattn_fgate_kernel, L0_xattn_fgate_bias, L0_xattn_rms_scale, L0_ffn_wg, L0_ffn_w1, L0_ffn_b1, L0_ffn_w2, L0_ffn_b2, L1_xattn_W1, L1_xattn_b1, L1_xattn_W2, L1_xattn_b2, L1_ffn_CB, L1_ffn_SCB, L1_ffn_bias):
    import jax
    import jax.numpy as jnp

    def _L0_xattn_ref(q, k, v, igate_kernel, igate_bias, fgate_kernel, fgate_bias, rms_scale):
        import jax, jax.numpy as jnp
        import numpy as np
        B, S, E, NH = (2, 256, 128, 4)
        HD = E // NH

        def _mlstm_head(q, k, v, ig, fg, eps=1e-06):
            s, dh = q.shape
            log_f = jax.nn.log_sigmoid(fg)
            cs = jnp.concatenate([jnp.zeros((1, 1), log_f.dtype), jnp.cumsum(log_f, axis=0)], axis=0)
            neg = jnp.asarray(-0.7 * jnp.finfo(cs.dtype).max, cs.dtype)
            log_d = jnp.where(jnp.tri(s, dtype=bool), (cs - cs.T)[1:, 1:] + ig.T, neg)
            m = jnp.max(log_d, axis=-1, keepdims=True)
            d = jnp.exp(log_d - m)
            c = q @ (k.T / jnp.sqrt(dh)) * d
            n = jnp.maximum(jnp.sum(c, axis=-1, keepdims=True), jnp.exp(-m))
            return c / (n + eps) @ v
        b, s, e = q.shape
        nh = igate_kernel.shape[1]
        hd = e // nh
        gate_in = jnp.concatenate((q, k, v), axis=-1)
        ig = (gate_in @ igate_kernel + igate_bias).swapaxes(-1, -2)[..., None]
        fg = (gate_in @ fgate_kernel + fgate_bias).swapaxes(-1, -2)[..., None]
        qh = q.reshape(b, s, nh, hd).swapaxes(1, 2)
        kh = k.reshape(b, s, nh, hd).swapaxes(1, 2)
        vh = v.reshape(b, s, nh, hd).swapaxes(1, 2)
        h = jax.vmap(jax.vmap(_mlstm_head))(qh, kh, vh, ig, fg)
        var = jnp.mean(jnp.square(h.astype(jnp.float32)), axis=-1, keepdims=True)
        h = (h * jax.lax.rsqrt(var + 1e-06)).astype(h.dtype) * (1.0 + rms_scale)
        return h.swapaxes(1, 2).reshape(b, s, e)

    def _L0_ffn_ref(hidden_states, wg, w1, b1, w2, b2):
        import jax, jax.numpy as jnp
        import numpy as np
        B, T, M = hidden_states.shape
        E = wg.shape[1]
        S = B * T
        MIN_CAPACITY = 4
        C = max((S + E - 1) // E, MIN_CAPACITY)
        x = hidden_states.reshape(S, M)
        logits = x @ wg
        gates = jax.nn.softmax(logits, axis=-1)
        idx = jnp.argmax(gates, axis=-1)
        mask1 = jax.nn.one_hot(idx, E, dtype=gates.dtype)
        l_aux = jnp.sum(gates.mean(0) * mask1.mean(0)) * E
        locations1 = jnp.cumsum(mask1, axis=0) - 1.0
        mask1 = mask1 * (locations1 < C)
        gates1_s = jnp.sum(gates * mask1, axis=1)
        loc_s = jnp.sum(locations1 * mask1, axis=1).astype(jnp.int32)
        loc_sc = jax.nn.one_hot(loc_s, C, dtype=gates.dtype)
        combine_weights = jnp.einsum('se,sc->sec', gates1_s[:, None] * mask1, loc_sc)
        dispatch_mask = (combine_weights > 0).astype(x.dtype)
        dispatched = jnp.einsum('sec,sm->ecm', dispatch_mask, x)
        h = jax.nn.gelu(jnp.einsum('ecm,emf->ecf', dispatched, w1) + b1[:, None, :])
        expert_out = jnp.einsum('ecf,efm->ecm', h, w2) + b2[:, None, :]
        out = jnp.einsum('sec,ecm->sm', combine_weights, expert_out)
        return out.reshape(B, T, M)

    def _L1_xattn_ref(q, k, v1, mask, W1, b1, W2, b2):
        import jax, jax.numpy as jnp
        import numpy as np
        import math
        D = 128
        B, S = (8, 256)

        def _proj(x, W1, b1, W2, b2):
            h = jnp.einsum('bsd,od->bso', x, W1) + b1
            return jnp.einsum('bsd,od->bso', h, W2) + b2
        qp = _proj(q, W1, b1, W2, b2)
        kp = _proj(k, W1, b1, W2, b2)
        scale = 1.0 / math.sqrt(qp.shape[-1])
        qk = jnp.einsum('bqd,bkd->bqk', qp, kp) * scale
        qk = qk + mask
        attn = jax.nn.softmax(qk, axis=-1)
        return jnp.einsum('bqk,bkd->bqd', attn, v1)

    def _L1_ffn_ref(x, CB, SCB, bias):
        import jax, jax.numpy as jnp
        import numpy as np
        B, S, K, N = (8, 1024, 128, 128)
        out = jnp.einsum('bsk,nk->bsn', x, CB)
        out = out * (SCB * (1.0 / 127.0)) + bias
        return out
    x = x + jnp.tanh(g_xattn[0]) * _L0_xattn_ref(_layernorm(x, axis=-1), ctx_1024, ctx_1024, L0_xattn_igate_kernel, L0_xattn_igate_bias, L0_xattn_fgate_kernel, L0_xattn_fgate_bias, L0_xattn_rms_scale)
    x = x + jnp.tanh(g_ffn[0]) * _L0_ffn_ref(_layernorm(x, axis=-1), L0_ffn_wg, L0_ffn_w1, L0_ffn_b1, L0_ffn_w2, L0_ffn_b2)
    x = x + jnp.tanh(g_xattn[1]) * _L1_xattn_ref(_layernorm(x, axis=-1), ctx_1024, ctx_1024, fside_1xSxS2_0, L1_xattn_W1, L1_xattn_b1, L1_xattn_W2, L1_xattn_b2)
    x = x + jnp.tanh(g_ffn[1]) * _L1_ffn_ref(_layernorm(x, axis=-1), L1_ffn_CB, L1_ffn_SCB, L1_ffn_bias)
    return x

_drawn_inputs = setup_inputs


def setup_inputs(seed=0):
    import zlib

    import numpy as np

    out = dict(_drawn_inputs(seed))
    spreads = {'g_ffn': (-1.0, 0.2), 'L0_ffn_b1': (0.0, 0.638), 'L0_ffn_b2': (0.0, 0.436)}
    factors = {'L0_xattn_igate_bias': 64.0,
     'L0_xattn_fgate_kernel': 4.356,
     'L0_xattn_rms_scale': 3.672,
     'L1_xattn_b1': 8.0,
     'L1_xattn_W2': 3.725,
     'L1_xattn_b2': 8.0,
     'L1_ffn_bias': 8.0}
    for name, (base, spread) in spreads.items():
        noise = np.random.default_rng([zlib.crc32(name.encode()), seed]).standard_normal(out[name].shape)
        drawn = base * np.exp(spread * noise) if base else spread * noise
        out[name] = jnp.asarray(drawn.astype(out[name].dtype))
    for name, factor in factors.items():
        out[name] = (out[name] * factor).astype(out[name].dtype)
    return out
```

```python
from contextlib import ExitStack

import concourse.bass as bass
from concourse import mybir

F32 = mybir.dt.float32
BF16 = mybir.dt.bfloat16
I32 = mybir.dt.int32
ALU = mybir.AluOpType
ACT = mybir.ActivationFunctionType
AX = mybir.AxisListType.X

P = 128
GT = 4
GW = GT * P
LN_EPS = 1e-5
MASKED = -1e30


def nth(g, k, n):
    return g * n + k


def need(eng, sem, value):
    if isinstance(value, int) and value <= 0:
        return
    eng.wait_ge(sem, value)


def hold(eng, sem, value, go):
    if not isinstance(value, int):
        value = eng.to_reg(value)
        eng.wait_ge(go, 1)
    need(eng, sem, value)


def over_groups(eng, groups, stages, body):
    def step(half, parity, static):
        at = []
        for s in range(stages):
            back = s - parity
            h, q = (half, parity - s) if back <= 0 else (half - (back + 1) // 2, (parity - s) % 2)
            g = h * 2 + q
            at.append(None if static and not 0 <= g < groups else (g, h, q))
        body(at)

    first = (stages + 1) // 2
    for k in range(2 * first):
        step(k // 2, k % 2, True)
    with eng.Fori(first, groups // 2) as half:
        step(half, 0, False)
        step(half, 1, False)
    for k in range(groups, groups + stages - 1):
        step(k // 2, k % 2, True)


class Norm:

    def __init__(self, name, sb, sem, go):
        self.go = go
        self.stats = sb(f"{name}_stats", [P, GT, 6])
        self.mv = sb(f"{name}_mv", [P, GT, 2])
        self.ve = sb(f"{name}_ve", [P, GT])
        self.log = sb(f"{name}_log", [P, GT])
        self.y0 = sb(f"{name}_y0", [P, GT])
        self.t = sb(f"{name}_t", [P, 3, GT])
        self.rstd = sb(f"{name}_rstd", [P, GT])
        self.stats_done = sem(f"{name}_stats_done")
        self.mv_done = sem(f"{name}_mv_done")
        self.ve_done = sem(f"{name}_ve_done")
        self.log_done = sem(f"{name}_log_done")
        self.y0_done = sem(f"{name}_y0_done")
        self.newton = sem(f"{name}_newton")
        self.applied = sem(f"{name}_applied")

    def dve_stats(self, dve, g, tile):
        for t in range(GT):
            last = dve.bn_stats(self.stats[:, t, :], tile(t))
        last.then_inc(self.stats_done, 1)
        hold(dve, self.stats_done, g + 1, self.go)
        for t in range(GT):
            last = dve.bn_aggr(self.mv[:, t, :], self.stats[:, t, :])
        last.then_inc(self.mv_done, 1)

    def pool_var(self, pool, g):
        hold(pool, self.mv_done, g + 1, self.go)
        pool.tensor_scalar(self.ve[:, :], self.mv[:, :, 1], LN_EPS, None, ALU.add).then_inc(self.ve_done, 1)

    def act_guess(self, act, g):
        act.wait_ge(self.ve_done, g + 1)
        act.activation(self.log[:, :], self.ve[:, :], ACT.Ln).then_inc(self.log_done, 1)
        act.wait_ge(self.log_done, g + 1)
        act.activation(self.y0[:, :], self.log[:, :], ACT.Exp, scale=-0.5).then_inc(self.y0_done, 1)

    def pool_newton(self, pool, g):
        hold(pool, self.y0_done, g + 1, self.go)
        pool.tensor_tensor(self.t[:, 0, :], self.y0[:, :], self.y0[:, :], ALU.mult).then_inc(self.newton, 1)
        hold(pool, self.newton, nth(g, 1, 4), self.go)
        pool.tensor_tensor(self.t[:, 1, :], self.t[:, 0, :], self.ve[:, :], ALU.mult).then_inc(self.newton, 1)
        hold(pool, self.newton, nth(g, 2, 4), self.go)
        pool.tensor_scalar(self.t[:, 2, :], self.t[:, 1, :], -0.5, 1.5, ALU.mult, ALU.add).then_inc(self.newton, 1)
        hold(pool, self.newton, nth(g, 3, 4), self.go)
        pool.tensor_tensor(self.rstd[:, :], self.t[:, 2, :], self.y0[:, :], ALU.mult).then_inc(self.newton, 1)

    def dve_apply(self, dve, g, out, tile):
        dve.wait_ge(self.newton, nth(g, 4, 4))
        for t in range(GT):
            last = dve.tensor_scalar(out(t), tile(t), self.mv[:, t, 0:1], self.rstd[:, t:t + 1],
                                     ALU.subtract, ALU.mult)
        last.then_inc(self.applied, 1)


def flamingo(nc, x, ctx_1024, fside, g_xattn, g_ffn, igate_kernel, igate_bias, fgate_kernel, fgate_bias,
             rms_scale, wg, w1, b1, w2, b2, pw1, pb1, pw2, pb2, CB, SCB, cbias, out):
    NB, S, D = x.shape
    N = NB * S
    NH = igate_kernel.shape[1]
    HD = D // NH
    E = wg.shape[1]
    F = w1.shape[2]
    FC = F // P
    CAP = max((N + E - 1) // E, 4)
    NT = N // P
    NG = N // GW
    BG = GW // S
    R = GT * NH
    HA = HD + 1
    assert D == P and S == P // 2 and CAP == 2 * GW and E * CAP == N and R == 16 and NG == 2 * E

    ctx = ExitStack()
    with ctx:
        def sb(name, shape, dt=F32):
            return ctx.enter_context(nc.sbuf_tensor("s_" + name, shape, dt))

        def sem(name):
            return ctx.enter_context(nc.semaphore(name))

        m_dram = [nc.dram_tensor(f"m_scratch{i}", (2, R * S), F32, kind="Internal").ap() for i in range(2)]
        slots_x = nc.dram_tensor("slots_x", (2 * N, D), F32, kind="Internal").ap()
        slots_y = nc.dram_tensor("slots_y", (N, D), F32, kind="Internal").ap()

        ident = sb("ident", [P, P])
        tri = sb("tri", [P, P])
        tri_b = sb("tri_b", [P, P], BF16)
        ones_b = sb("ones_b", [P, P], BF16)
        cap = sb("cap", [P, S])
        prio = sb("prio", [P, E])
        prio_i = sb("prio_i", [P, E], I32)
        trash_i = sb("trash_i", [P, NT], I32)
        trash = sb("trash", [P, NT])
        carry = sb("carry", [P, 2, E])
        carry_i = sb("carry_i", [P, E], I32)
        reset = sb("reset", [R, P])
        kq = sb("kq", [P, 2 * NH])
        kk = sb("kk", [P, 2 * NH])
        kv = sb("kv", [P, 2 * NH])
        kc = sb("kc", [P, 2 * NH])
        gate_bias = sb("gate_bias", [P, 2 * NH])
        gx = sb("gx", [P, 2])
        gf = sb("gf", [P, 2])
        tx = sb("tx", [P, 2])
        tf = sb("tf", [P, 2])
        rmsb = sb("rmsb", [P, HD])
        rmsw = sb("rmsw", [P, HD])
        head_w = sb("head_w", [P, D])
        wg_sb = sb("wg_sb", [P, E])
        pw1_sb = sb("pw1_sb", [P, P])
        pw2_sb = sb("pw2_sb", [P, P])
        pw2t = sb("pw2t", [P, P])
        cb_sb = sb("cb_sb", [P, P])
        cbs = sb("cbs", [P, P])
        cbt = sb("cbt", [P, P])
        rows = sb("rows", [P, P])
        cols = sb("cols", [P, 40])
        pa = sb("pa", [P, P])
        pc = sb("pc", [P, 1])
        scb_t = sb("scb_t", [P, 1])
        cbias_b = sb("cbias_b", [P, P])
        fbias = sb("fbias", [P, P])
        mask = sb("mask", [P, S])
        b2b = sb("b2b", [P, E, D])

        xs = sb("xs", [P, NT * D])
        kpt = sb("kpt", [P, N])
        gw = sb("gw", [P, NT])
        gidx = sb("gidx", [P, NT], I32)

        ctxb = sb("ctxb", [P, 2, GT, D])
        vaug = sb("vaug", [P, 2, GT, NH, HA])
        xn1 = sb("xn1", [P, GT, D])
        qt = sb("qt", [P, 2, GW])
        kt = sb("kt", [P, 2, GW])
        gates = sb("gates", [P, 2, R])
        negabs = sb("negabs", [P, R])
        eneg = sb("eneg", [P, R])
        softp = sb("softp", [P, R])
        logf = sb("logf", [P, R])
        fcum = sb("fcum", [P, R])
        am = sb("am", [P, 2, R])
        mrow = sb("mrow", [R, 2, P])
        mtok = sb("mtok", [P, R])
        em = sb("em", [P, 2, R])
        mb = sb("mb", [P, 2, R * S])
        ex = sb("ex", [P, 2, R * S])
        cw = sb("cw", [P, NH, GT, S])
        sq = sb("sq", [P, NH, GT, HD])
        nn = sb("nn", [P, 3, NH, GT])
        ss = sb("ss", [P, NH, GT])
        zz = sb("zz", [P, 6, NH, GT])
        hs = sb("hs", [P, 2, GT, D])
        xn2 = sb("xn2", [P, 2, GT, D])
        xt2 = sb("xt2", [P, GW])
        rt = sb("rt", [P, 6, GT, E])
        onehot = sb("onehot", [P, GT + 1, E], BF16)
        rs = sb("rs", [P, 13, GT])
        sidx = sb("sidx", [P, 2, GT], I32)

        w1_sb = sb("w1_sb", [P, 2, F])
        w2_sb = sb("w2_sb", [P, 2, FC, D])
        xe = sb("xe", [P, 2, GT, D])
        xet = sb("xet", [P, GW])
        ht = sb("ht", [P, 2, FC, GW])
        ye = sb("ye", [P, 2, GT, D])

        yg = sb("yg", [P, 2, GT, D])
        kpr = sb("kpr", [P, 2, GW])
        gix = sb("gix", [P, 2, GT], I32)
        ctxv = sb("ctxv", [P, 2, GT, D + 1])
        xn3 = sb("xn3", [P, GT, D])
        qt3 = sb("qt3", [P, GW])
        qp = sb("qp", [P, 2, GW])
        sm = sb("sm", [P, 2, GT, S])
        smx = sb("smx", [P, GT])
        pr = sb("pr", [P, GT, S])
        prt = sb("prt", [P, 2, P])
        rsum = sb("rsum", [P, 2, GT])
        xn4 = sb("xn4", [P, GT, D])
        xt4 = sb("xt4", [P, GW])
        zeros = ht[:, 0, :, :].rearrange("p c n -> p (c n)")
        xo = mb[:, :, 0:GT * D].rearrange("p q (t d) -> p q t d", t=GT)
        xb = ex[:, :, 0:GT * D].rearrange("p q (t d) -> p q t d", t=GT)

        bank = [ctx.enter_context(nc.psum_tensor(f"bank{i}", [P, 512], F32)) for i in range(2)]
        heads = ctx.enter_context(nc.psum_tensor("heads", [P, 4, 512], F32))
        bank += [None] * 4 + [ctx.enter_context(nc.psum_tensor(f"bank{i}", [P, 512], F32)) for i in (6, 7)]

        par_in = sem("par_in")
        iotas = sem("iotas")
        consts = sem("consts")
        dve_setup = sem("dve_setup")
        act_setup = sem("act_setup")
        pe_setup = sem("pe_setup")
        filled = sem("filled")
        x_in = [sem(f"x_in{i}") for i in range(2)]
        ctx_in = [sem(f"ctx_in{i}") for i in range(2)]
        vaug_done = sem("vaug_done")
        xt1_done = sem("xt1_done")
        ct_done = sem("ct_done")
        qt_done = sem("qt_done")
        kt_done = sem("kt_done")
        kp_done = sem("kp_done")
        kpt_done = sem("kpt_done")
        gates_ps = sem("gates_ps")
        gate_steps = sem("gate_steps")
        gate_act = sem("gate_act")
        f_ps = sem("f_ps")
        a_done = sem("a_done")
        at_ps = sem("at_ps")
        mrow_done = sem("mrow_done")
        m_out = [sem(f"m_out{i}") for i in range(2)]
        m_in = [sem(f"m_in{i}") for i in range(2)]
        mt_ps = sem("mt_ps")
        mtok_done = sem("mtok_done")
        em_done = sem("em_done")
        l_done = sem("l_done")
        lcap_done = sem("lcap_done")
        ex_done = sem("ex_done")
        scores_done = sem("scores_done")
        cw_done = sem("cw_done")
        pv_done = sem("pv_done")
        sq_done = sem("sq_done")
        n_done = sem("n_done")
        ss_done = sem("ss_done")
        z_done = sem("z_done")
        z_act = sem("z_act")
        hs_done = sem("hs_done")
        hsw_done = sem("hsw_done")
        x1_done = sem("x1_done")
        xt2_ps = sem("xt2_ps")
        xt2_done = sem("xt2_done")
        logits_ps = sem("logits_ps")
        route = sem("route")
        route_act = sem("route_act")
        onehot_done = sem("onehot_done")
        cum_ps = sem("cum_ps")
        slot_done = sem("slot_done")
        idx_steps = sem("idx_steps")
        scattered = [sem(f"scattered{i}") for i in range(2)]
        w_in = [sem(f"w_in{i}") for i in range(2)]
        xe_in = [sem(f"xe_in{i}") for i in range(2)]
        xet_ps = sem("xet_ps")
        xet_done = sem("xet_done")
        h_ps = sem("h_ps")
        h_done = sem("h_done")
        y_ps = sem("y_ps")
        y_done = sem("y_done")
        y_out = [sem(f"y_out{i}") for i in range(2)]
        kpr_in = [sem(f"kpr_in{i}") for i in range(2)]
        gix_done = sem("gix_done")
        yg_in = [sem(f"yg_in{i}") for i in range(2)]
        v_in = [sem(f"v_in{i}") for i in range(2)]
        x2_done = sem("x2_done")
        q3_ps = sem("q3_ps")
        q3_done = sem("q3_done")
        qp_ps = sem("qp_ps")
        qp_done = sem("qp_done")
        s3_ps = sem("s3_ps")
        sm_steps = sem("sm_steps")
        pr_done = sem("pr_done")
        prt_ps = sem("prt_ps")
        prt_done = sem("prt_done")
        o3_ps = sem("o3_ps")
        o3_steps = sem("o3_steps")
        x3_done = sem("x3_done")
        xb_done = sem("xb_done")
        xt4_ps = sem("xt4_ps")
        xt4_done = sem("xt4_done")
        f_out_ps = sem("f_out_ps")
        xo_done = sem("xo_done")
        stored = [sem(f"stored{i}") for i in range(2)]

        ln1, ln2, ln3, ln4 = (Norm(f"ln{i}", sb, sem, consts) for i in range(1, 5))

        x_rows = x.rearrange("b s d -> (b s) d").rearrange("(t p) d -> p t d", p=P)
        ctx_rows = ctx_1024.rearrange("b s d -> (b s) d").rearrange("(t p) d -> p t d", p=P)
        out_rows = out.rearrange("b s d -> (b s) d").rearrange("(t p) d -> p t d", p=P)
        slots_rows = slots_x.rearrange("(t p) d -> p t d", p=P)
        y_rows = slots_y.rearrange("(t p) d -> p t d", p=P)
        w1_rows = w1.rearrange("e m f -> m e f")
        w2_rows = w2.rearrange("e (c f) m -> f e c m", f=P)

        def tiles(g):
            return bass.ds(g * GT, GT)

        def xtile(g):
            return lambda t: xs[:, bass.ds(g * GW + t * P, P)]

        def xgroup(g):
            return xs[:, bass.ds(g * GW, GW)]

        def one_row(v):
            return v.rearrange("(a n) -> a n", a=1)

        CONSTS = 23
        block = ctx.enter_context(nc.Block())

        setup_loads = [
            (kq[:, 0:NH], igate_kernel[0:D, :]), (kq[:, NH:], fgate_kernel[0:D, :]),
            (kk[:, 0:NH], igate_kernel[D:2 * D, :]), (kk[:, NH:], fgate_kernel[D:2 * D, :]),
            (kv[:, 0:NH], igate_kernel[2 * D:, :]), (kv[:, NH:], fgate_kernel[2 * D:, :]),
            (gate_bias[:, 0:NH], one_row(igate_bias).to_broadcast([P, NH])),
            (gate_bias[:, NH:], one_row(fgate_bias).to_broadcast([P, NH])),
            (gx[:, :], one_row(g_xattn).to_broadcast([P, 2])),
            (gf[:, :], one_row(g_ffn).to_broadcast([P, 2])),
            (rmsb[:, :], one_row(rms_scale).to_broadcast([P, HD])),
            (wg_sb[:, :], wg), (pw1_sb[:, :], pw1), (pw2_sb[:, :], pw2), (cb_sb[:, :], CB),
            (rows[0:E * FC, :], b1.rearrange("e (c f) -> (e c) f", f=P)),
            (rows[32:33, :], one_row(pb1)), (rows[33:34, :], one_row(pb2)), (rows[34:35, :], one_row(SCB)),
            (cbias_b[:, :], one_row(cbias).to_broadcast([P, P])),
            (mask[0:S, :], fside[0]), (mask[S:P, :], fside[0]),
        ]
        PARAMS = 16 * len(setup_loads)
        B1, PB1, PB2, SCBC = 0, 32, 33, 34
        assert E * FC == 32

        @block.sync
        def _(sp):
            def load(g, half, q):
                if not isinstance(g, int) or g >= 2:
                    hold(sp, ct_done, g - 1, consts)
                    hold(sp, vaug_done, g - 1, consts)
                sp.dma_start(xgroup(g).rearrange("p (t d) -> p t d", t=GT), x_rows[:, tiles(g), :]).then_inc(x_in[q], 16)
                sp.dma_start(ctxb[:, q, :, :], ctx_rows[:, tiles(g), :]).then_inc(ctx_in[q], 16)

            def spread_max(g, half, q):
                hold(sp, mrow_done, g + 1, consts)
                sp.dma_start(m_dram[q].rearrange("b (r i) -> r b i", i=S),
                             mrow[:, q, :].rearrange("r (b i) -> r b i", b=2)).then_inc(m_out[q], 16)
                hold(sp, m_out[q], half * 16 + 16, consts)
                hold(sp, l_done, g - 1, consts)
                for b in range(2):
                    sp.dma_start(mb[b * S:(b + 1) * S, q, :],
                                 m_dram[q][b:b + 1, :].to_broadcast([S, R * S])).then_inc(m_in[q], 16)

            load(0, 0, 0)
            sp.wait_ge(consts, 2)
            for dst, src in setup_loads:
                sp.dma_start(dst, src).then_inc(par_in, 16)
            load(1, 0, 1)
            sp.wait_ge(consts, 1)
            for n in range(NT * D // 2048):
                per = 2048 // D
                sp.dma_start(slots_rows[:, n * per:(n + 1) * per, :],
                             zeros.rearrange("p (t d) -> p t d", d=D)).then_inc(filled, 16)

            spread_max(0, 0, 0)
            load(2, 1, 0)
            spread_max(1, 0, 1)
            with sp.Fori(1, NG // 2 - 1) as half:
                load(half * 2 + 1, half, 1)
                spread_max(half * 2, half, 0)
                load(half * 2 + 2, half + 1, 0)
                spread_max(half * 2 + 1, half, 1)
            load(NG - 1, NG // 2 - 1, 1)
            spread_max(NG - 2, NG // 2 - 1, 0)
            spread_max(NG - 1, NG // 2 - 1, 1)

            for e in range(E):
                sp.dma_start(b2b[:, e, :], one_row(b2[e]).to_broadcast([P, D])).then_inc(par_in, 16)

            def load_w(e, half, q):
                hold(sp, y_ps, e * 2 - 2, consts)
                sp.dma_start(w1_sb[:, q, :], w1_rows[:, e, :]).then_inc(w_in[q], 16)
                sp.dma_start(w2_sb[:, q, :, :], w2_rows[:, e, :, :]).then_inc(w_in[q], 16)

            def load_xe(s, half, q):
                hold(sp, xet_ps, s - 1, consts)
                sp.dma_start(xe[:, q, :, :], slots_rows[:, tiles(s), :]).then_inc(xe_in[q], 16)

            def store_y(s, half, q):
                hold(sp, y_done, s + 1, consts)
                sp.dma_start(y_rows[:, tiles(s), :], ye[:, q, :, :]).then_inc(y_out[q], 16)

            load_w(0, 0, 0)
            load_w(1, 0, 1)
            for q in range(2):
                sp.wait_ge(scattered[q], 16 * GT * NG // 2)
            load_xe(0, 0, 0)
            load_xe(1, 0, 1)
            with sp.Fori(0, E // 2 - 1) as quad:
                for j in range(4):
                    s = quad * 4 + j
                    load_xe(s + 2, None, j % 2)
                    store_y(s, None, j % 2)
                    if j % 2:
                        load_w(quad * 2 + 2 + j // 2, None, j // 2)
            for s in range(NG - 4, NG):
                if s + 2 < NG:
                    load_xe(s + 2, None, s % 2)
                store_y(s, None, s % 2)
            for q in range(2):
                sp.wait_ge(y_out[q], 16 * NG // 2)

            def load_v(g, half, q):
                hold(sp, o3_ps, g - 1, consts)
                sp.dma_start(ctxv[:, q, :, 0:D], ctx_rows[:, tiles(g), :]).then_inc(v_in[q], 16)
                sp.dma_start(kpr[:, q, :], kpt[:, bass.ds(g * GW, GW)]).then_inc(kpr_in[q], 16)

            def store(g, half, q):
                hold(sp, xo_done, g + 1, consts)
                sp.dma_start(out_rows[:, tiles(g), :], xo[:, q, :, :]).then_inc(stored[q], 16)

            load_v(0, 0, 0)
            load_v(1, 0, 1)
            with sp.Fori(0, NG // 2 - 1) as half:
                for q in range(2):
                    load_v(half * 2 + q + 2, half + 1, q)
                    store(half * 2 + q, half, q)
            store(NG - 2, NG // 2 - 1, 0)
            store(NG - 1, NG // 2 - 1, 1)
            for q in range(2):
                sp.wait_ge(stored[q], 16 * NG // 2)

        @block.gpsimd
        def _(pool):
            done = 0

            def step(ins):
                nonlocal done
                done += 1
                ins.then_inc(consts, 1)
                pool.wait_ge(consts, done)

            step(pool.memset(zeros, 0.0))
            step(pool.memset(rows[:, :], 0.0))
            step(pool.memset(ident[:, :], 0.0))
            step(pool.affine_select(out=ident[:, :], in_=ident[:, :], compare_op=ALU.not_equal, fill=1.0, base=0,
                                    pattern=[[-1, P]], channel_multiplier=1))
            step(pool.memset(tri[:, :], 1.0))
            step(pool.affine_select(out=tri[:, :], in_=tri[:, :], compare_op=ALU.is_ge, fill=0.0, base=0,
                                    pattern=[[1, P]], channel_multiplier=-1))
            step(pool.tensor_copy(tri_b[:, :], tri[:, :]))
            step(pool.memset(tri[0:S, S:P], 0.0))
            step(pool.memset(cap[:, :], 0.0))
            for b in range(2):
                half = cap[b * S:(b + 1) * S, :]
                step(pool.affine_select(out=half, in_=half, compare_op=ALU.is_ge, fill=MASKED, base=0,
                                        pattern=[[1, S]], channel_multiplier=-1))
            step(pool.memset(reset[:, :], 0.0))
            step(pool.memset(reset[:, :].rearrange("r (b i) -> r b i", b=2)[:, :, 0:1], -1e38))
            step(pool.memset(ones_b[:, :], 1.0))
            step(pool.memset(onehot[:, :, :], 0.0))
            step(pool.memset(vaug[:, :, :, :, HD:HA], 1.0))
            step(pool.memset(ctxv[:, :, :, D:D + 1], 1.0))
            step(pool.iota(prio_i[:, :], pattern=[[-1, E]], base=E, channel_multiplier=0))
            step(pool.iota(trash_i[:, :], pattern=[[P, NT]], base=N, channel_multiplier=1))
            step(pool.iota(carry_i[:, :], pattern=[[CAP, E]], base=-1, channel_multiplier=0))
            step(pool.tensor_copy(prio[:, :], prio_i[:, :]))
            step(pool.tensor_copy(trash[:, :], trash_i[:, :]))
            step(pool.tensor_copy(carry[:, 0, :], carry_i[:, :]))
            assert done == CONSTS

            def first_pass(at):
                one, two, three = at
                if one:
                    g, half, q = one
                    ln1.pool_var(pool, g)
                    hold(pool, ctx_in[q], half * 16 + 16, consts)
                    hold(pool, pv_done, nth(g - 2, NH, NH), consts)
                    pool.tensor_copy(vaug[:, q, :, :, 0:HD],
                                     ctxb[:, q, :, :].rearrange("p t (h d) -> p t h d", h=NH)).then_inc(vaug_done, 1)
                if two:
                    g, half, q = two
                    hold(pool, m_in[q], half * 32 + 32, consts)
                    hold(pool, a_done, g + 1, consts)
                    hold(pool, ex_done, g - 1, consts)
                    pool.tensor_tensor(ex[:, q, :].rearrange("p (r i) -> p r i", i=S),
                                       am[:, q, :].unsqueeze(2).to_broadcast([P, R, S]),
                                       mb[:, q, :].rearrange("p (r i) -> p r i", i=S),
                                       ALU.subtract).then_inc(l_done, 1)
                if one:
                    ln1.pool_newton(pool, one[0])
                if three:
                    g, half, q = three
                    ln2.pool_var(pool, g)
                    ln2.pool_newton(pool, g)
                if two:
                    g, half, q = two
                    hold(pool, hs_done, g + 1, consts)
                    pool.tensor_tensor(hs[:, q, :, :], hs[:, q, :, :],
                                       head_w[:, :].unsqueeze(1).to_broadcast([P, GT, D]), ALU.mult).then_inc(hsw_done, 1)
                if three:
                    g, half, q = three
                    ntl = tiles(g)
                    hold(pool, slot_done, g + 1, consts)
                    if g is None or not isinstance(g, int) or g >= 2:
                        hold(pool, scattered[q], half * (16 * GT), consts)
                    k = 0

                    def step(ins):
                        nonlocal k
                        k += 1
                        ins.then_inc(idx_steps, 1)
                        hold(pool, idx_steps, nth(g, k, 11), consts)

                    slot, limit, beyond, kept = rs[:, 0, :], rs[:, 3, :], rs[:, 7, :], rs[:, 4, :]
                    step(pool.tensor_scalar(limit, rs[:, 1, :], -float(CAP), float((E + 1) * CAP), ALU.mult, ALU.add))
                    step(pool.tensor_tensor(beyond, slot, limit, ALU.subtract))
                    step(pool.tensor_scalar(kept, beyond, 0.0, None, ALU.is_lt))
                    step(pool.tensor_tensor(rs[:, 5, :], slot, trash[:, ntl], ALU.subtract))
                    step(pool.tensor_tensor(rs[:, 6, :], rs[:, 5, :], kept, ALU.mult))
                    step(pool.tensor_tensor(rs[:, 11, :], rs[:, 6, :], trash[:, ntl], ALU.add))
                    step(pool.tensor_copy(sidx[:, q, :], rs[:, 11, :]))
                    step(pool.tensor_scalar(rs[:, 10, :], beyond, -1.0, None, ALU.min))
                    step(pool.tensor_tensor(rs[:, 12, :], rs[:, 10, :], limit, ALU.add))
                    step(pool.tensor_copy(gidx[:, ntl], rs[:, 12, :]))
                    step(pool.tensor_tensor(gw[:, ntl], rs[:, 2, :], kept, ALU.mult))
                    if isinstance(g, int) and g == 0:
                        pool.wait_ge(filled, 16 * (NT * D // 2048))
                    for t in range(GT):
                        pool.indirect_dma_start(out=slots_x, out_offset=bass.IndirectOffsetOnAxis(ap=sidx[:, q, t:t + 1], axis=0),
                                                in_=xn2[:, q, t, :], in_offset=None).then_inc(scattered[q], 16)

            over_groups(pool, NG, 3, first_pass)

            for q in range(2):
                pool.wait_ge(y_out[q], 16 * NG // 2)

            def last_pass(at):
                one, two, three = at
                if one:
                    g, half, q = one
                    hold(pool, x2_done, g - 1, consts)
                    pool.tensor_copy(gix[:, q, :], gidx[:, tiles(g)]).then_inc(gix_done, 1)
                    hold(pool, gix_done, g + 1, consts)
                    for t in range(GT):
                        pool.indirect_dma_start(out=yg[:, q, t, :], out_offset=None, in_=slots_y,
                                                in_offset=bass.IndirectOffsetOnAxis(ap=gix[:, q, t:t + 1], axis=0)
                                                ).then_inc(yg_in[q], 16)
                    ln3.pool_var(pool, g)
                if three:
                    g, half, q = three
                    ln4.pool_var(pool, g)
                if one:
                    ln3.pool_newton(pool, one[0])
                if three:
                    ln4.pool_newton(pool, three[0])
                    g, half, q = three
                    hold(pool, xo_done, g, consts)
                    pool.tensor_tensor(xb[:, q, :, :], xgroup(g).rearrange("p (t d) -> p t d", t=GT),
                                       fbias[:, :].unsqueeze(1).to_broadcast([P, GT, D]), ALU.add).then_inc(xb_done, 1)

            over_groups(pool, NG, 3, last_pass)

        @block.scalar
        def _(act):
            act.wait_ge(par_in, PARAMS)
            act.activation(tx[:, :], gx[:, :], ACT.Tanh).then_inc(act_setup, 1)
            act.activation(tf[:, :], gf[:, :], ACT.Tanh).then_inc(act_setup, 1)

            def first_pass(at):
                one, two, three = at
                if one:
                    g, half, q = one
                    ln1.act_guess(act, g)
                    act.wait_ge(ct_done, g + 1)
                    act.activation(kt[:, q, :], bank[1][:, :], ACT.Copy).then_inc(kt_done, 1)
                if two:
                    g, half, q = two
                    act.wait_ge(lcap_done, g + 1)
                    act.activation(ex[:, q, :], ex[:, q, :], ACT.Exp).then_inc(ex_done, 1)
                if one:
                    g, half, q = one
                    act.wait_ge(xt1_done, g + 1)
                    act.activation(qt[:, q, :], bank[0][:, :], ACT.Copy).then_inc(qt_done, 1)
                    hold(act, kp_done, g + 1, consts)
                    act.activation(kpt[:, bass.ds(g * GW, GW)], bank[1][:, :], ACT.Identity,
                                   bias=pc[:, 0:1]).then_inc(kpt_done, 1)
                if three:
                    g, half, q = three
                    ln2.act_guess(act, g)
                if one:
                    g, half, q = one
                    act.wait_ge(gate_steps, nth(g, 2, 3))
                    act.activation(eneg[:, :], negabs[:, :], ACT.Exp).then_inc(gate_act, 1)
                    act.wait_ge(gate_act, nth(g, 1, 2))
                    act.activation(softp[:, :], eneg[:, :], ACT.Ln, bias=1.0).then_inc(gate_act, 1)
                if two:
                    g, half, q = two
                    act.wait_ge(n_done, nth(g, 1, 4))
                    act.activation(sq[:, :, :, :],
                                   heads[:, :, 256:256 + GT * HA].rearrange("p h (t d) -> p h t d", d=HA)[:, :, :, 0:HD],
                                   ACT.Square).then_inc(sq_done, 1)
                if three:
                    g, half, q = three
                    act.wait_ge(xt2_ps, g + 1)
                    act.activation(xt2[:, :], bank[7][:, :], ACT.Copy).then_inc(xt2_done, 1)
                if two:
                    g, half, q = two
                    act.wait_ge(z_done, nth(g, 1, 4))
                    act.activation(zz[:, 1, :, :], zz[:, 0, :, :], ACT.Ln).then_inc(z_act, 1)
                    act.wait_ge(z_act, nth(g, 1, 2))
                    act.activation(zz[:, 2, :, :], zz[:, 1, :, :], ACT.Exp, scale=-0.5).then_inc(z_act, 1)
                if one:
                    g, half, q = one
                    act.wait_ge(mtok_done, g + 1)
                    need(act, n_done, nth(g - 2, 1, 4))
                    act.activation(em[:, q, :], mtok[:, :], ACT.Exp, scale=-1.0).then_inc(em_done, 1)
                if three:
                    g, half, q = three
                    act.wait_ge(route, nth(g, 2, 6))
                    act.activation(rt[:, 1, :, :], rt[:, 0, :, :], ACT.Exp).then_inc(route_act, 1)

            act.preload_act_table_set("natural_log_exp_and_others")
            over_groups(act, NG, 3, first_pass)

            def gelu(s, e):
                for c in range(FC):
                    hold(act, h_ps, nth(s, c + 1, FC), consts)
                    if c == 0:
                        hold(act, y_ps, s - 1, consts)
                    col = cols[:, bass.ds(e * FC + c, 1)]
                    act.activation(ht[:, s_par, c, :], heads[:, c, :], ACT.Gelu_apprx_tanh,
                                   bias=col).then_inc(h_done, 1)

            s_par = 0
            for s in range(2):
                s_par = s
                gelu(s, 0)
            with act.Fori(1, E) as e:
                for j in range(2):
                    s_par = j
                    gelu(e * 2 + j, e)

            def last_pass(at):
                one, two, three = at
                if one:
                    g, half, q = one
                    ln3.act_guess(act, g)
                if three:
                    ln4.act_guess(act, three[0])
                if two:
                    g, half, q = two
                    act.wait_ge(sm_steps, nth(g, 3, 3))
                    act.activation(pr[:, :, :], sm[:, 1, :, :], ACT.Exp).then_inc(pr_done, 1)
                if one:
                    g, half, q = one
                    act.wait_ge(q3_ps, g + 1)
                    act.activation(qt3[:, :], bank[0][:, :], ACT.Copy).then_inc(q3_done, 1)
                if two:
                    g, half, q = two
                    act.wait_ge(prt_ps, g + 1)
                    act.activation(prt[:, :, :].rearrange("p u n -> p (u n)"), heads[:, 1, 0:2 * P], ACT.Copy).then_inc(prt_done, 1)
                if one:
                    g, half, q = one
                    act.wait_ge(qp_ps, g + 1)
                    act.activation(qp[:, q, :], bank[1][:, :], ACT.Identity, bias=pc[:, 0:1]).then_inc(qp_done, 1)
                if three:
                    g, half, q = three
                    act.wait_ge(xt4_ps, g + 1)
                    act.activation(xt4[:, :], bank[6][:, :], ACT.Copy).then_inc(xt4_done, 1)

            act.preload_act_table_set("natural_log_exp_and_others")
            over_groups(act, NG, 3, last_pass)

        @block.tensor
        def _(pe):
            pe.wait_ge(consts, CONSTS)
            pe.wait_ge(par_in, PARAMS)
            pe.transpose(bank[0][:, 0:40], rows[0:40, :], ident[0:40, 0:40]).then_inc(pe_setup, 1)
            pe.transpose(bank[0][:, 128:256], pw2_sb[:, :], ident[:, :]).then_inc(pe_setup, 1)
            pe.wait_ge(dve_setup, 8)
            pe.matmul(bank[0][:, 256:384], pw1_sb[:, :], pw2t[:, :], start=True, stop=True).then_inc(pe_setup, 1)
            pe.matmul(bank[1][:, 0:1], pw2t[:, :], cols[:, PB1:PB1 + 1], start=True, stop=True).then_inc(pe_setup, 1)
            pe.transpose(bank[1][:, 128:256], cbs[:, :], ident[:, :]).then_inc(pe_setup, 1)
            pe.wait_ge(dve_setup, 11)

            def first_pass(at):
                one, two, three = at
                if one:
                    g, half, q = one
                    pe.wait_ge(ctx_in[q], half * 16 + 16)
                    need(pe, kpt_done, g)
                    for t in range(GT):
                        last = pe.transpose(bank[1][:, t * P:(t + 1) * P], ctxb[:, q, t, :], ident[:, :])
                    last.then_inc(ct_done, 1)
                if two:
                    g, half, q = two
                    pe.wait_ge(qt_done, g + 1)
                    pe.wait_ge(kt_done, g + 1)
                    need(pe, hs_done, g)
                    for h in range(NH):
                        hp = slice(h * HD, (h + 1) * HD)
                        for b in range(BG):
                            bp = slice(b * S, (b + 1) * S)
                            last = pe.matmul(heads[(b % 2) * S:(b % 2 + 1) * S, h, (b // 2) * S:(b // 2 + 1) * S],
                                             kt[hp, q, bp], qt[hp, q, bp], start=True, stop=True)
                        last.then_inc(scores_done, 1)
                if one:
                    g, half, q = one
                    pe.wait_ge(ln1.applied, g + 1)
                    need(pe, qt_done, g)
                    for t in range(GT):
                        last = pe.transpose(bank[0][:, t * P:(t + 1) * P], xn1[:, t, :], ident[:, :])
                    last.then_inc(xt1_done, 1)
                    pe.wait_ge(kt_done, g + 1)
                    pe.matmul(bank[1][:, :], pa[:, :], kt[:, q, :], start=True, stop=True).then_inc(kp_done, 1)
                    pe.wait_ge(qt_done, g + 1)
                    need(pe, mtok_done, g)
                    for t in range(GT):
                        o = bank[6][:, t * 2 * NH:(t + 1) * 2 * NH]
                        pe.matmul(o, qt[:, q, t * P:(t + 1) * P], kq[:, :], start=True, stop=False)
                        last = pe.matmul(o, kt[:, q, t * P:(t + 1) * P], kc[:, :], start=False, stop=True)
                    last.then_inc(gates_ps, 1)
                if three:
                    g, half, q = three
                    pe.wait_ge(ln2.applied, g + 1)
                    need(pe, slot_done, g)
                    for t in range(GT):
                        last = pe.transpose(bank[7][:, t * P:(t + 1) * P], xn2[:, q, t, :], ident[:, :])
                    last.then_inc(xt2_ps, 1)
                if two:
                    g, half, q = two
                    for h in range(NH):
                        hold(pe, cw_done, nth(g, h + 1, NH), consts)
                        for b in range(BG):
                            bp = slice((b % 2) * S, (b % 2 + 1) * S)
                            t = b // 2
                            last = pe.matmul(heads[bp, h, 256 + t * HA:256 + (t + 1) * HA],
                                             cw[bp, h, t, :], vaug[bp, q, t, h, :], start=True, stop=True)
                        last.then_inc(pv_done, 1)
                if one:
                    g, half, q = one
                    pe.wait_ge(gate_steps, nth(g, 3, 3))
                    pe.matmul(bank[6][:, 64:64 + R], tri[:, :], logf[:, :], start=True, stop=True).then_inc(f_ps, 1)
                if three:
                    g, half, q = three
                    pe.wait_ge(xt2_done, g + 1)
                    for t in range(GT):
                        last = pe.matmul(bank[7][:, t * E:(t + 1) * E], xt2[:, t * P:(t + 1) * P], wg_sb[:, :], start=True, stop=True)
                    last.then_inc(logits_ps, 1)
                if one:
                    g, half, q = one
                    pe.wait_ge(a_done, g + 1)
                    pe.transpose(bank[6][0:R, 128:256], am[:, q, :], ident[:, :]).then_inc(at_ps, 1)
                    hold(pe, mrow_done, g + 1, consts)
                    pe.transpose(bank[6][:, 256:256 + R], mrow[:, q, :], ident[0:R, 0:R]).then_inc(mt_ps, 1)
                if three:
                    g, half, q = three
                    pe.wait_ge(onehot_done, g + 1)
                    W = (GT + 1) * E
                    cum = bank[7][:, 128:128 + W]
                    pe.matmul(cum, tri_b[:, :], onehot[:, :, :].rearrange("p t e -> p (t e)"), start=True, stop=False)
                    for t in range(GT):
                        last = pe.matmul(cum[:, (t + 1) * E:W], ones_b[:, :],
                                         onehot[:, t:t + 1, :].to_broadcast([P, GT - t, E]),
                                         start=False, stop=(t == GT - 1))
                    last.then_inc(cum_ps, 1)

            over_groups(pe, NG, 3, first_pass)

            def turn_and_up(s, half, q, wq):
                pe.wait_ge(xe_in[q], half * 16 + 16)
                need(pe, xet_done, s)
                for t in range(GT):
                    last = pe.transpose(bank[0][:, t * P:(t + 1) * P], xe[:, q, t, :], ident[:, :])
                last.then_inc(xet_ps, 1)
                pe.wait_ge(xet_done, s + 1)
                for c in range(FC):
                    need(pe, h_done, nth(s - 1, c + 1, FC))
                    pe.matmul(heads[:, c, :], w1_sb[:, wq, c * P:(c + 1) * P], xet[:, :], start=True, stop=True).then_inc(h_ps, 1)

            def down(s, q, wq):
                pe.wait_ge(h_done, nth(s, FC, FC))
                need(pe, y_done, s)
                for t in range(GT):
                    for c in range(FC):
                        last = pe.matmul(bank[6][:, t * D:(t + 1) * D], ht[:, q, c, t * P:(t + 1) * P], w2_sb[:, wq, c, :],
                                         start=(c == 0), stop=(c == FC - 1))
                last.then_inc(y_ps, 1)

            def expert_quad(quad, first=False):
                for j in range(4):
                    s = quad * 4 + j
                    if j % 2 == 0:
                        pe.wait_ge(w_in[j // 2], quad * 32 + 32)
                    turn_and_up(s, quad * 2 + j // 2, j % 2, j // 2)
                    if not (first and j == 0):
                        down(s - 1, (j - 1) % 2, ((j - 1) % 4) // 2)

            need(pe, hs_done, NG)
            pe.wait_ge(x1_done, NG)
            expert_quad(0, first=True)
            with pe.Fori(1, E // 2) as quad:
                expert_quad(quad)
            down(NG - 1, 1, 1)

            def last_pass(at):
                one, two, three = at
                if two:
                    g, half, q = two
                    pe.wait_ge(qp_done, g + 1)
                    pe.wait_ge(kpr_in[q], half * 16 + 16)
                    need(pe, sm_steps, nth(g - 1, 1, 3))
                    for b in range(BG):
                        u, p, c = b // 4, b // 2 % 2, b % 2
                        last = pe.matmul(heads[p * S:(p + 1) * S, 0, (2 * u + c) * S:(2 * u + c + 1) * S],
                                         qp[:, q, b * S:(b + 1) * S], kpr[:, q, b * S:(b + 1) * S], start=True, stop=True)
                    last.then_inc(s3_ps, 1)
                if one:
                    g, half, q = one
                    pe.wait_ge(ln3.applied, g + 1)
                    need(pe, q3_done, g)
                    for t in range(GT):
                        last = pe.transpose(bank[0][:, t * P:(t + 1) * P], xn3[:, t, :], ident[:, :])
                    last.then_inc(q3_ps, 1)
                if three:
                    g, half, q = three
                    pe.wait_ge(ln4.applied, g + 1)
                    need(pe, xt4_done, g)
                    for t in range(GT):
                        last = pe.transpose(bank[6][:, t * P:(t + 1) * P], xn4[:, t, :], ident[:, :])
                    last.then_inc(xt4_ps, 1)
                if one:
                    g, half, q = one
                    pe.wait_ge(q3_done, g + 1)
                    need(pe, qp_done, g)
                    pe.matmul(bank[1][:, :], pa[:, :], qt3[:, :], start=True, stop=True).then_inc(qp_ps, 1)
                if two:
                    g, half, q = two
                    pe.wait_ge(pr_done, g + 1)
                    need(pe, prt_done, g)
                    for u in range(2):
                        last = pe.transpose(heads[:, 1, u * P:(u + 1) * P],
                                            pr[:, 2 * u:2 * u + 2, :].rearrange("p c k -> p (c k)"), ident[:, :])
                    last.then_inc(prt_ps, 1)
                    hold(pe, prt_done, g + 1, consts)
                    pe.wait_ge(v_in[q], half * 16 + 16)
                    need(pe, x3_done, g)
                    for b in range(BG):
                        u, p, c = b // 4, b // 2 % 2, b % 2
                        t = b // 2
                        cp = slice(c * S, (c + 1) * S)
                        last = pe.matmul(heads[cp, 2 + t // 2, (t % 2) * (D + 1):(t % 2 + 1) * (D + 1)],
                                         prt[cp, u, p * S:(p + 1) * S], ctxv[cp, q, t, :], start=True, stop=True)
                    last.then_inc(o3_ps, 1)
                if three:
                    g, half, q = three
                    pe.wait_ge(xt4_done, g + 1)
                    need(pe, xo_done, g)
                    for t in range(GT):
                        last = pe.matmul(bank[7][:, t * D:(t + 1) * D], xt4[:, t * P:(t + 1) * P], cbt[:, :], start=True, stop=True)
                    last.then_inc(f_out_ps, 1)

            over_groups(pe, NG, 3, last_pass)

        @block.vector
        def _(dve):
            dve.wait_ge(par_in, PARAMS)
            dve.tensor_tensor(kc[:, :], kk[:, :], kv[:, :], ALU.add).then_inc(dve_setup, 1)
            dve.wait_ge(act_setup, 2)
            dve.tensor_scalar(rmsw[:, :], rmsb[:, :], 1.0, tx[:, 0:1], ALU.add, ALU.mult).then_inc(dve_setup, 1)
            dve.wait_ge(dve_setup, 2)
            dve.tensor_copy(head_w[:, :].rearrange("p (h d) -> p h d", h=NH),
                            rmsw[:, :].unsqueeze(1).to_broadcast([P, NH, HD])).then_inc(dve_setup, 1)
            dve.tensor_scalar(fbias[:, :], cbias_b[:, :], tf[:, 1:2], None, ALU.mult).then_inc(dve_setup, 1)
            dve.wait_ge(pe_setup, 2)
            dve.tensor_copy(cols[:, :], bank[0][:, 0:40]).then_inc(dve_setup, 1)
            dve.tensor_copy(pw2t[:, :], bank[0][:, 128:256]).then_inc(dve_setup, 1)
            dve.wait_ge(dve_setup, 5)
            dve.tensor_scalar(scb_t[:, :], cols[:, SCBC:SCBC + 1], 1.0 / 127.0, tf[:, 1:2], ALU.mult, ALU.mult).then_inc(dve_setup, 1)
            dve.wait_ge(dve_setup, 7)
            dve.tensor_scalar(cbs[:, :], cb_sb[:, :], scb_t[:, 0:1], None, ALU.mult).then_inc(dve_setup, 1)
            dve.wait_ge(pe_setup, 5)
            dve.tensor_copy(pa[:, :], bank[0][:, 256:384]).then_inc(dve_setup, 1)
            dve.tensor_tensor(pc[:, :], bank[1][:, 0:1], cols[:, PB2:PB2 + 1], ALU.add).then_inc(dve_setup, 1)
            dve.tensor_copy(cbt[:, :], bank[1][:, 128:256]).then_inc(dve_setup, 1)

            def first_pass(at):
                one, two, three = at
                if one:
                    g, half, q = one
                    hold(dve, x_in[q], half * 16 + 16, consts)
                    ln1.dve_stats(dve, g, xtile(g))
                if two:
                    g, half, q = two
                    dve.wait_ge(l_done, g + 1)
                    e3 = ex[:, q, :].rearrange("p (r i) -> p r i", i=S)
                    dve.tensor_tensor(e3, e3, cap[:, :].unsqueeze(1).to_broadcast([P, R, S]), ALU.min).then_inc(lcap_done, 1)
                if one:
                    g, half, q = one
                    need(dve, xt1_done, g)
                    ln1.dve_apply(dve, g, lambda t: xn1[:, t, :], xtile(g))
                if three:
                    g, half, q = three
                    hold(dve, x1_done, g + 1, consts)
                    ln2.dve_stats(dve, g, xtile(g))
                if two:
                    g, half, q = two
                    dve.wait_ge(ex_done, g + 1)
                    e4 = ex[:, q, :].rearrange("p (t h i) -> p t h i", t=GT, h=NH)
                    for h in range(NH):
                        dve.wait_ge(scores_done, nth(g, h + 1, NH))
                        need(dve, pv_done, nth(g - 1, h + 1, NH))
                        dve.scalar_tensor_tensor(out=cw[:, h, :, :],
                                                 in0=heads[:, h, 0:GT * S].rearrange("p (t i) -> p t i", t=GT),
                                                 scalar=float(HD) ** -0.5, in1=e4[:, :, h, :],
                                                 op0=ALU.mult, op1=ALU.mult).then_inc(cw_done, 1)
                if one:
                    g, half, q = one
                    dve.wait_ge(gates_ps, g + 1)
                    dve.tensor_tensor(gates[:, :, :].rearrange("p k (t h) -> p k t h", t=GT),
                                      bank[6][:, 0:2 * R].rearrange("p (t k h) -> p k t h", t=GT, k=2),
                                      gate_bias[:, :].rearrange("p (k h) -> p k h", k=2).unsqueeze(2).to_broadcast([P, 2, GT, NH]),
                                      ALU.add).then_inc(gate_steps, 1)
                    dve.wait_ge(gate_steps, nth(g, 1, 3))
                    dve.scalar_tensor_tensor(out=negabs[:, :], in0=gates[:, 1, :], scalar=-1.0, in1=gates[:, 1, :],
                                             op0=ALU.mult, op1=ALU.min).then_inc(gate_steps, 1)
                if three:
                    g, half, q = three
                    if not isinstance(g, int) or g >= 2:
                        dve.wait_ge(scattered[q], half * (16 * GT))
                    ln2.dve_apply(dve, g, lambda t: xn2[:, q, t, :], xtile(g))
                if one:
                    g, half, q = one
                    dve.wait_ge(gate_act, nth(g, 2, 2))
                    dve.scalar_tensor_tensor(out=logf[:, :], in0=gates[:, 1, :], scalar=0.0, in1=softp[:, :],
                                             op0=ALU.min, op1=ALU.subtract).then_inc(gate_steps, 1)
                if two:
                    g, half, q = two
                    dve.wait_ge(pv_done, nth(g, NH, NH))
                    dve.wait_ge(em_done, g + 1)
                    o4 = heads[:, :, 256:256 + GT * HA].rearrange("p h (t d) -> p h t d", d=HA)
                    dve.tensor_tensor(nn[:, 0, :, :], o4[:, :, :, HD], em[:, q, :].rearrange("p (t h) -> p h t", t=GT),
                                      ALU.max).then_inc(n_done, 1)
                    dve.wait_ge(n_done, nth(g, 1, 4))
                    dve.tensor_scalar(nn[:, 1, :, :], nn[:, 0, :, :], 1e-6, None, ALU.add).then_inc(n_done, 1)
                    dve.wait_ge(n_done, nth(g, 2, 4))
                    dve.scalar_tensor_tensor(out=nn[:, 2, :, :], in0=nn[:, 1, :, :], scalar=1e-6, in1=nn[:, 1, :, :],
                                             op0=ALU.mult, op1=ALU.mult).then_inc(n_done, 1)
                if one:
                    g, half, q = one
                    dve.wait_ge(f_ps, g + 1)
                    dve.tensor_copy(fcum[:, :], bank[6][:, 64:64 + R]).then_inc(gate_copy, 1)
                    dve.wait_ge(gate_copy, g + 1)
                    need(dve, l_done, g - 1)
                    dve.tensor_tensor(am[:, q, :], gates[:, 0, :], fcum[:, :], ALU.subtract).then_inc(a_done, 1)
                if two:
                    g, half, q = two
                    dve.wait_ge(sq_done, g + 1)
                    dve.tensor_reduce(ss[:, :, :], sq[:, :, :, :], AX, ALU.add).then_inc(n_done, 1)
                    dve.wait_ge(n_done, nth(g, 4, 4))
                    dve.scalar_tensor_tensor(out=zz[:, 0, :, :], in0=ss[:, :, :], scalar=1.0 / HD, in1=nn[:, 2, :, :],
                                             op0=ALU.mult, op1=ALU.add).then_inc(z_done, 1)
                if one:
                    g, half, q = one
                    dve.wait_ge(at_ps, g + 1)
                    if not isinstance(g, int) or g >= 2:
                        dve.wait_ge(m_out[q], half * 16)
                    dve.tensor_tensor_scan(mrow[:, q, :], reset[:, :], bank[6][0:R, 128:256], 0.0, ALU.add, ALU.max).then_inc(mrow_done, 1)
                if three:
                    g, half, q = three
                    lg = bank[7][:, 0:GT * E].rearrange("p (t e) -> p t e", t=GT)
                    dve.wait_ge(logits_ps, g + 1)
                    dve.tensor_reduce(rs[:, 8, :], lg, AX, ALU.max).then_inc(route, 1)
                    dve.wait_ge(route, nth(g, 1, 6))
                    dve.tensor_tensor(rt[:, 0, :, :], lg, rs[:, 8, :].unsqueeze(2).to_broadcast([P, GT, E]), ALU.subtract).then_inc(route, 1)
                    dve.wait_ge(route, nth(g, 2, 6))
                    dve.scalar_tensor_tensor(out=rt[:, 2, :, :].rearrange("p t e -> p t e"), in0=rt[:, 0, :, :], scalar=0.0,
                                             in1=prio[:, :].unsqueeze(1).to_broadcast([P, GT, E]),
                                             op0=ALU.is_ge, op1=ALU.mult).then_inc(route, 1)
                    dve.wait_ge(route, nth(g, 3, 6))
                    need(dve, idx_steps, nth(g - 1, 11, 11))
                    dve.tensor_reduce(rs[:, 1, :], rt[:, 2, :, :], AX, ALU.max).then_inc(route, 1)
                    dve.wait_ge(route, nth(g, 4, 6))
                    dve.tensor_tensor(onehot[:, 0:GT, :], rt[:, 2, :, :],
                                      rs[:, 1, :].unsqueeze(2).to_broadcast([P, GT, E]), ALU.is_equal).then_inc(onehot_done, 1)
                if one:
                    g, half, q = one
                    dve.wait_ge(mt_ps, g + 1)
                    dve.tensor_tensor(mtok[:, :], bank[6][:, 256:256 + R], fcum[:, :], ALU.add).then_inc(mtok_done, 1)
                if two:
                    g, half, q = two
                    dve.wait_ge(z_act, nth(g, 2, 2))
                    dve.tensor_tensor(zz[:, 3, :, :], zz[:, 2, :, :], zz[:, 2, :, :], ALU.mult).then_inc(z_done, 1)
                    dve.wait_ge(z_done, nth(g, 2, 4))
                    dve.scalar_tensor_tensor(out=zz[:, 4, :, :], in0=zz[:, 3, :, :], scalar=-0.5, in1=zz[:, 0, :, :],
                                             op0=ALU.mult, op1=ALU.mult).then_inc(z_done, 1)
                    dve.wait_ge(z_done, nth(g, 3, 4))
                    dve.scalar_tensor_tensor(out=zz[:, 5, :, :], in0=zz[:, 4, :, :], scalar=1.5, in1=zz[:, 2, :, :],
                                             op0=ALU.add, op1=ALU.mult).then_inc(z_done, 1)
                    dve.wait_ge(z_done, nth(g, 4, 4))
                    for h in range(NH):
                        last = dve.tensor_tensor(hs[:, q, :, h * HD:(h + 1) * HD],
                                                 heads[:, h, 256:256 + GT * HA].rearrange("p (t d) -> p t d", d=HA)[:, :, 0:HD],
                                                 zz[:, 5, h, :].unsqueeze(2).to_broadcast([P, GT, HD]), ALU.mult)
                    last.then_inc(hs_done, 1)
                if three:
                    g, half, q = three
                    dve.wait_ge(route_act, g + 1)
                    dve.tensor_reduce(rs[:, 9, :], rt[:, 1, :, :], AX, ALU.add).then_inc(route, 1)
                    dve.wait_ge(route, nth(g, 5, 6))
                    dve.reciprocal(rs[:, 2, :], rs[:, 9, :]).then_inc(route, 1)
                    dve.wait_ge(cum_ps, g + 1)
                    cum = bank[7][:, 128:128 + (GT + 1) * E].rearrange("p (t e) -> p t e", e=E)
                    dve.tensor_tensor(rt[:, 3, :, :], cum[:, 0:GT, :], carry[:, q:q + 1, :].to_broadcast([P, GT, E]), ALU.add).then_inc(slot_steps, 1)
                    dve.tensor_tensor(carry[:, 1 - q, :], cum[:, GT, :], carry[:, q, :], ALU.add).then_inc(slot_steps, 1)
                    dve.wait_ge(slot_steps, nth(g, 2, 3))
                    dve.tensor_tensor(rt[:, 4, :, :], rt[:, 3, :, :], onehot[:, 0:GT, :], ALU.mult).then_inc(slot_steps, 1)
                    dve.wait_ge(slot_steps, nth(g, 3, 3))
                    dve.tensor_reduce(rs[:, 0, :], rt[:, 4, :, :], AX, ALU.add).then_inc(slot_done, 1)
                if two:
                    g, half, q = two
                    dve.wait_ge(hsw_done, g + 1)
                    dve.tensor_tensor(xgroup(g), xgroup(g), hs[:, q, :, :].rearrange("p t d -> p (t d)"), ALU.add).then_inc(x1_done, 1)

            gate_copy = sem("gate_copy")
            slot_steps = sem("slot_steps")
            dve.wait_ge(consts, CONSTS)
            over_groups(dve, NG, 3, first_pass)

            dve.wait_ge(par_in, PARAMS + 16 * E)

            def evac_x(s):
                dve.wait_ge(xet_ps, s + 1)
                need(dve, h_ps, nth(s - 1, FC, FC))
                dve.tensor_copy(xet[:, :], bank[0][:, :]).then_inc(xet_done, 1)

            def evac_y(s, q, e):
                dve.wait_ge(y_ps, s + 1)
                if not isinstance(s, int) or s >= 2:
                    dve.wait_ge(y_out[q], e * 16)
                dve.tensor_tensor(ye[:, q, :, :], bank[6][:, :].rearrange("p (t d) -> p t d", t=GT),
                                  b2b[:, bass.ds(e, 1), :].to_broadcast([P, GT, D]), ALU.add).then_inc(y_done, 1)

            evac_x(0)
            evac_x(1)
            evac_y(0, 0, 0)
            evac_x(2)
            evac_y(1, 1, 0)
            evac_x(3)
            evac_y(2, 0, 1)
            with dve.Fori(2, E) as e:
                evac_x(e * 2)
                evac_y(e * 2 - 1, 1, e - 1)
                evac_x(e * 2 + 1)
                evac_y(e * 2, 0, e)
            evac_y(NG - 1, 1, E - 1)

            def last_pass(at):
                one, two, three = at
                if one:
                    g, half, q = one
                    dve.tensor_scalar(rsum[:, 0, :], gw[:, tiles(g)], tf[:, 0:1], None, ALU.mult).then_inc(gwt_done, 1)
                    dve.wait_ge(gwt_done, g + 1)
                    dve.wait_ge(yg_in[q], half * (16 * GT) + 16 * GT)
                    for t in range(GT):
                        last = dve.scalar_tensor_tensor(out=xtile(g)(t), in0=yg[:, q, t, :], scalar=rsum[:, 0, t:t + 1],
                                                        in1=xtile(g)(t), op0=ALU.mult, op1=ALU.add)
                    last.then_inc(x2_done, 1)
                    hold(dve, x2_done, g + 1, consts)
                    ln3.dve_stats(dve, g, xtile(g))
                if two:
                    g, half, q = two
                    dve.wait_ge(s3_ps, g + 1)
                    dve.scalar_tensor_tensor(out=sm[:, 0, :, :], in0=heads[:, 0, 0:GT * S].rearrange("p (c k) -> p c k", k=S),
                                             scalar=float(D) ** -0.5, in1=mask[:, :].unsqueeze(1).to_broadcast([P, GT, S]),
                                             op0=ALU.mult, op1=ALU.add).then_inc(sm_steps, 1)
                    dve.wait_ge(sm_steps, nth(g, 1, 3))
                    dve.tensor_reduce(smx[:, :], sm[:, 0, :, :], AX, ALU.max).then_inc(sm_steps, 1)
                    dve.wait_ge(sm_steps, nth(g, 2, 3))
                    need(dve, pr_done, g)
                    dve.tensor_tensor(sm[:, 1, :, :], sm[:, 0, :, :], smx[:, :].unsqueeze(2).to_broadcast([P, GT, S]),
                                      ALU.subtract).then_inc(sm_steps, 1)
                if three:
                    g, half, q = three
                    hold(dve, x3_done, g + 1, consts)
                    ln4.dve_stats(dve, g, xtile(g))
                if one:
                    g, half, q = one
                    need(dve, q3_ps, g)
                    ln3.dve_apply(dve, g, lambda t: xn3[:, t, :], xtile(g))
                if three:
                    g, half, q = three
                    need(dve, xt4_ps, g)
                    ln4.dve_apply(dve, g, lambda t: xn4[:, t, :], xtile(g))
                if two:
                    g, half, q = two
                    dve.wait_ge(o3_ps, g + 1)
                    o = heads[:, 2:4, 0:2 * (D + 1)].rearrange("p b (t d) -> p b t d", d=D + 1)
                    dve.reciprocal(rsum[:, 1, :].rearrange("p (b t) -> p b t", b=2), o[:, :, :, D]).then_inc(o3_steps, 1)
                    dve.wait_ge(o3_steps, nth(g, 1, 2))
                    dve.tensor_scalar(smx3[:, :], rsum[:, 1, :], tx[:, 1:2], None, ALU.mult).then_inc(o3_steps, 1)
                    dve.wait_ge(o3_steps, nth(g, 2, 2))
                    for t in range(GT):
                        last = dve.scalar_tensor_tensor(out=xtile(g)(t), in0=o[:, t // 2, t % 2, 0:D], scalar=smx3[:, t:t + 1],
                                                        in1=xtile(g)(t), op0=ALU.mult, op1=ALU.add)
                    last.then_inc(x3_done, 1)
                if three:
                    g, half, q = three
                    dve.wait_ge(f_out_ps, g + 1)
                    dve.wait_ge(xb_done, g + 1)
                    if not isinstance(g, int) or g >= 2:
                        dve.wait_ge(stored[q], half * 16)
                    dve.tensor_tensor(xo[:, q, :, :], bank[7][:, :].rearrange("p (t d) -> p t d", t=GT), xb[:, q, :, :],
                                      ALU.add).then_inc(xo_done, 1)

            gwt_done = sem("gwt_done")
            smx3 = sb("smx3", [P, GT])
            over_groups(dve, NG, 3, last_pass)


_INS = ['x', 'ctx_1024', 'fside_1xSxS2_0', 'g_xattn', 'g_ffn', 'L0_xattn_igate_kernel', 'L0_xattn_igate_bias',
        'L0_xattn_fgate_kernel', 'L0_xattn_fgate_bias', 'L0_xattn_rms_scale', 'L0_ffn_wg', 'L0_ffn_w1', 'L0_ffn_b1',
        'L0_ffn_w2', 'L0_ffn_b2', 'L1_xattn_W1', 'L1_xattn_b1', 'L1_xattn_W2', 'L1_xattn_b2', 'L1_ffn_CB',
        'L1_ffn_SCB', 'L1_ffn_bias']
_OUTS = [((128, 64, 128), 'float32')]


def kernel(**inputs):
    import numpy as _np
    import concourse.bacc as _bacc
    from concourse import mybir as _mybir
    from concourse.bass_utils import run_bass_kernel_spmd as _run

    nc = _bacc.Bacc("TRN2", target_bir_lowering=False, num_devices=1)
    arrays, args = {}, []
    for name in _INS:
        a = _np.ascontiguousarray(inputs[name])
        arrays[f"in_{name}_dram"] = a
        args.append(nc.dram_tensor(f"in_{name}_dram", a.shape, _mybir.dt.from_np(a.dtype), kind="ExternalInput").ap())
    for i, (shape, dtype) in enumerate(_OUTS):
        dt = _mybir.dt.from_np(_np.dtype(dtype))
        args.append(nc.dram_tensor(f"out_{i}_dram", shape, dt, kind="ExternalOutput").ap())
    flamingo(nc, *args)
    r = _run(nc, [arrays], core_ids=[0])
    return r.results[0]["out_0_dram"]
```

```python
from contextlib import ExitStack

import concourse.bass as bass
from concourse import mybir

F32 = mybir.dt.float32
BF16 = mybir.dt.bfloat16
I32 = mybir.dt.int32
ALU = mybir.AluOpType
ACT = mybir.ActivationFunctionType
AX = mybir.AxisListType.X

P = 128
GT = 4
GW = GT * P
LN_EPS = 1e-5
MASKED = -1e30


def nth(g, k, n):
    return g * n + k


def need(eng, sem, value):
    if isinstance(value, int) and value <= 0:
        return
    eng.wait_ge(sem, value)


def hold(eng, sem, value, go):
    if not isinstance(value, int):
        value = eng.to_reg(value)
        eng.wait_ge(go, 1)
    need(eng, sem, value)


def over_groups(eng, groups, stages, body):
    def step(half, parity, static):
        at = []
        for s in range(stages):
            back = s - parity
            h, q = (half, parity - s) if back <= 0 else (half - (back + 1) // 2, (parity - s) % 2)
            g = h * 2 + q
            at.append(None if static and not 0 <= g < groups else (g, h, q))
        body(at)

    first = (stages + 1) // 2
    for k in range(2 * first):
        step(k // 2, k % 2, True)
    with eng.Fori(first, groups // 2) as half:
        step(half, 0, False)
        step(half, 1, False)
    for k in range(groups, groups + stages - 1):
        step(k // 2, k % 2, True)


class Norm:

    def __init__(self, name, sb, sem, go):
        self.go = go
        self.stats = sb(f"{name}_stats", [P, GT, 6])
        self.mv = sb(f"{name}_mv", [P, GT, 2])
        self.ve = sb(f"{name}_ve", [P, GT])
        self.log = sb(f"{name}_log", [P, GT])
        self.y0 = sb(f"{name}_y0", [P, GT])
        self.t = sb(f"{name}_t", [P, 2, GT])
        self.rstd = sb(f"{name}_rstd", [P, GT])
        self.stats_done = sem(f"{name}_stats_done")
        self.mv_done = sem(f"{name}_mv_done")
        self.ve_done = sem(f"{name}_ve_done")
        self.log_done = sem(f"{name}_log_done")
        self.y0_done = sem(f"{name}_y0_done")
        self.newton = sem(f"{name}_newton")
        self.applied = sem(f"{name}_applied")

    def dve_stats(self, dve, g, tile):
        for t in range(GT):
            last = dve.bn_stats(self.stats[:, t, :], tile(t))
        last.then_inc(self.stats_done, 1)
        hold(dve, self.stats_done, g + 1, self.go)
        for t in range(GT):
            last = dve.bn_aggr(self.mv[:, t, :], self.stats[:, t, :])
        last.then_inc(self.mv_done, 1)
        dve.wait_ge(self.mv_done, g + 1)
        dve.tensor_scalar(self.ve[:, :], self.mv[:, :, 1], LN_EPS, None, ALU.add).then_inc(self.ve_done, 1)

    def act_guess(self, act, g):
        act.wait_ge(self.ve_done, g + 1)
        act.activation(self.log[:, :], self.ve[:, :], ACT.Ln).then_inc(self.log_done, 1)
        act.wait_ge(self.log_done, g + 1)
        act.activation(self.y0[:, :], self.log[:, :], ACT.Exp, scale=-0.5).then_inc(self.y0_done, 1)

    def dve_newton(self, dve, g):
        dve.wait_ge(self.y0_done, g + 1)
        dve.tensor_tensor(self.t[:, 0, :], self.y0[:, :], self.y0[:, :], ALU.mult).then_inc(self.newton, 1)
        dve.wait_ge(self.newton, nth(g, 1, 3))
        dve.scalar_tensor_tensor(out=self.t[:, 1, :], in0=self.t[:, 0, :], scalar=-0.5, in1=self.ve[:, :],
                                 op0=ALU.mult, op1=ALU.mult).then_inc(self.newton, 1)
        dve.wait_ge(self.newton, nth(g, 2, 3))
        dve.scalar_tensor_tensor(out=self.rstd[:, :], in0=self.t[:, 1, :], scalar=1.5, in1=self.y0[:, :],
                                 op0=ALU.add, op1=ALU.mult).then_inc(self.newton, 1)

    def dve_apply(self, dve, g, out, tile):
        dve.wait_ge(self.newton, nth(g, 3, 3))
        for t in range(GT):
            last = dve.tensor_scalar(out(t), tile(t), self.mv[:, t, 0:1], self.rstd[:, t:t + 1],
                                     ALU.subtract, ALU.mult)
        last.then_inc(self.applied, 1)


def flamingo(nc, x, ctx_1024, fside, g_xattn, g_ffn, igate_kernel, igate_bias, fgate_kernel, fgate_bias,
             rms_scale, wg, w1, b1, w2, b2, pw1, pb1, pw2, pb2, CB, SCB, cbias, out):
    NB, S, D = x.shape
    N = NB * S
    NH = igate_kernel.shape[1]
    HD = D // NH
    E = wg.shape[1]
    F = w1.shape[2]
    FC = F // P
    CAP = max((N + E - 1) // E, 4)
    NT = N // P
    NG = N // GW
    BG = GW // S
    R = GT * NH
    HA = HD + 1
    assert D == P and S == P // 2 and CAP == 2 * GW and E * CAP == N and R == 16 and NG == 2 * E

    ctx = ExitStack()
    with ctx:
        def sb(name, shape, dt=F32):
            return ctx.enter_context(nc.sbuf_tensor("s_" + name, shape, dt))

        def sem(name):
            return ctx.enter_context(nc.semaphore(name))

        m_dram = [nc.dram_tensor(f"m_scratch{i}", (2, R * S), F32, kind="Internal").ap() for i in range(2)]
        slots_x = nc.dram_tensor("slots_x", (2 * N, D), F32, kind="Internal").ap()
        slots_y = nc.dram_tensor("slots_y", (N, D), F32, kind="Internal").ap()

        ident = sb("ident", [P, P])
        tri = sb("tri", [P, P])
        tri_b = sb("tri_b", [P, P], BF16)
        ones_b = sb("ones_b", [P, P], BF16)
        cap = sb("cap", [P, S])
        prio = sb("prio", [P, E])
        prio_i = sb("prio_i", [P, E], I32)
        trash_i = sb("trash_i", [P, NT], I32)
        trash = sb("trash", [P, NT])
        carry = sb("carry", [P, 2, E])
        carry_i = sb("carry_i", [P, E], I32)
        reset = sb("reset", [R, P])
        kq = sb("kq", [P, 2 * NH])
        kk = sb("kk", [P, 2 * NH])
        kv = sb("kv", [P, 2 * NH])
        kc = sb("kc", [P, 2 * NH])
        gate_bias = sb("gate_bias", [P, 2 * NH])
        gx = sb("gx", [P, 2])
        gf = sb("gf", [P, 2])
        tx = sb("tx", [P, 2])
        tf = sb("tf", [P, 2])
        rmsb = sb("rmsb", [P, HD])
        rmsw = sb("rmsw", [P, HD])
        head_w = sb("head_w", [P, D])
        wg_sb = sb("wg_sb", [P, E])
        pw1_sb = sb("pw1_sb", [P, P])
        pw2_sb = sb("pw2_sb", [P, P])
        pw2t = sb("pw2t", [P, P])
        cb_sb = sb("cb_sb", [P, P])
        cbs = sb("cbs", [P, P])
        cbt = sb("cbt", [P, P])
        rows = sb("rows", [P, P])
        cols = sb("cols", [P, 40])
        pa = sb("pa", [P, P])
        pc = sb("pc", [P, 1])
        scb_t = sb("scb_t", [P, 1])
        cbias_b = sb("cbias_b", [P, P])
        fbias = sb("fbias", [P, P])
        mask = sb("mask", [P, S])
        b2b = sb("b2b", [P, E, D])

        xs = sb("xs", [P, NT * D])
        kpt = sb("kpt", [P, N])
        gw = sb("gw", [P, NT])
        gidx = sb("gidx", [P, NT], I32)

        ctxb = sb("ctxb", [P, 2, GT, D])
        vaug = sb("vaug", [P, 2, GT, NH, HA])
        xn1 = sb("xn1", [P, GT, D])
        qt = sb("qt", [P, GW])
        kt = sb("kt", [P, 2, GW])
        gates = sb("gates", [P, 2, R])
        negabs = sb("negabs", [P, R])
        eneg = sb("eneg", [P, R])
        softp = sb("softp", [P, R])
        logf = sb("logf", [P, R])
        fcum = sb("fcum", [P, R])
        am = sb("am", [P, 2, R])
        mrow = sb("mrow", [R, 2, P])
        mtok = sb("mtok", [P, R])
        em = sb("em", [P, 2, R])
        mb = sb("mb", [P, 2, R * S])
        ex = sb("ex", [P, 2, R * S])
        cw = sb("cw", [P, GT, NH, S])
        sq = sb("sq", [P, GT, NH, HD])
        nn = sb("nn", [P, 3, R])
        ss = sb("ss", [P, R])
        zz = sb("zz", [P, 6, R])
        hs = sb("hs", [P, 2, GT, D])
        xn2 = sb("xn2", [P, 2, GT, D])
        xt2 = sb("xt2", [P, GW])
        rt = sb("rt", [P, 6, GT, E])
        onehot = sb("onehot", [P, GT + 1, E], BF16)
        rs = sb("rs", [P, 13, GT])
        sidx = sb("sidx", [P, 2, GT], I32)

        w1_sb = sb("w1_sb", [P, 2, F])
        w2_sb = sb("w2_sb", [P, 2, FC, D])
        xe = sb("xe", [P, 2, GT, D])
        xet = sb("xet", [P, GW])
        ht = sb("ht", [P, 2, FC, GW])
        ye = sb("ye", [P, 2, GT, D])

        yg = sb("yg", [P, 2, GT, D])
        kpr = sb("kpr", [P, 2, GW])
        gix = sb("gix", [P, 2, GT], I32)
        ctxv = sb("ctxv", [P, 2, GT, D + 1])
        xn3 = sb("xn3", [P, GT, D])
        qt3 = sb("qt3", [P, GW])
        qp = sb("qp", [P, 2, GW])
        sm = sb("sm", [P, 2, GT, S])
        smx = sb("smx", [P, GT])
        pr = sb("pr", [P, GT, S])
        prt = sb("prt", [P, 2, P])
        rsum = sb("rsum", [P, 2, GT])
        xn4 = sb("xn4", [P, GT, D])
        xt4 = sb("xt4", [P, GW])
        qbd = ht[:, :, :, :].rearrange("p q c n -> p q (c n)")
        zeros = xe[:, :, :, :].rearrange("p q t d -> p (q t d)")
        xo = mb[:, :, 0:GT * D].rearrange("p q (t d) -> p q t d", t=GT)
        xb = ex[:, :, 0:GT * D].rearrange("p q (t d) -> p q t d", t=GT)

        bank = [ctx.enter_context(nc.psum_tensor(f"bank{i}", [P, 512], F32)) for i in range(2)]
        heads = ctx.enter_context(nc.psum_tensor("heads", [P, 4, 512], F32))
        bank += [None] * 4 + [ctx.enter_context(nc.psum_tensor(f"bank{i}", [P, 512], F32)) for i in (6, 7)]

        par_in = sem("par_in")
        iotas = sem("iotas")
        consts = sem("consts")
        dve_setup = sem("dve_setup")
        act_setup = sem("act_setup")
        pe_setup = sem("pe_setup")
        filled = sem("filled")
        x_in = [sem(f"x_in{i}") for i in range(2)]
        ctx_in = [sem(f"ctx_in{i}") for i in range(2)]
        vaug_done = sem("vaug_done")
        xt1_done = sem("xt1_done")
        ct_done = sem("ct_done")
        qt_done = sem("qt_done")
        qbd_done = sem("qbd_done")
        kt_done = sem("kt_done")
        kp_done = sem("kp_done")
        kpt_done = sem("kpt_done")
        gates_ps = sem("gates_ps")
        gate_steps = sem("gate_steps")
        gate_act = sem("gate_act")
        f_ps = sem("f_ps")
        a_done = sem("a_done")
        at_ps = sem("at_ps")
        mrow_done = sem("mrow_done")
        m_out = [sem(f"m_out{i}") for i in range(2)]
        m_in = [sem(f"m_in{i}") for i in range(2)]
        mt_ps = sem("mt_ps")
        mtok_done = sem("mtok_done")
        em_done = sem("em_done")
        l_done = sem("l_done")
        lcap_done = sem("lcap_done")
        ex_done = sem("ex_done")
        scores_done = sem("scores_done")
        cw_done = sem("cw_done")
        pv_done = sem("pv_done")
        sq_done = sem("sq_done")
        n_done = sem("n_done")
        ss_done = sem("ss_done")
        z_done = sem("z_done")
        z_act = sem("z_act")
        hs_done = sem("hs_done")
        hsw_done = sem("hsw_done")
        x1_done = sem("x1_done")
        xt2_ps = sem("xt2_ps")
        xt2_done = sem("xt2_done")
        logits_ps = sem("logits_ps")
        route = sem("route")
        route_act = sem("route_act")
        onehot_done = sem("onehot_done")
        cum_ps = sem("cum_ps")
        slot_done = sem("slot_done")
        cum_used = sem("cum_used")
        read_done = sem("read_done")
        scattered = [sem(f"scattered{i}") for i in range(2)]
        w_in = [sem(f"w_in{i}") for i in range(2)]
        xe_in = [sem(f"xe_in{i}") for i in range(2)]
        xet_ps = sem("xet_ps")
        xet_done = sem("xet_done")
        h_ps = sem("h_ps")
        h_done = sem("h_done")
        y_ps = sem("y_ps")
        y_done = sem("y_done")
        y_out = [sem(f"y_out{i}") for i in range(2)]
        kpr_in = [sem(f"kpr_in{i}") for i in range(2)]
        gix_done = sem("gix_done")
        yg_in = [sem(f"yg_in{i}") for i in range(2)]
        v_in = [sem(f"v_in{i}") for i in range(2)]
        x2_done = sem("x2_done")
        q3_ps = sem("q3_ps")
        q3_done = sem("q3_done")
        qp_ps = sem("qp_ps")
        qp_done = sem("qp_done")
        s3_ps = sem("s3_ps")
        sm_steps = sem("sm_steps")
        pr_done = sem("pr_done")
        prt_ps = sem("prt_ps")
        prt_done = sem("prt_done")
        o3_ps = sem("o3_ps")
        o3_steps = sem("o3_steps")
        x3_done = sem("x3_done")
        xb_done = sem("xb_done")
        xt4_ps = sem("xt4_ps")
        xt4_done = sem("xt4_done")
        f_out_ps = sem("f_out_ps")
        xo_done = sem("xo_done")
        stored = [sem(f"stored{i}") for i in range(2)]

        ln1, ln2, ln3, ln4 = (Norm(f"ln{i}", sb, sem, consts) for i in range(1, 5))

        x_rows = x.rearrange("b s d -> (b s) d").rearrange("(t p) d -> p t d", p=P)
        ctx_rows = ctx_1024.rearrange("b s d -> (b s) d").rearrange("(t p) d -> p t d", p=P)
        out_rows = out.rearrange("b s d -> (b s) d").rearrange("(t p) d -> p t d", p=P)
        slots_rows = slots_x.rearrange("(t p) d -> p t d", p=P)
        y_rows = slots_y.rearrange("(t p) d -> p t d", p=P)
        w1_rows = w1.rearrange("e m f -> m e f")
        w2_rows = w2.rearrange("e (c f) m -> f e c m", f=P)

        def tiles(g):
            return bass.ds(g * GT, GT)

        def xtile(g):
            return lambda t: xs[:, bass.ds(g * GW + t * P, P)]

        def xgroup(g):
            return xs[:, bass.ds(g * GW, GW)]

        def one_row(v):
            return v.rearrange("(a n) -> a n", a=1)

        CONSTS = 24
        block = ctx.enter_context(nc.Block())

        setup_loads = [
            (kq[:, 0:NH], igate_kernel[0:D, :]), (kq[:, NH:], fgate_kernel[0:D, :]),
            (kk[:, 0:NH], igate_kernel[D:2 * D, :]), (kk[:, NH:], fgate_kernel[D:2 * D, :]),
            (kv[:, 0:NH], igate_kernel[2 * D:, :]), (kv[:, NH:], fgate_kernel[2 * D:, :]),
            (gate_bias[:, 0:NH], one_row(igate_bias).to_broadcast([P, NH])),
            (gate_bias[:, NH:], one_row(fgate_bias).to_broadcast([P, NH])),
            (gx[:, :], one_row(g_xattn).to_broadcast([P, 2])),
            (gf[:, :], one_row(g_ffn).to_broadcast([P, 2])),
            (rmsb[:, :], one_row(rms_scale).to_broadcast([P, HD])),
            (wg_sb[:, :], wg), (pw1_sb[:, :], pw1), (pw2_sb[:, :], pw2), (cb_sb[:, :], CB),
            (rows[0:E * FC, :], b1.rearrange("e (c f) -> (e c) f", f=P)),
            (rows[32:33, :], one_row(pb1)), (rows[33:34, :], one_row(pb2)), (rows[34:35, :], one_row(SCB)),
            (cbias_b[:, :], one_row(cbias).to_broadcast([P, P])),
            (mask[0:S, :], fside[0]), (mask[S:P, :], fside[0]),
        ]
        PARAMS = 16 * len(setup_loads)
        FILL = 2 * GW
        B1, PB1, PB2, SCBC = 0, 32, 33, 34
        assert E * FC == 32

        @block.sync
        def _(sp):
            def load(g, half, q):
                if not isinstance(g, int) or g >= 2:
                    hold(sp, ct_done, g - 1, consts)
                    hold(sp, vaug_done, g - 1, consts)
                sp.dma_start(xgroup(g).rearrange("p (t d) -> p t d", t=GT), x_rows[:, tiles(g), :]).then_inc(x_in[q], 16)
                sp.dma_start(ctxb[:, q, :, :], ctx_rows[:, tiles(g), :]).then_inc(ctx_in[q], 16)

            def spread_max(g, half, q):
                hold(sp, mrow_done, g + 1, consts)
                sp.dma_start(m_dram[q].rearrange("b (r i) -> r b i", i=S),
                             mrow[:, q, :].rearrange("r (b i) -> r b i", b=2)).then_inc(m_out[q], 16)
                hold(sp, m_out[q], half * 16 + 16, consts)
                hold(sp, l_done, g - 1, consts)
                for b in range(2):
                    sp.dma_start(mb[b * S:(b + 1) * S, q, :],
                                 m_dram[q][b:b + 1, :].to_broadcast([S, R * S])).then_inc(m_in[q], 16)

            load(0, 0, 0)
            sp.wait_ge(consts, 2)
            for dst, src in setup_loads:
                sp.dma_start(dst, src).then_inc(par_in, 16)
            load(1, 0, 1)
            sp.wait_ge(consts, 1)
            for n in range(NT * D // FILL):
                per = FILL // D
                sp.dma_start(slots_rows[:, n * per:(n + 1) * per, :],
                             zeros.rearrange("p (t d) -> p t d", d=D)).then_inc(filled, 16)

            spread_max(0, 0, 0)
            load(2, 1, 0)
            spread_max(1, 0, 1)
            load(3, 1, 1)
            with sp.Fori(1, NG // 2 - 1) as half:
                spread_max(half * 2, half, 0)
                load(half * 2 + 2, half + 1, 0)
                spread_max(half * 2 + 1, half, 1)
                load(half * 2 + 3, half + 1, 1)
            spread_max(NG - 2, NG // 2 - 1, 0)
            spread_max(NG - 1, NG // 2 - 1, 1)

            for e in range(E):
                sp.dma_start(b2b[:, e, :], one_row(b2[e]).to_broadcast([P, D])).then_inc(par_in, 16)

            def load_w(e, half, q):
                hold(sp, y_ps, e * 2 - 2, consts)
                sp.dma_start(w1_sb[:, q, :], w1_rows[:, e, :]).then_inc(w_in[q], 16)
                sp.dma_start(w2_sb[:, q, :, :], w2_rows[:, e, :, :]).then_inc(w_in[q], 16)

            def load_xe(s, half, q):
                hold(sp, xet_ps, s - 1, consts)
                sp.dma_start(xe[:, q, :, :], slots_rows[:, tiles(s), :]).then_inc(xe_in[q], 16)

            def store_y(s, half, q):
                hold(sp, y_done, s + 1, consts)
                sp.dma_start(y_rows[:, tiles(s), :], ye[:, q, :, :]).then_inc(y_out[q], 16)

            load_w(0, 0, 0)
            load_w(1, 0, 1)
            for q in range(2):
                sp.wait_ge(scattered[q], 16 * GT * NG // 2)
            load_xe(0, 0, 0)
            load_xe(1, 0, 1)
            with sp.Fori(0, E // 2 - 1) as quad:
                for j in range(4):
                    s = quad * 4 + j
                    load_xe(s + 2, None, j % 2)
                    store_y(s, None, j % 2)
                    if j % 2:
                        load_w(quad * 2 + 2 + j // 2, None, j // 2)
            for s in range(NG - 4, NG):
                if s + 2 < NG:
                    load_xe(s + 2, None, s % 2)
                store_y(s, None, s % 2)
            for q in range(2):
                sp.wait_ge(y_out[q], 16 * NG // 2)

            def load_v(g, half, q):
                hold(sp, o3_ps, g - 1, consts)
                sp.dma_start(ctxv[:, q, :, 0:D], ctx_rows[:, tiles(g), :]).then_inc(v_in[q], 16)
                sp.dma_start(kpr[:, q, :], kpt[:, bass.ds(g * GW, GW)]).then_inc(kpr_in[q], 16)

            def store(g, half, q):
                hold(sp, xo_done, g + 1, consts)
                sp.dma_start(out_rows[:, tiles(g), :], xo[:, q, :, :]).then_inc(stored[q], 16)

            load_v(0, 0, 0)
            load_v(1, 0, 1)
            with sp.Fori(0, NG // 2 - 1) as half:
                for q in range(2):
                    load_v(half * 2 + q + 2, half + 1, q)
                    store(half * 2 + q, half, q)
            store(NG - 2, NG // 2 - 1, 0)
            store(NG - 1, NG // 2 - 1, 1)
            for q in range(2):
                sp.wait_ge(stored[q], 16 * NG // 2)

        @block.gpsimd
        def _(pool):
            done = 0

            def step(ins):
                nonlocal done
                done += 1
                ins.then_inc(consts, 1)
                pool.wait_ge(consts, done)

            step(pool.memset(zeros, 0.0))
            step(pool.memset(rows[:, :], 0.0))
            step(pool.memset(qbd, 0.0))
            step(pool.memset(ident[:, :], 0.0))
            step(pool.affine_select(out=ident[:, :], in_=ident[:, :], compare_op=ALU.not_equal, fill=1.0, base=0,
                                    pattern=[[-1, P]], channel_multiplier=1))
            step(pool.memset(tri[:, :], 1.0))
            step(pool.affine_select(out=tri[:, :], in_=tri[:, :], compare_op=ALU.is_ge, fill=0.0, base=0,
                                    pattern=[[1, P]], channel_multiplier=-1))
            step(pool.tensor_copy(tri_b[:, :], tri[:, :]))
            step(pool.memset(tri[0:S, S:P], 0.0))
            step(pool.memset(cap[:, :], 0.0))
            for b in range(2):
                half = cap[b * S:(b + 1) * S, :]
                step(pool.affine_select(out=half, in_=half, compare_op=ALU.is_ge, fill=MASKED, base=0,
                                        pattern=[[1, S]], channel_multiplier=-1))
            step(pool.memset(reset[:, :], 0.0))
            step(pool.memset(reset[:, :].rearrange("r (b i) -> r b i", b=2)[:, :, 0:1], -1e38))
            step(pool.memset(ones_b[:, :], 1.0))
            step(pool.memset(onehot[:, :, :], 0.0))
            step(pool.memset(vaug[:, :, :, :, HD:HA], 1.0))
            step(pool.memset(ctxv[:, :, :, D:D + 1], 1.0))
            step(pool.iota(prio_i[:, :], pattern=[[-1, E]], base=E, channel_multiplier=0))
            step(pool.iota(trash_i[:, :], pattern=[[P, NT]], base=N, channel_multiplier=1))
            step(pool.iota(carry_i[:, :], pattern=[[CAP, E]], base=-1, channel_multiplier=0))
            step(pool.tensor_copy(prio[:, :], prio_i[:, :]))
            step(pool.tensor_copy(trash[:, :], trash_i[:, :]))
            step(pool.tensor_copy(carry[:, 0, :], carry_i[:, :]))
            assert done == CONSTS

            def exponents(g, half, q):
                hold(pool, m_in[q], half * 32 + 32, consts)
                hold(pool, a_done, g + 1, consts)
                hold(pool, cw_done, nth(g - 1, 0, GT), consts)
                pool.tensor_tensor(ex[:, q, :].rearrange("p (r i) -> p r i", i=S),
                                   am[:, q, :].unsqueeze(2).to_broadcast([P, R, S]),
                                   mb[:, q, :].rearrange("p (r i) -> p r i", i=S),
                                   ALU.subtract).then_inc(l_done, 1)

            def add_heads(g, half, q):
                hold(pool, hs_done, g + 1, consts)
                pool.tensor_tensor(hs[:, q, :, :], hs[:, q, :, :],
                                   head_w[:, :].unsqueeze(1).to_broadcast([P, GT, D]), ALU.mult).then_inc(hsw_done, 1)
                hold(pool, hsw_done, g + 1, consts)
                pool.tensor_tensor(xgroup(g), xgroup(g), hs[:, q, :, :].rearrange("p t d -> p (t d)"),
                                   ALU.add).then_inc(x1_done, 1)

            def scatter(g, half, q):
                hold(pool, slot_done, g + 1, consts)
                if isinstance(g, int) and g == 0:
                    pool.wait_ge(filled, 16 * (NT * D // FILL))
                for t in range(GT):
                    pool.indirect_dma_start(out=slots_x, out_offset=bass.IndirectOffsetOnAxis(ap=sidx[:, q, t:t + 1], axis=0),
                                            in_=xn2[:, q, t, :], in_offset=None).then_inc(scattered[q], 16)

            def first_pass(at):
                _, two, three, _, five = at
                if five:
                    scatter(*five)
                if two:
                    exponents(*two)
                if three:
                    add_heads(*three)

            over_groups(pool, NG, 5, first_pass)

            for q in range(2):
                pool.wait_ge(y_out[q], 16 * NG // 2)

            def last_pass(at):
                one, two, three = at
                if one:
                    g, half, q = one
                    if isinstance(g, int) and g == 0:
                        pool.wait_ge(read_done, 2 * NG)
                    hold(pool, x2_done, g - 1, consts)
                    pool.tensor_copy(gix[:, q, :], gidx[:, tiles(g)]).then_inc(gix_done, 1)
                    hold(pool, gix_done, g + 1, consts)
                    for t in range(GT):
                        pool.indirect_dma_start(out=yg[:, q, t, :], out_offset=None, in_=slots_y,
                                                in_offset=bass.IndirectOffsetOnAxis(ap=gix[:, q, t:t + 1], axis=0)
                                                ).then_inc(yg_in[q], 16)
                if three:
                    g, half, q = three
                    hold(pool, x3_done, g + 1, consts)
                    hold(pool, xo_done, g, consts)
                    pool.tensor_tensor(xb[:, q, :, :], xgroup(g).rearrange("p (t d) -> p t d", t=GT),
                                       fbias[:, :].unsqueeze(1).to_broadcast([P, GT, D]), ALU.add).then_inc(xb_done, 1)

            over_groups(pool, NG, 3, last_pass)

        @block.scalar
        def _(act):
            act.wait_ge(par_in, PARAMS)
            act.activation(tx[:, :], gx[:, :], ACT.Tanh).then_inc(act_setup, 1)
            act.activation(tf[:, :], gf[:, :], ACT.Tanh).then_inc(act_setup, 1)

            def keys(g, half, q):
                act.wait_ge(ct_done, g + 1)
                act.activation(kt[:, q, :], bank[1][:, :], ACT.Copy).then_inc(kt_done, 1)

            def projected_keys(g, half, q):
                hold(act, kp_done, g + 1, consts)
                act.activation(kpt[:, bass.ds(g * GW, GW)], bank[1][:, :], ACT.Identity,
                               bias=pc[:, 0:1]).then_inc(kpt_done, 1)

            def values(g, half, q):
                act.wait_ge(ctx_in[q], half * 16 + 16)
                need(act, pv_done, nth(g - 2, GT, GT))
                act.activation(vaug[:, q, :, :, 0:HD], ctxb[:, q, :, :].rearrange("p t (h d) -> p t h d", h=NH),
                               ACT.Copy).then_inc(vaug_done, 1)

            def queries(g, half, q):
                act.wait_ge(xt1_done, g + 1)
                act.activation(qt[:, :], bank[0][:, :], ACT.Copy).then_inc(qt_done, 1)
                for h in range(NH):
                    hp = slice(h * HD, (h + 1) * HD)
                    act.activation(qbd[hp, q, :].rearrange("p (b h i) -> p b h i", b=BG, h=NH)[:, :, h, :],
                                   bank[0][hp, :].rearrange("p (b i) -> p b i", b=BG), ACT.Copy).then_inc(qbd_done, 1)

            def soft_part(g, half, q):
                act.wait_ge(gate_steps, nth(g, 2, 3))
                act.activation(eneg[:, :], negabs[:, :], ACT.Exp).then_inc(gate_act, 1)
                act.wait_ge(gate_act, nth(g, 1, 2))
                act.activation(softp[:, :], eneg[:, :], ACT.Ln, bias=1.0).then_inc(gate_act, 1)

            def exp_m(g, half, q):
                act.wait_ge(mtok_done, g + 1)
                need(act, n_done, nth(g - 2, 1, 4))
                act.activation(em[:, q, :], mtok[:, :], ACT.Exp, scale=-1.0).then_inc(em_done, 1)

            def decays(g, half, q):
                act.wait_ge(lcap_done, g + 1)
                act.activation(ex[:, q, :], ex[:, q, :], ACT.Exp).then_inc(ex_done, 1)

            def squares(g, half, q):
                act.wait_ge(n_done, nth(g, 1, 4))
                act.activation(sq[:, :, :, :],
                               heads[:, :, NH * S:NH * (S + HA)].rearrange("p t (h d) -> p t h d", d=HA)[:, :, :, 0:HD],
                               ACT.Square).then_inc(sq_done, 1)

            def rms_guess(g, half, q):
                act.wait_ge(z_done, nth(g, 1, 4))
                act.activation(zz[:, 1, :], zz[:, 0, :], ACT.Ln).then_inc(z_act, 1)
                act.wait_ge(z_act, nth(g, 1, 2))
                act.activation(zz[:, 2, :], zz[:, 1, :], ACT.Exp, scale=-0.5).then_inc(z_act, 1)

            def routed_rows(g, half, q):
                act.wait_ge(xt2_ps, g + 1)
                act.activation(xt2[:, :], bank[7][:, :], ACT.Copy).then_inc(xt2_done, 1)

            def route_exp(g, half, q):
                act.wait_ge(route, nth(g, 2, 6))
                act.activation(rt[:, 1, :, :], rt[:, 0, :, :], ACT.Exp).then_inc(route_act, 1)

            def first_pass(at):
                one, two, three, four = at
                if two:
                    soft_part(*two)
                if four:
                    ln2.act_guess(act, four[0])
                if two:
                    exp_m(*two)
                if one:
                    ln1.act_guess(act, one[0])
                if two:
                    values(*two)
                if four:
                    routed_rows(*four)
                if three:
                    squares(*three)
                    rms_guess(*three)
                if four:
                    route_exp(*four)
                if one:
                    keys(*one)
                    projected_keys(*one)
                    queries(*one)
                if two:
                    decays(*two)

            act.preload_act_table_set("natural_log_exp_and_others")
            over_groups(act, NG, 4, first_pass)

            def gelu(s, e):
                for c in range(FC):
                    hold(act, h_ps, nth(s, c + 1, FC), consts)
                    if c == 0:
                        hold(act, y_ps, s - 1, consts)
                    col = cols[:, bass.ds(e * FC + c, 1)]
                    act.activation(ht[:, s_par, c, :], heads[:, c, :], ACT.Gelu_apprx_tanh,
                                   bias=col).then_inc(h_done, 1)

            s_par = 0
            for s in range(2):
                s_par = s
                gelu(s, 0)
            with act.Fori(1, E) as e:
                for j in range(2):
                    s_par = j
                    gelu(e * 2 + j, e)

            def last_pass(at):
                one, two, three = at
                if one:
                    g, half, q = one
                    ln3.act_guess(act, g)
                if three:
                    ln4.act_guess(act, three[0])
                if two:
                    g, half, q = two
                    act.wait_ge(sm_steps, nth(g, 3, 3))
                    act.activation(pr[:, :, :], sm[:, 1, :, :], ACT.Exp).then_inc(pr_done, 1)
                if one:
                    g, half, q = one
                    act.wait_ge(q3_ps, g + 1)
                    act.activation(qt3[:, :], bank[0][:, :], ACT.Copy).then_inc(q3_done, 1)
                if two:
                    g, half, q = two
                    act.wait_ge(prt_ps, g + 1)
                    act.activation(prt[:, :, :].rearrange("p u n -> p (u n)"), heads[:, 1, 0:2 * P], ACT.Copy).then_inc(prt_done, 1)
                if one:
                    g, half, q = one
                    act.wait_ge(qp_ps, g + 1)
                    act.activation(qp[:, q, :], bank[1][:, :], ACT.Identity, bias=pc[:, 0:1]).then_inc(qp_done, 1)
                if three:
                    g, half, q = three
                    act.wait_ge(xt4_ps, g + 1)
                    act.activation(xt4[:, :], bank[6][:, :], ACT.Copy).then_inc(xt4_done, 1)

            act.preload_act_table_set("natural_log_exp_and_others")
            over_groups(act, NG, 3, last_pass)

        @block.tensor
        def _(pe):
            pe.wait_ge(consts, CONSTS)
            pe.wait_ge(par_in, PARAMS)
            pe.transpose(bank[0][:, 0:40], rows[0:40, :], ident[0:40, 0:40]).then_inc(pe_setup, 1)
            pe.transpose(bank[0][:, 128:256], pw2_sb[:, :], ident[:, :]).then_inc(pe_setup, 1)
            pe.wait_ge(dve_setup, 8)
            pe.matmul(bank[0][:, 256:384], pw1_sb[:, :], pw2t[:, :], start=True, stop=True).then_inc(pe_setup, 1)
            pe.matmul(bank[1][:, 0:1], pw2t[:, :], cols[:, PB1:PB1 + 1], start=True, stop=True).then_inc(pe_setup, 1)
            pe.transpose(bank[1][:, 128:256], cbs[:, :], ident[:, :]).then_inc(pe_setup, 1)
            pe.wait_ge(dve_setup, 11)

            def turn_context(g, half, q):
                pe.wait_ge(ctx_in[q], half * 16 + 16)
                need(pe, kpt_done, g)
                for t in range(GT):
                    last = pe.transpose(bank[1][:, t * P:(t + 1) * P], ctxb[:, q, t, :], ident[:, :])
                last.then_inc(ct_done, 1)

            def project_keys(g, half, q):
                pe.wait_ge(kt_done, g + 1)
                pe.matmul(bank[1][:, :], pa[:, :], kt[:, q, :], start=True, stop=True).then_inc(kp_done, 1)

            def turn_queries(g, half, q):
                pe.wait_ge(ln1.applied, g + 1)
                need(pe, qbd_done, NH * g)
                for t in range(GT):
                    last = pe.transpose(bank[0][:, t * P:(t + 1) * P], xn1[:, t, :], ident[:, :])
                last.then_inc(xt1_done, 1)

            def gate_products(g, half, q):
                pe.wait_ge(qt_done, g + 1)
                need(pe, mtok_done, g)
                for t in range(GT):
                    o = bank[6][:, t * 2 * NH:(t + 1) * 2 * NH]
                    pe.matmul(o, qt[:, t * P:(t + 1) * P], kq[:, :], start=True, stop=False)
                    last = pe.matmul(o, kt[:, q, t * P:(t + 1) * P], kc[:, :], start=False, stop=True)
                last.then_inc(gates_ps, 1)

            def forget_sums(g, half, q):
                pe.wait_ge(gate_steps, nth(g, 3, 3))
                pe.matmul(bank[6][:, 64:64 + R], tri[:, :], logf[:, :], start=True, stop=True).then_inc(f_ps, 1)

            def turn_a(g, half, q):
                pe.wait_ge(a_done, g + 1)
                pe.transpose(bank[6][0:R, 128:256], am[:, q, :], ident[:, :]).then_inc(at_ps, 1)

            def turn_maxima(g, half, q):
                hold(pe, mrow_done, g + 1, consts)
                pe.transpose(bank[6][:, 256:256 + R], mrow[:, q, :], ident[0:R, 0:R]).then_inc(mt_ps, 1)

            def scores(g, q, tiles_of):
                for t in tiles_of:
                    if t == 0:
                        pe.wait_ge(qbd_done, nth(g, NH, NH))
                        need(pe, hs_done, g)
                    for b in range(2 * t, 2 * t + 2):
                        last = pe.matmul(heads[(b % 2) * S:(b % 2 + 1) * S, t, 0:NH * S], kt[:, q, b * S:(b + 1) * S],
                                         qbd[:, q, b * NH * S:(b + 1) * NH * S], start=True, stop=True)
                    last.then_inc(scores_done, 1)

            def head_values(g, q, tiles_of):
                for t in tiles_of:
                    hold(pe, cw_done, nth(g, t + 1, GT), consts)
                    if t == 0:
                        pe.wait_ge(vaug_done, g + 1)
                    for h in range(NH):
                        for b in range(2):
                            bp = slice(b * S, (b + 1) * S)
                            last = pe.matmul(heads[bp, t, NH * S + h * HA:NH * S + (h + 1) * HA],
                                             cw[bp, t, h, :], vaug[bp, q, t, h, :], start=True, stop=True)
                    last.then_inc(pv_done, 1)

            def turn_routed(g, half, q):
                pe.wait_ge(ln2.applied, g + 1)
                need(pe, cum_used, g)
                for t in range(GT):
                    last = pe.transpose(bank[7][:, t * P:(t + 1) * P], xn2[:, q, t, :], ident[:, :])
                last.then_inc(xt2_ps, 1)

            def logits(g, half, q):
                pe.wait_ge(xt2_done, g + 1)
                for t in range(GT):
                    last = pe.matmul(bank[7][:, t * E:(t + 1) * E], xt2[:, t * P:(t + 1) * P], wg_sb[:, :], start=True, stop=True)
                last.then_inc(logits_ps, 1)

            def count_tokens(g, half, q):
                pe.wait_ge(onehot_done, g + 1)
                W = (GT + 1) * E
                cum = bank[7][:, 128:128 + W]
                pe.matmul(cum, tri_b[:, :], onehot[:, :, :].rearrange("p t e -> p (t e)"), start=True, stop=False)
                for t in range(GT):
                    last = pe.matmul(cum[:, (t + 1) * E:W], ones_b[:, :],
                                     onehot[:, t:t + 1, :].to_broadcast([P, GT - t, E]),
                                     start=False, stop=(t == GT - 1))
                last.then_inc(cum_ps, 1)

            def first_pass(at):
                one, two, three, four = at
                if three:
                    scores(three[0], three[2], (0, 1))
                if two:
                    forget_sums(*two)
                if three:
                    scores(three[0], three[2], (2, 3))
                if two:
                    turn_a(*two)
                if three:
                    head_values(three[0], three[2], (0,))
                if two:
                    turn_maxima(*two)
                if four:
                    turn_routed(*four)
                if three:
                    head_values(three[0], three[2], (1, 2, 3))
                if four:
                    logits(*four)
                if one:
                    turn_context(*one)
                    turn_queries(*one)
                    project_keys(*one)
                if four:
                    count_tokens(*four)
                if one:
                    gate_products(*one)

            over_groups(pe, NG, 4, first_pass)

            def turn_and_up(s, half, q, wq):
                pe.wait_ge(xe_in[q], half * 16 + 16)
                need(pe, xet_done, s)
                for t in range(GT):
                    last = pe.transpose(bank[0][:, t * P:(t + 1) * P], xe[:, q, t, :], ident[:, :])
                last.then_inc(xet_ps, 1)
                pe.wait_ge(xet_done, s + 1)
                for c in range(FC):
                    need(pe, h_done, nth(s - 1, c + 1, FC))
                    pe.matmul(heads[:, c, :], w1_sb[:, wq, c * P:(c + 1) * P], xet[:, :], start=True, stop=True).then_inc(h_ps, 1)

            def down(s, q, wq):
                pe.wait_ge(h_done, nth(s, FC, FC))
                need(pe, y_done, s)
                for t in range(GT):
                    for c in range(FC):
                        last = pe.matmul(bank[6][:, t * D:(t + 1) * D], ht[:, q, c, t * P:(t + 1) * P], w2_sb[:, wq, c, :],
                                         start=(c == 0), stop=(c == FC - 1))
                last.then_inc(y_ps, 1)

            def expert_quad(quad, first=False):
                for j in range(4):
                    s = quad * 4 + j
                    if j % 2 == 0:
                        pe.wait_ge(w_in[j // 2], quad * 32 + 32)
                    turn_and_up(s, quad * 2 + j // 2, j % 2, j // 2)
                    if not (first and j == 0):
                        down(s - 1, (j - 1) % 2, ((j - 1) % 4) // 2)

            need(pe, hs_done, NG)
            pe.wait_ge(x1_done, NG)
            expert_quad(0, first=True)
            with pe.Fori(1, E // 2) as quad:
                expert_quad(quad)
            down(NG - 1, 1, 1)

            def last_pass(at):
                one, two, three = at
                if two:
                    g, half, q = two
                    pe.wait_ge(qp_done, g + 1)
                    pe.wait_ge(kpr_in[q], half * 16 + 16)
                    need(pe, sm_steps, nth(g - 1, 1, 3))
                    for b in range(BG):
                        u, p, c = b // 4, b // 2 % 2, b % 2
                        last = pe.matmul(heads[p * S:(p + 1) * S, 0, (2 * u + c) * S:(2 * u + c + 1) * S],
                                         qp[:, q, b * S:(b + 1) * S], kpr[:, q, b * S:(b + 1) * S], start=True, stop=True)
                    last.then_inc(s3_ps, 1)
                if one:
                    g, half, q = one
                    pe.wait_ge(ln3.applied, g + 1)
                    need(pe, q3_done, g)
                    for t in range(GT):
                        last = pe.transpose(bank[0][:, t * P:(t + 1) * P], xn3[:, t, :], ident[:, :])
                    last.then_inc(q3_ps, 1)
                if three:
                    g, half, q = three
                    pe.wait_ge(ln4.applied, g + 1)
                    need(pe, xt4_done, g)
                    for t in range(GT):
                        last = pe.transpose(bank[6][:, t * P:(t + 1) * P], xn4[:, t, :], ident[:, :])
                    last.then_inc(xt4_ps, 1)
                if one:
                    g, half, q = one
                    pe.wait_ge(q3_done, g + 1)
                    need(pe, qp_done, g)
                    pe.matmul(bank[1][:, :], pa[:, :], qt3[:, :], start=True, stop=True).then_inc(qp_ps, 1)
                if two:
                    g, half, q = two
                    pe.wait_ge(pr_done, g + 1)
                    need(pe, prt_done, g)
                    for u in range(2):
                        last = pe.transpose(heads[:, 1, u * P:(u + 1) * P],
                                            pr[:, 2 * u:2 * u + 2, :].rearrange("p c k -> p (c k)"), ident[:, :])
                    last.then_inc(prt_ps, 1)
                    hold(pe, prt_done, g + 1, consts)
                    pe.wait_ge(v_in[q], half * 16 + 16)
                    need(pe, x3_done, g)
                    for b in range(BG):
                        u, p, c = b // 4, b // 2 % 2, b % 2
                        t = b // 2
                        cp = slice(c * S, (c + 1) * S)
                        last = pe.matmul(heads[cp, 2 + t // 2, (t % 2) * (D + 1):(t % 2 + 1) * (D + 1)],
                                         prt[cp, u, p * S:(p + 1) * S], ctxv[cp, q, t, :], start=True, stop=True)
                    last.then_inc(o3_ps, 1)
                if three:
                    g, half, q = three
                    pe.wait_ge(xt4_done, g + 1)
                    need(pe, xo_done, g)
                    for t in range(GT):
                        last = pe.matmul(bank[7][:, t * D:(t + 1) * D], xt4[:, t * P:(t + 1) * P], cbt[:, :], start=True, stop=True)
                    last.then_inc(f_out_ps, 1)

            over_groups(pe, NG, 3, last_pass)

        @block.vector
        def _(dve):
            dve.wait_ge(par_in, PARAMS)
            dve.tensor_tensor(kc[:, :], kk[:, :], kv[:, :], ALU.add).then_inc(dve_setup, 1)
            dve.wait_ge(act_setup, 2)
            dve.tensor_scalar(rmsw[:, :], rmsb[:, :], 1.0, tx[:, 0:1], ALU.add, ALU.mult).then_inc(dve_setup, 1)
            dve.wait_ge(dve_setup, 2)
            dve.tensor_copy(head_w[:, :].rearrange("p (h d) -> p h d", h=NH),
                            rmsw[:, :].unsqueeze(1).to_broadcast([P, NH, HD])).then_inc(dve_setup, 1)
            dve.tensor_scalar(fbias[:, :], cbias_b[:, :], tf[:, 1:2], None, ALU.mult).then_inc(dve_setup, 1)
            dve.wait_ge(pe_setup, 2)
            dve.tensor_copy(cols[:, :], bank[0][:, 0:40]).then_inc(dve_setup, 1)
            dve.tensor_copy(pw2t[:, :], bank[0][:, 128:256]).then_inc(dve_setup, 1)
            dve.wait_ge(dve_setup, 5)
            dve.tensor_scalar(scb_t[:, :], cols[:, SCBC:SCBC + 1], 1.0 / 127.0, tf[:, 1:2], ALU.mult, ALU.mult).then_inc(dve_setup, 1)
            dve.wait_ge(dve_setup, 7)
            dve.tensor_scalar(cbs[:, :], cb_sb[:, :], scb_t[:, 0:1], None, ALU.mult).then_inc(dve_setup, 1)
            dve.wait_ge(pe_setup, 5)
            dve.tensor_copy(pa[:, :], bank[0][:, 256:384]).then_inc(dve_setup, 1)
            dve.tensor_tensor(pc[:, :], bank[1][:, 0:1], cols[:, PB2:PB2 + 1], ALU.add).then_inc(dve_setup, 1)
            dve.tensor_copy(cbt[:, :], bank[1][:, 128:256]).then_inc(dve_setup, 1)

            def stats1(g, half, q):
                hold(dve, x_in[q], half * 16 + 16, consts)
                ln1.dve_stats(dve, g, xtile(g))

            def norm1(g, half, q):
                ln1.dve_newton(dve, g)
                need(dve, xt1_done, g)
                ln1.dve_apply(dve, g, lambda t: xn1[:, t, :], xtile(g))

            def gate_values(g, half, q):
                dve.wait_ge(gates_ps, g + 1)
                dve.tensor_tensor(gates[:, :, :].rearrange("p k (t h) -> p k t h", t=GT),
                                  bank[6][:, 0:2 * R].rearrange("p (t k h) -> p k t h", t=GT, k=2),
                                  gate_bias[:, :].rearrange("p (k h) -> p k h", k=2).unsqueeze(2).to_broadcast([P, 2, GT, NH]),
                                  ALU.add).then_inc(gate_steps, 1)
                dve.wait_ge(gate_steps, nth(g, 1, 3))
                dve.scalar_tensor_tensor(out=negabs[:, :], in0=gates[:, 1, :], scalar=-1.0, in1=gates[:, 1, :],
                                         op0=ALU.mult, op1=ALU.min).then_inc(gate_steps, 1)

            def log_forget(g, half, q):
                dve.wait_ge(gate_act, nth(g, 2, 2))
                dve.scalar_tensor_tensor(out=logf[:, :], in0=gates[:, 1, :], scalar=0.0, in1=softp[:, :],
                                         op0=ALU.min, op1=ALU.subtract).then_inc(gate_steps, 1)

            def a_values(g, half, q):
                dve.wait_ge(f_ps, g + 1)
                dve.tensor_copy(fcum[:, :], bank[6][:, 64:64 + R]).then_inc(gate_copy, 1)
                dve.wait_ge(gate_copy, g + 1)
                need(dve, l_done, g - 1)
                dve.tensor_tensor(am[:, q, :], gates[:, 0, :], fcum[:, :], ALU.subtract).then_inc(a_done, 1)

            def running_max(g, half, q):
                dve.wait_ge(at_ps, g + 1)
                if not isinstance(g, int) or g >= 2:
                    dve.wait_ge(m_out[q], half * 16)
                dve.tensor_tensor_scan(mrow[:, q, :], reset[:, :], bank[6][0:R, 128:256], 0.0, ALU.add, ALU.max).then_inc(mrow_done, 1)

            def max_by_token(g, half, q):
                dve.wait_ge(mt_ps, g + 1)
                dve.tensor_tensor(mtok[:, :], bank[6][:, 256:256 + R], fcum[:, :], ALU.add).then_inc(mtok_done, 1)

            def cap_exponents(g, half, q):
                dve.wait_ge(l_done, g + 1)
                e3 = ex[:, q, :].rearrange("p (r i) -> p r i", i=S)
                dve.tensor_tensor(e3, e3, cap[:, :].unsqueeze(1).to_broadcast([P, R, S]), ALU.min).then_inc(lcap_done, 1)

            def decayed_scores(g, q, tiles_of):
                for t in tiles_of:
                    if t == 0:
                        dve.wait_ge(ex_done, g + 1)
                    dve.wait_ge(scores_done, nth(g, t + 1, GT))
                    need(dve, pv_done, nth(g - 1, t + 1, GT))
                    dve.scalar_tensor_tensor(out=cw[:, t, :, :].rearrange("p h i -> p (h i)"), in0=heads[:, t, 0:NH * S],
                                             scalar=float(HD) ** -0.5, in1=ex[:, q, t * NH * S:(t + 1) * NH * S],
                                             op0=ALU.mult, op1=ALU.mult).then_inc(cw_done, 1)

            def normalisers(g, half, q):
                dve.wait_ge(pv_done, nth(g, GT, GT))
                dve.wait_ge(em_done, g + 1)
                o4 = heads[:, :, NH * S:NH * (S + HA)].rearrange("p t (h d) -> p t h d", d=HA)
                dve.tensor_tensor(nn[:, 0, :].rearrange("p (t h) -> p t h", t=GT), o4[:, :, :, HD],
                                  em[:, q, :].rearrange("p (t h) -> p t h", t=GT), ALU.max).then_inc(n_done, 1)
                dve.wait_ge(n_done, nth(g, 1, 4))
                dve.tensor_scalar(nn[:, 1, :], nn[:, 0, :], 1e-6, None, ALU.add).then_inc(n_done, 1)
                dve.wait_ge(n_done, nth(g, 2, 4))
                dve.scalar_tensor_tensor(out=nn[:, 2, :], in0=nn[:, 1, :], scalar=1e-6, in1=nn[:, 1, :],
                                         op0=ALU.mult, op1=ALU.mult).then_inc(n_done, 1)

            def mean_squares(g, half, q):
                dve.wait_ge(sq_done, g + 1)
                dve.tensor_reduce(ss[:, :].rearrange("p (t h) -> p t h", t=GT), sq[:, :, :, :], AX, ALU.add).then_inc(n_done, 1)
                dve.wait_ge(n_done, nth(g, 4, 4))
                dve.scalar_tensor_tensor(out=zz[:, 0, :], in0=ss[:, :], scalar=1.0 / HD, in1=nn[:, 2, :],
                                         op0=ALU.mult, op1=ALU.add).then_inc(z_done, 1)

            def scaled_heads(g, half, q):
                dve.wait_ge(z_act, nth(g, 2, 2))
                dve.tensor_tensor(zz[:, 3, :], zz[:, 2, :], zz[:, 2, :], ALU.mult).then_inc(z_done, 1)
                dve.wait_ge(z_done, nth(g, 2, 4))
                dve.scalar_tensor_tensor(out=zz[:, 4, :], in0=zz[:, 3, :], scalar=-0.5, in1=zz[:, 0, :],
                                         op0=ALU.mult, op1=ALU.mult).then_inc(z_done, 1)
                dve.wait_ge(z_done, nth(g, 3, 4))
                dve.scalar_tensor_tensor(out=zz[:, 5, :], in0=zz[:, 4, :], scalar=1.5, in1=zz[:, 2, :],
                                         op0=ALU.add, op1=ALU.mult).then_inc(z_done, 1)
                dve.wait_ge(z_done, nth(g, 4, 4))
                need(dve, x1_done, g - 1)
                for t in range(GT):
                    last = dve.tensor_tensor(hs[:, q, t, :].rearrange("p (h d) -> p h d", h=NH),
                                             heads[:, t, NH * S:NH * (S + HA)].rearrange("p (h d) -> p h d", d=HA)[:, :, 0:HD],
                                             zz[:, 5, t * NH:(t + 1) * NH].unsqueeze(2).to_broadcast([P, NH, HD]), ALU.mult)
                last.then_inc(hs_done, 1)

            def stats2(g, half, q):
                hold(dve, x1_done, g + 1, consts)
                ln2.dve_stats(dve, g, xtile(g))

            def norm2(g, half, q):
                ln2.dve_newton(dve, g)
                if not isinstance(g, int) or g >= 2:
                    dve.wait_ge(scattered[q], half * (16 * GT))
                ln2.dve_apply(dve, g, lambda t: xn2[:, q, t, :], xtile(g))

            def choose(g, half, q):
                lg = bank[7][:, 0:GT * E].rearrange("p (t e) -> p t e", t=GT)
                dve.wait_ge(logits_ps, g + 1)
                dve.tensor_reduce(rs[:, 8, :], lg, AX, ALU.max).then_inc(route, 1)
                dve.wait_ge(route, nth(g, 1, 6))
                dve.tensor_tensor(rt[:, 0, :, :], lg, rs[:, 8, :].unsqueeze(2).to_broadcast([P, GT, E]), ALU.subtract).then_inc(route, 1)
                dve.wait_ge(route, nth(g, 2, 6))
                dve.scalar_tensor_tensor(out=rt[:, 2, :, :], in0=rt[:, 0, :, :], scalar=0.0,
                                         in1=prio[:, :].unsqueeze(1).to_broadcast([P, GT, E]),
                                         op0=ALU.is_ge, op1=ALU.mult).then_inc(route, 1)
                dve.wait_ge(route, nth(g, 3, 6))
                dve.tensor_reduce(rs[:, 1, :], rt[:, 2, :, :], AX, ALU.max).then_inc(route, 1)
                dve.wait_ge(route, nth(g, 4, 6))
                dve.tensor_tensor(onehot[:, 0:GT, :], rt[:, 2, :, :],
                                  rs[:, 1, :].unsqueeze(2).to_broadcast([P, GT, E]), ALU.is_equal).then_inc(onehot_done, 1)
                dve.tensor_scalar(rs[:, 3, :], rs[:, 1, :], -float(CAP), float((E + 1) * CAP), ALU.mult, ALU.add).then_inc(limit_done, 1)

            def place(g, half, q):
                dve.wait_ge(route_act, g + 1)
                dve.tensor_reduce(rs[:, 9, :], rt[:, 1, :, :], AX, ALU.add).then_inc(route, 1)
                dve.wait_ge(cum_ps, g + 1)
                cum = bank[7][:, 128:128 + (GT + 1) * E].rearrange("p (t e) -> p t e", e=E)
                dve.tensor_tensor(rt[:, 3, :, :], cum[:, 0:GT, :], carry[:, q:q + 1, :].to_broadcast([P, GT, E]), ALU.add).then_inc(slot_steps, 1)
                dve.tensor_tensor(carry[:, 1 - q, :], cum[:, GT, :], carry[:, q, :], ALU.add).then_inc(cum_used, 1)
                dve.wait_ge(slot_steps, nth(g, 1, 6))
                dve.tensor_tensor(rt[:, 4, :, :], rt[:, 3, :, :], onehot[:, 0:GT, :], ALU.mult).then_inc(slot_steps, 1)
                dve.wait_ge(route, nth(g, 5, 6))
                dve.reciprocal(rs[:, 2, :], rs[:, 9, :]).then_inc(route, 1)
                dve.wait_ge(slot_steps, nth(g, 2, 6))
                slot, limit, beyond = rs[:, 0, :], rs[:, 3, :], rs[:, 7, :]
                dve.tensor_reduce(slot, rt[:, 4, :, :], AX, ALU.add).then_inc(slot_steps, 1)
                dve.wait_ge(slot_steps, nth(g, 3, 6))
                dve.wait_ge(limit_done, g + 1)
                dve.tensor_tensor(beyond, slot, limit, ALU.subtract).then_inc(slot_steps, 1)
                dve.tensor_tensor(rs[:, 5, :], slot, trash[:, tiles(g)], ALU.subtract).then_inc(slot_steps, 1)
                dve.wait_ge(slot_steps, nth(g, 5, 6))
                dve.scalar_tensor_tensor(out=rs[:, 6, :], in0=beyond, scalar=0.0, in1=rs[:, 5, :],
                                         op0=ALU.is_lt, op1=ALU.mult).then_inc(slot_steps, 1)
                dve.scalar_tensor_tensor(out=gidx[:, tiles(g)], in0=beyond, scalar=-1.0, in1=limit,
                                         op0=ALU.min, op1=ALU.add).then_inc(read_done, 1)
                dve.wait_ge(route, nth(g, 6, 6))
                dve.scalar_tensor_tensor(out=gw[:, tiles(g)], in0=beyond, scalar=0.0, in1=rs[:, 2, :],
                                         op0=ALU.is_lt, op1=ALU.mult).then_inc(read_done, 1)
                dve.wait_ge(slot_steps, nth(g, 6, 6))
                dve.tensor_tensor(sidx[:, q, :], rs[:, 6, :], trash[:, tiles(g)], ALU.add).then_inc(slot_done, 1)

            def first_pass(at):
                one, two, three, four = at
                if two:
                    log_forget(*two)
                if four:
                    stats2(*four)
                if three:
                    decayed_scores(three[0], three[2], (0, 1))
                if two:
                    a_values(*two)
                if three:
                    decayed_scores(three[0], three[2], (2, 3))
                if four:
                    norm2(*four)
                if two:
                    running_max(*two)
                if one:
                    stats1(*one)
                if two:
                    max_by_token(*two)
                if one:
                    norm1(*one)
                if three:
                    normalisers(*three)
                    mean_squares(*three)
                if four:
                    choose(*four)
                if three:
                    scaled_heads(*three)
                if two:
                    cap_exponents(*two)
                if four:
                    place(*four)
                if one:
                    gate_values(*one)

            gate_copy = sem("gate_copy")
            slot_steps = sem("slot_steps")
            limit_done = sem("limit_done")
            dve.wait_ge(consts, CONSTS)
            over_groups(dve, NG, 4, first_pass)

            dve.wait_ge(par_in, PARAMS + 16 * E)

            def evac_x(s):
                dve.wait_ge(xet_ps, s + 1)
                need(dve, h_ps, nth(s - 1, FC, FC))
                dve.tensor_copy(xet[:, :], bank[0][:, :]).then_inc(xet_done, 1)

            def evac_y(s, q, e):
                dve.wait_ge(y_ps, s + 1)
                if not isinstance(s, int) or s >= 2:
                    dve.wait_ge(y_out[q], e * 16)
                dve.tensor_tensor(ye[:, q, :, :], bank[6][:, :].rearrange("p (t d) -> p t d", t=GT),
                                  b2b[:, bass.ds(e, 1), :].to_broadcast([P, GT, D]), ALU.add).then_inc(y_done, 1)

            evac_x(0)
            evac_x(1)
            evac_y(0, 0, 0)
            evac_x(2)
            evac_y(1, 1, 0)
            evac_x(3)
            evac_y(2, 0, 1)
            with dve.Fori(2, E) as e:
                evac_x(e * 2)
                evac_y(e * 2 - 1, 1, e - 1)
                evac_x(e * 2 + 1)
                evac_y(e * 2, 0, e)
            evac_y(NG - 1, 1, E - 1)

            def last_pass(at):
                one, two, three = at
                if one:
                    g, half, q = one
                    dve.tensor_scalar(rsum[:, 0, :], gw[:, tiles(g)], tf[:, 0:1], None, ALU.mult).then_inc(gwt_done, 1)
                    dve.wait_ge(gwt_done, g + 1)
                    dve.wait_ge(yg_in[q], half * (16 * GT) + 16 * GT)
                    for t in range(GT):
                        last = dve.scalar_tensor_tensor(out=xtile(g)(t), in0=yg[:, q, t, :], scalar=rsum[:, 0, t:t + 1],
                                                        in1=xtile(g)(t), op0=ALU.mult, op1=ALU.add)
                    last.then_inc(x2_done, 1)
                    hold(dve, x2_done, g + 1, consts)
                    ln3.dve_stats(dve, g, xtile(g))
                if two:
                    g, half, q = two
                    dve.wait_ge(s3_ps, g + 1)
                    dve.scalar_tensor_tensor(out=sm[:, 0, :, :], in0=heads[:, 0, 0:GT * S].rearrange("p (c k) -> p c k", k=S),
                                             scalar=float(D) ** -0.5, in1=mask[:, :].unsqueeze(1).to_broadcast([P, GT, S]),
                                             op0=ALU.mult, op1=ALU.add).then_inc(sm_steps, 1)
                    dve.wait_ge(sm_steps, nth(g, 1, 3))
                    dve.tensor_reduce(smx[:, :], sm[:, 0, :, :], AX, ALU.max).then_inc(sm_steps, 1)
                    dve.wait_ge(sm_steps, nth(g, 2, 3))
                    need(dve, pr_done, g)
                    dve.tensor_tensor(sm[:, 1, :, :], sm[:, 0, :, :], smx[:, :].unsqueeze(2).to_broadcast([P, GT, S]),
                                      ALU.subtract).then_inc(sm_steps, 1)
                if three:
                    g, half, q = three
                    hold(dve, x3_done, g + 1, consts)
                    ln4.dve_stats(dve, g, xtile(g))
                if one:
                    g, half, q = one
                    ln3.dve_newton(dve, g)
                    need(dve, q3_ps, g)
                    ln3.dve_apply(dve, g, lambda t: xn3[:, t, :], xtile(g))
                if three:
                    g, half, q = three
                    ln4.dve_newton(dve, g)
                    need(dve, xt4_ps, g)
                    ln4.dve_apply(dve, g, lambda t: xn4[:, t, :], xtile(g))
                if two:
                    g, half, q = two
                    dve.wait_ge(o3_ps, g + 1)
                    o = heads[:, 2:4, 0:2 * (D + 1)].rearrange("p b (t d) -> p b t d", d=D + 1)
                    dve.reciprocal(rsum[:, 1, :].rearrange("p (b t) -> p b t", b=2), o[:, :, :, D]).then_inc(o3_steps, 1)
                    dve.wait_ge(o3_steps, nth(g, 1, 2))
                    dve.tensor_scalar(smx3[:, :], rsum[:, 1, :], tx[:, 1:2], None, ALU.mult).then_inc(o3_steps, 1)
                    dve.wait_ge(o3_steps, nth(g, 2, 2))
                    for t in range(GT):
                        last = dve.scalar_tensor_tensor(out=xtile(g)(t), in0=o[:, t // 2, t % 2, 0:D], scalar=smx3[:, t:t + 1],
                                                        in1=xtile(g)(t), op0=ALU.mult, op1=ALU.add)
                    last.then_inc(x3_done, 1)
                if three:
                    g, half, q = three
                    dve.wait_ge(f_out_ps, g + 1)
                    dve.wait_ge(xb_done, g + 1)
                    if not isinstance(g, int) or g >= 2:
                        dve.wait_ge(stored[q], half * 16)
                    dve.tensor_tensor(xo[:, q, :, :], bank[7][:, :].rearrange("p (t d) -> p t d", t=GT), xb[:, q, :, :],
                                      ALU.add).then_inc(xo_done, 1)

            gwt_done = sem("gwt_done")
            smx3 = sb("smx3", [P, GT])
            over_groups(dve, NG, 3, last_pass)


_INS = ['x', 'ctx_1024', 'fside_1xSxS2_0', 'g_xattn', 'g_ffn', 'L0_xattn_igate_kernel', 'L0_xattn_igate_bias',
        'L0_xattn_fgate_kernel', 'L0_xattn_fgate_bias', 'L0_xattn_rms_scale', 'L0_ffn_wg', 'L0_ffn_w1', 'L0_ffn_b1',
        'L0_ffn_w2', 'L0_ffn_b2', 'L1_xattn_W1', 'L1_xattn_b1', 'L1_xattn_W2', 'L1_xattn_b2', 'L1_ffn_CB',
        'L1_ffn_SCB', 'L1_ffn_bias']
_OUTS = [((128, 64, 128), 'float32')]


def kernel(**inputs):
    import numpy as _np
    import concourse.bacc as _bacc
    from concourse import mybir as _mybir
    from concourse.bass_utils import run_bass_kernel_spmd as _run

    nc = _bacc.Bacc("TRN2", target_bir_lowering=False, num_devices=1)
    arrays, args = {}, []
    for name in _INS:
        a = _np.ascontiguousarray(inputs[name])
        arrays[f"in_{name}_dram"] = a
        args.append(nc.dram_tensor(f"in_{name}_dram", a.shape, _mybir.dt.from_np(a.dtype), kind="ExternalInput").ap())
    for i, (shape, dtype) in enumerate(_OUTS):
        dt = _mybir.dt.from_np(_np.dtype(dtype))
        args.append(nc.dram_tensor(f"out_{i}_dram", shape, dt, kind="ExternalOutput").ap())
    flamingo(nc, *args)
    r = _run(nc, [arrays], core_ids=[0])
    return r.results[0]["out_0_dram"]
```

```python
from contextlib import ExitStack

import concourse.bass as bass
from concourse import mybir

F32 = mybir.dt.float32
BF16 = mybir.dt.bfloat16
I32 = mybir.dt.int32
ALU = mybir.AluOpType
ACT = mybir.ActivationFunctionType
AX = mybir.AxisListType.X

P = 128
GT = 4
GW = GT * P
LN_EPS = 1e-5
MASKED = -1e30


def nth(g, k, n):
    return g * n + k


def need(eng, sem, value):
    if isinstance(value, int) and value <= 0:
        return
    eng.wait_ge(sem, value)


def hold(eng, sem, value, go):
    if not isinstance(value, int):
        value = eng.to_reg(value)
        eng.wait_ge(go, 1)
    need(eng, sem, value)


def over_groups(eng, groups, stages, body):
    def step(half, parity, static):
        at = []
        for s in range(stages):
            back = s - parity
            h, q = (half, parity - s) if back <= 0 else (half - (back + 1) // 2, (parity - s) % 2)
            g = h * 2 + q
            at.append(None if static and not 0 <= g < groups else (g, h, q))
        body(at)

    first = (stages + 1) // 2
    for k in range(2 * first):
        step(k // 2, k % 2, True)
    with eng.Fori(first, groups // 2) as half:
        step(half, 0, False)
        step(half, 1, False)
    for k in range(groups, groups + stages - 1):
        step(k // 2, k % 2, True)


class Norms:

    def __init__(self, name, sb, sem, go):
        self.go = go
        self.stats = sb(f"{name}_stats", [P, 2 * GT, 6])
        self.mv = sb(f"{name}_mv", [P, 2 * GT, 2])
        self.ve = sb(f"{name}_ve", [P, 2 * GT])
        self.log = sb(f"{name}_log", [P, 2 * GT])
        self.y0 = sb(f"{name}_y0", [P, 2 * GT])
        self.t = sb(f"{name}_t", [P, 2, 2 * GT])
        self.rstd = sb(f"{name}_rstd", [P, 2 * GT])
        self.stats_done = [sem(f"{name}_stats_done{i}") for i in range(2)]
        self.mv_done = sem(f"{name}_mv_done")
        self.ve_done = sem(f"{name}_ve_done")
        self.log_done = sem(f"{name}_log_done")
        self.y0_done = sem(f"{name}_y0_done")
        self.newton = sem(f"{name}_newton")
        self.shift = sb(f"{name}_shift", [P, 2 * GT])
        self.shift_done = sem(f"{name}_shift_done")
        self.applied = [sem(f"{name}_applied{i}") for i in range(2)]

    @staticmethod
    def span(parts):
        return slice(parts[0][0] * GT, (parts[-1][0] + 1) * GT)

    def dve_stats(self, dve, i, tile):
        for t in range(GT):
            last = dve.bn_stats(self.stats[:, i * GT + t, :], tile(t))
        last.then_inc(self.stats_done[i], 1)

    def dve_moments(self, dve, k, parts):
        for i, g in parts:
            hold(dve, self.stats_done[i], g + 1, self.go)
        for i, _ in parts:
            for t in range(GT):
                last = dve.bn_aggr(self.mv[:, i * GT + t, :], self.stats[:, i * GT + t, :])
        last.then_inc(self.mv_done, 1)
        c = self.span(parts)
        dve.wait_ge(self.mv_done, k + 1)
        dve.tensor_scalar(self.ve[:, c], self.mv[:, c, 1], LN_EPS, None, ALU.add).then_inc(self.ve_done, 1)

    def act_guess(self, act, k, parts):
        c = self.span(parts)
        act.wait_ge(self.ve_done, k + 1)
        act.activation(self.log[:, c], self.ve[:, c], ACT.Ln).then_inc(self.log_done, 1)
        act.wait_ge(self.log_done, k + 1)
        act.activation(self.y0[:, c], self.log[:, c], ACT.Exp, scale=-0.5).then_inc(self.y0_done, 1)

    def dve_newton(self, dve, k, parts):
        c = self.span(parts)
        dve.wait_ge(self.y0_done, k + 1)
        dve.tensor_tensor(self.t[:, 0, c], self.y0[:, c], self.y0[:, c], ALU.mult).then_inc(self.newton, 1)
        dve.wait_ge(self.newton, nth(k, 1, 3))
        dve.scalar_tensor_tensor(out=self.t[:, 1, c], in0=self.t[:, 0, c], scalar=-0.5, in1=self.ve[:, c],
                                 op0=ALU.mult, op1=ALU.mult).then_inc(self.newton, 1)
        dve.wait_ge(self.newton, nth(k, 2, 3))
        dve.scalar_tensor_tensor(out=self.rstd[:, c], in0=self.t[:, 1, c], scalar=1.5, in1=self.y0[:, c],
                                 op0=ALU.add, op1=ALU.mult).then_inc(self.newton, 1)

    def dve_shift(self, dve, k, parts):
        for i, g in parts:
            need(dve, self.applied[i], g)
        c = self.span(parts)
        dve.wait_ge(self.newton, nth(k, 3, 3))
        dve.scalar_tensor_tensor(out=self.shift[:, c], in0=self.mv[:, c, 0], scalar=-1.0, in1=self.rstd[:, c],
                                 op0=ALU.mult, op1=ALU.mult).then_inc(self.shift_done, 1)

    def act_apply(self, act, k, i, out, tile):
        act.wait_ge(self.shift_done, k + 1)
        for t in range(GT):
            j = i * GT + t
            last = act.activation(out(t), tile(t), ACT.Identity, bias=self.shift[:, j:j + 1], scale=self.rstd[:, j:j + 1])
        last.then_inc(self.applied[i], 1)

    def dve_apply(self, dve, k, i, out, tile):
        dve.wait_ge(self.newton, nth(k, 3, 3))
        for t in range(GT):
            j = i * GT + t
            last = dve.tensor_scalar(out(t), tile(t), self.mv[:, j, 0:1], self.rstd[:, j:j + 1],
                                     ALU.subtract, ALU.mult)
        last.then_inc(self.applied[i], 1)


def step_of(at):
    s = next(s for s, here in enumerate(at) if here)
    return at[s][0] + s


def flamingo(nc, x, ctx_1024, fside, g_xattn, g_ffn, igate_kernel, igate_bias, fgate_kernel, fgate_bias,
             rms_scale, wg, w1, b1, w2, b2, pw1, pb1, pw2, pb2, CB, SCB, cbias, out):
    NB, S, D = x.shape
    N = NB * S
    NH = igate_kernel.shape[1]
    HD = D // NH
    E = wg.shape[1]
    F = w1.shape[2]
    FC = F // P
    CAP = max((N + E - 1) // E, 4)
    NT = N // P
    NG = N // GW
    BG = GW // S
    R = GT * NH
    HA = HD + 1
    assert D == P and S == P // 2 and CAP == 2 * GW and E * CAP == N and R == 16 and NG == 2 * E

    ctx = ExitStack()
    with ctx:
        def sb(name, shape, dt=F32):
            return ctx.enter_context(nc.sbuf_tensor("s_" + name, shape, dt))

        def sem(name):
            return ctx.enter_context(nc.semaphore(name))

        m_dram = [nc.dram_tensor(f"m_scratch{i}", (2, R * S), F32, kind="Internal").ap() for i in range(2)]
        slots_x = nc.dram_tensor("slots_x", (2 * N, D), F32, kind="Internal").ap()
        slots_y = nc.dram_tensor("slots_y", (N, D), F32, kind="Internal").ap()

        ident = sb("ident", [P, P])
        tri = sb("tri", [P, P])
        tri_b = sb("tri_b", [P, P], BF16)
        ones_b = sb("ones_b", [P, P], BF16)
        cap = sb("cap", [P, S])
        prio = sb("prio", [P, E])
        prio_i = sb("prio_i", [P, E], I32)
        trash_i = sb("trash_i", [P, NT], I32)
        trash = sb("trash", [P, NT])
        carry = sb("carry", [P, 2, E])
        carry_i = sb("carry_i", [P, E], I32)
        reset = sb("reset", [R, P])
        kqkv = sb("kqkv", [P, 3, 2 * NH])
        kc = sb("kc", [P, 2 * NH])
        gate_bias = sb("gate_bias", [P, 2 * NH])
        gx = sb("gx", [P, 2])
        gf = sb("gf", [P, 2])
        tx = sb("tx", [P, 2])
        tf = sb("tf", [P, 2])
        rmsb = sb("rmsb", [P, HD])
        rmsw = sb("rmsw", [P, HD])
        head_w = sb("head_w", [P, D])
        wg_sb = sb("wg_sb", [P, E])
        pw1_sb = sb("pw1_sb", [P, P])
        pw2_sb = sb("pw2_sb", [P, P])
        pw2t = sb("pw2t", [P, P])
        cb_sb = sb("cb_sb", [P, P])
        cbs = sb("cbs", [P, P])
        cbt = sb("cbt", [P, P])
        rows = sb("rows", [P, P])
        cols = sb("cols", [P, 40])
        pa = sb("pa", [P, P])
        pc = sb("pc", [P, 1])
        scb_t = sb("scb_t", [P, 1])
        cbias_b = sb("cbias_b", [P, P])
        fbias = sb("fbias", [P, P])
        mask = sb("mask", [P, S])
        b2b = sb("b2b", [P, E, D])

        xs = sb("xs", [P, NT * D])
        kpt = sb("kpt", [P, N])
        gw = sb("gw", [P, NT])
        gwt = sb("gwt", [P, NT])
        gidx = sb("gidx", [P, NT], I32)

        ctxb = sb("ctxb", [P, 2, GT, D])
        vaug = sb("vaug", [P, 2, GT, NH, HA])
        xn1 = sb("xn1", [P, GT, D])
        qt = sb("qt", [P, GW])
        kt = sb("kt", [P, 2, GW])
        gate_rows = sb("gate_rows", [2 * NH, GW])
        gates = sb("gates", [P, 2, R])
        negabs = sb("negabs", [P, R])
        eneg = sb("eneg", [P, R])
        softp = sb("softp", [P, R])
        logf = sb("logf", [P, R])
        fcum = sb("fcum", [P, R])
        am = sb("am", [P, 2, R])
        mrow = sb("mrow", [R, 2, P])
        mtok = sb("mtok", [P, R])
        em = sb("em", [P, 2, R])
        mb = sb("mb", [P, 2, R * S])
        ex = sb("ex", [P, 2, R * S])
        cw = sb("cw", [P, GT, NH, S])
        sq = sb("sq", [P, GT, NH, HD])
        nn = sb("nn", [P, 3, R])
        ss = sb("ss", [P, R])
        zz = sb("zz", [P, 6, R])
        hs = sb("hs", [P, 2, GT, D])
        xn2 = sb("xn2", [P, 2, GT, D])
        xt2 = sb("xt2", [P, GW])
        logit_rows = sb("logit_rows", [E, GW])
        rt = sb("rt", [P, 6, GT, E])
        onehot = sb("onehot", [P, GT + 1, E], BF16)
        rs = sb("rs", [P, 13, GT])
        sidx = sb("sidx", [P, 2, GT], I32)

        w1_sb = sb("w1_sb", [P, 2, F])
        w2_sb = sb("w2_sb", [P, 2, FC, D])
        xe = sb("xe", [P, 2, GT, D])
        xet = sb("xet", [P, GW])
        ht = sb("ht", [P, 2, FC, GW])
        ye = sb("ye", [P, 2, GT, D])

        yg = sb("yg", [P, 2, GT, D])
        kpr = sb("kpr", [P, 2, GW])
        gix = sb("gix", [P, 2, GT], I32)
        ctxv = sb("ctxv", [P, 2, GT, D + 1])
        xn3 = sb("xn3", [P, GT, D])
        qt3 = sb("qt3", [P, GW])
        qp = sb("qp", [P, 2, GW])
        sm = sb("sm", [P, 2, GT, S])
        smx = sb("smx", [P, GT])
        pr = sb("pr", [P, GT, S])
        prt = sb("prt", [P, 2, P])
        rsum = sb("rsum", [P, 2, GT])
        xn4 = sb("xn4", [P, GT, D])
        xt4 = sb("xt4", [P, GW])
        qbd = ht[:, :, :, :].rearrange("p q c n -> p q (c n)")
        zeros = xe[:, :, :, :].rearrange("p q t d -> p (q t d)")
        xo = mb[:, :, 0:GT * D].rearrange("p q (t d) -> p q t d", t=GT)
        xb = ex[:, :, 0:GT * D].rearrange("p q (t d) -> p q t d", t=GT)

        bank = [ctx.enter_context(nc.psum_tensor(f"bank{i}", [P, 512], F32)) for i in range(2)]
        heads = ctx.enter_context(nc.psum_tensor("heads", [P, 4, 512], F32))
        bank += [None] * 4 + [ctx.enter_context(nc.psum_tensor(f"bank{i}", [P, 512], F32)) for i in (6, 7)]

        par_in = sem("par_in")
        late_in = sem("late_in")
        cleared = sem("cleared")
        consts = sem("consts")
        dve_setup = sem("dve_setup")
        act_setup = sem("act_setup")
        pe_setup = sem("pe_setup")
        filled = sem("filled")
        x_in = [sem(f"x_in{i}") for i in range(2)]
        ctx_in = [sem(f"ctx_in{i}") for i in range(2)]
        vaug_done = sem("vaug_done")
        xt1_done = sem("xt1_done")
        ct_done = sem("ct_done")
        qt_done = sem("qt_done")
        qbd_done = sem("qbd_done")
        kt_done = sem("kt_done")
        kp_done = sem("kp_done")
        kpt_done = sem("kpt_done")
        gate_rows_ps = sem("gate_rows_ps")
        gate_rows_done = sem("gate_rows_done")
        gates_ps = sem("gates_ps")
        gate_steps = sem("gate_steps")
        gate_act = sem("gate_act")
        f_ps = sem("f_ps")
        a_done = sem("a_done")
        at_ps = sem("at_ps")
        mrow_done = sem("mrow_done")
        m_out = [sem(f"m_out{i}") for i in range(2)]
        m_in = [sem(f"m_in{i}") for i in range(2)]
        mt_ps = sem("mt_ps")
        mtok_done = sem("mtok_done")
        em_done = sem("em_done")
        l_done = sem("l_done")
        lcap_done = sem("lcap_done")
        ex_done = sem("ex_done")
        scores_done = sem("scores_done")
        cw_done = sem("cw_done")
        pv_done = sem("pv_done")
        sq_done = sem("sq_done")
        n_done = sem("n_done")
        z_done = sem("z_done")
        z_act = sem("z_act")
        hs_done = sem("hs_done")
        hsw_done = sem("hsw_done")
        x1_done = sem("x1_done")
        xt2_ps = sem("xt2_ps")
        xt2_done = sem("xt2_done")
        logit_rows_ps = sem("logit_rows_ps")
        logit_rows_done = sem("logit_rows_done")
        logits_ps = sem("logits_ps")
        route = sem("route")
        route_act = sem("route_act")
        onehot_done = sem("onehot_done")
        cum_ps = sem("cum_ps")
        slot_done = sem("slot_done")
        cum_used = sem("cum_used")
        read_done = sem("read_done")
        gwt_done = sem("gwt_done")
        scattered = [sem(f"scattered{i}") for i in range(2)]
        w_in = [sem(f"w_in{i}") for i in range(2)]
        xe_in = [sem(f"xe_in{i}") for i in range(2)]
        xet_ps = sem("xet_ps")
        xet_done = sem("xet_done")
        h_ps = sem("h_ps")
        h_done = sem("h_done")
        y_ps = sem("y_ps")
        y_done = sem("y_done")
        y_out = [sem(f"y_out{i}") for i in range(2)]
        kpr_in = [sem(f"kpr_in{i}") for i in range(2)]
        gix_done = sem("gix_done")
        yg_in = [sem(f"yg_in{i}") for i in range(2)]
        v_in = [sem(f"v_in{i}") for i in range(2)]
        x2_done = sem("x2_done")
        q3_ps = sem("q3_ps")
        q3_done = sem("q3_done")
        qp_ps = sem("qp_ps")
        qp_done = sem("qp_done")
        s3_ps = sem("s3_ps")
        sm_steps = sem("sm_steps")
        pr_done = sem("pr_done")
        prt_ps = sem("prt_ps")
        prt_done = sem("prt_done")
        o3_ps = sem("o3_ps")
        o3_steps = sem("o3_steps")
        x3_done = sem("x3_done")
        xb_done = sem("xb_done")
        xt4_ps = sem("xt4_ps")
        xt4_done = sem("xt4_done")
        f_out_ps = sem("f_out_ps")
        xo_done = sem("xo_done")
        stored = [sem(f"stored{i}") for i in range(2)]

        ln12, ln34 = (Norms(name, sb, sem, consts) for name in ("ln12", "ln34"))

        x_rows = x.rearrange("b s d -> (b s) d").rearrange("(t p) d -> p t d", p=P)
        ctx_rows = ctx_1024.rearrange("b s d -> (b s) d").rearrange("(t p) d -> p t d", p=P)
        out_rows = out.rearrange("b s d -> (b s) d").rearrange("(t p) d -> p t d", p=P)
        slots_rows = slots_x.rearrange("(t p) d -> p t d", p=P)
        y_rows = slots_y.rearrange("(t p) d -> p t d", p=P)
        w1_rows = w1.rearrange("e m f -> m e f")
        w2_rows = w2.rearrange("e (c f) m -> f e c m", f=P)

        def tiles(g):
            return bass.ds(g * GT, GT)

        def xtile(g):
            return lambda t: xs[:, bass.ds(g * GW + t * P, P)]

        def xgroup(g):
            return xs[:, bass.ds(g * GW, GW)]

        def one_row(v):
            return v.rearrange("(a n) -> a n", a=1)

        CONSTS = 22
        block = ctx.enter_context(nc.Block())

        setup_loads = [
            (kqkv[:, :, 0:NH], igate_kernel.rearrange("(k d) h -> d k h", k=3)),
            (kqkv[:, :, NH:], fgate_kernel.rearrange("(k d) h -> d k h", k=3)),
            (gate_bias[:, 0:NH], one_row(igate_bias).to_broadcast([P, NH])),
            (gate_bias[:, NH:], one_row(fgate_bias).to_broadcast([P, NH])),
            (gx[:, :], one_row(g_xattn).to_broadcast([P, 2])),
            (gf[:, :], one_row(g_ffn).to_broadcast([P, 2])),
            (rmsb[:, :], one_row(rms_scale).to_broadcast([P, HD])),
            (pw1_sb[:, :], pw1), (pw2_sb[:, :], pw2), (cb_sb[:, :], CB),
            (rows[0:E * FC, :], b1.rearrange("e (c f) -> (e c) f", f=P)),
            (rows[32:33, :], one_row(pb1)), (rows[33:34, :], one_row(pb2)), (rows[34:35, :], one_row(SCB)),
            (cbias_b[:, :], one_row(cbias).to_broadcast([P, P])),
        ]
        late_loads = [(wg_sb[:, :], wg), (mask[0:S, :], fside[0]), (mask[S:P, :], fside[0])]
        PARAMS = 16 * len(setup_loads)
        FILL = 2 * GW
        B1, PB1, PB2, SCBC = 0, 32, 33, 34
        assert E * FC == 32

        @block.sync
        def _(sp):
            def load(g, half, q):
                sp.dma_start(xgroup(g).rearrange("p (t d) -> p t d", t=GT), x_rows[:, tiles(g), :]).then_inc(x_in[q], 16)
                if not isinstance(g, int) or g >= 2:
                    hold(sp, ct_done, g - 1, consts)
                    hold(sp, vaug_done, g - 1, consts)
                sp.dma_start(ctxb[:, q, :, :], ctx_rows[:, tiles(g), :]).then_inc(ctx_in[q], 16)

            def spread_max(g, half, q):
                hold(sp, mrow_done, g + 1, consts)
                sp.dma_start(m_dram[q].rearrange("b (r i) -> r b i", i=S),
                             mrow[:, q, :].rearrange("r (b i) -> r b i", b=2)).then_inc(m_out[q], 16)
                hold(sp, m_out[q], half * 16 + 16, consts)
                hold(sp, l_done, g - 1, consts)
                for b in range(2):
                    sp.dma_start(mb[b * S:(b + 1) * S, q, :],
                                 m_dram[q][b:b + 1, :].to_broadcast([S, R * S])).then_inc(m_in[q], 16)

            load(0, 0, 0)
            sp.wait_ge(consts, 1)
            for dst, src in setup_loads:
                sp.dma_start(dst, src).then_inc(par_in, 16)
            load(1, 0, 1)
            for dst, src in late_loads:
                sp.dma_start(dst, src).then_inc(late_in, 16)
            sp.wait_ge(cleared, 1)
            for n in range(NT * D // FILL):
                per = FILL // D
                sp.dma_start(slots_rows[:, n * per:(n + 1) * per, :],
                             zeros.rearrange("p (t d) -> p t d", d=D)).then_inc(filled, 16)

            spread_max(0, 0, 0)
            load(2, 1, 0)
            spread_max(1, 0, 1)
            load(3, 1, 1)
            with sp.Fori(1, NG // 2 - 1) as half:
                spread_max(half * 2, half, 0)
                load(half * 2 + 2, half + 1, 0)
                spread_max(half * 2 + 1, half, 1)
                load(half * 2 + 3, half + 1, 1)
            spread_max(NG - 2, NG // 2 - 1, 0)
            spread_max(NG - 1, NG // 2 - 1, 1)

            for e in range(E):
                sp.dma_start(b2b[:, e, :], one_row(b2[e]).to_broadcast([P, D])).then_inc(par_in, 16)

            def load_w(e, half, q):
                hold(sp, y_ps, e * 2 - 2, consts)
                sp.dma_start(w1_sb[:, q, :], w1_rows[:, e, :]).then_inc(w_in[q], 16)
                sp.dma_start(w2_sb[:, q, :, :], w2_rows[:, e, :, :]).then_inc(w_in[q], 16)

            def load_xe(s, half, q):
                hold(sp, xet_ps, s - 1, consts)
                sp.dma_start(xe[:, q, :, :], slots_rows[:, tiles(s), :]).then_inc(xe_in[q], 16)

            def store_y(s, half, q):
                hold(sp, y_done, s + 1, consts)
                sp.dma_start(y_rows[:, tiles(s), :], ye[:, q, :, :]).then_inc(y_out[q], 16)

            load_w(0, 0, 0)
            load_w(1, 0, 1)
            for q in range(2):
                sp.wait_ge(scattered[q], 16 * GT * NG // 2)
            load_xe(0, 0, 0)
            load_xe(1, 0, 1)
            load_xe(2, 1, 0)
            with sp.Fori(0, E // 2 - 1) as quad:
                for j in range(4):
                    s = quad * 4 + j
                    load_xe(s + 3, None, (j + 1) % 2)
                    store_y(s, None, j % 2)
                    if j % 2:
                        load_w(quad * 2 + 2 + j // 2, None, j // 2)
            for s in range(NG - 4, NG):
                if s + 3 < NG:
                    load_xe(s + 3, None, (s + 1) % 2)
                store_y(s, None, s % 2)
            for q in range(2):
                sp.wait_ge(y_out[q], 16 * NG // 2)

            def load_v(g, half, q):
                hold(sp, o3_ps, g - 1, consts)
                sp.dma_start(ctxv[:, q, :, 0:D], ctx_rows[:, tiles(g), :]).then_inc(v_in[q], 16)
                sp.dma_start(kpr[:, q, :], kpt[:, bass.ds(g * GW, GW)]).then_inc(kpr_in[q], 16)

            def store(g, half, q):
                hold(sp, xo_done, g + 1, consts)
                sp.dma_start(out_rows[:, tiles(g), :], xo[:, q, :, :]).then_inc(stored[q], 16)

            load_v(0, 0, 0)
            load_v(1, 0, 1)
            load_v(2, 1, 0)
            with sp.Fori(0, NG // 2 - 2) as half:
                for q in range(2):
                    load_v(half * 2 + q + 3, half + 1 + q, 1 - q)
                    store(half * 2 + q, half, q)
            for g in range(NG - 4, NG):
                if g + 3 < NG:
                    load_v(g + 3, (g + 3) // 2, (g + 3) % 2)
                store(g, g // 2, g % 2)
            for q in range(2):
                sp.wait_ge(stored[q], 16 * NG // 2)

        @block.gpsimd
        def _(pool):
            done = 0

            def step(ins):
                nonlocal done
                done += 1
                ins.then_inc(consts, 1)
                pool.wait_ge(consts, done)

            step(pool.memset(rows[:, :], 0.0))
            step(pool.memset(ident[:, :], 0.0))
            step(pool.affine_select(out=ident[:, :], in_=ident[:, :], compare_op=ALU.not_equal, fill=1.0, base=0,
                                    pattern=[[-1, P]], channel_multiplier=1))
            step(pool.memset(tri[:, :], 1.0))
            step(pool.affine_select(out=tri[:, :], in_=tri[:, :], compare_op=ALU.is_ge, fill=0.0, base=0,
                                    pattern=[[1, P]], channel_multiplier=-1))
            step(pool.tensor_copy(tri_b[:, :], tri[:, :]))
            step(pool.memset(tri[0:S, S:P], 0.0))
            step(pool.memset(cap[:, :], 0.0))
            for b in range(2):
                half = cap[b * S:(b + 1) * S, :]
                step(pool.affine_select(out=half, in_=half, compare_op=ALU.is_ge, fill=MASKED, base=0,
                                        pattern=[[1, S]], channel_multiplier=-1))
            step(pool.memset(reset[:, :], 0.0))
            step(pool.memset(reset[:, :].rearrange("r (b i) -> r b i", b=2)[:, :, 0:1], -1e38))
            step(pool.memset(ones_b[:, :], 1.0))
            step(pool.memset(onehot[:, :, :], 0.0))
            step(pool.memset(vaug[:, :, :, :, HD:HA], 1.0))
            step(pool.memset(ctxv[:, :, :, D:D + 1], 1.0))
            step(pool.iota(prio_i[:, :], pattern=[[-1, E]], base=E, channel_multiplier=0))
            step(pool.iota(trash_i[:, :], pattern=[[P, NT]], base=N, channel_multiplier=1))
            step(pool.iota(carry_i[:, :], pattern=[[CAP, E]], base=-1, channel_multiplier=0))
            step(pool.tensor_copy(prio[:, :], prio_i[:, :]))
            step(pool.tensor_copy(trash[:, :], trash_i[:, :]))
            step(pool.tensor_copy(carry[:, 0, :], carry_i[:, :]))
            assert done == CONSTS

            def exponents(g, half, q):
                hold(pool, m_in[q], half * 32 + 32, consts)
                hold(pool, a_done, g + 1, consts)
                hold(pool, cw_done, nth(g - 1, 0, GT), consts)
                pool.tensor_tensor(ex[:, q, :].rearrange("p (r i) -> p r i", i=S),
                                   am[:, q, :].unsqueeze(2).to_broadcast([P, R, S]),
                                   mb[:, q, :].rearrange("p (r i) -> p r i", i=S),
                                   ALU.subtract).then_inc(l_done, 1)
                hold(pool, l_done, g + 1, consts)
                pool.tensor_tensor(ex[:, q, :].rearrange("p (r i) -> p r i", i=S),
                                   ex[:, q, :].rearrange("p (r i) -> p r i", i=S),
                                   cap[:, :].unsqueeze(1).to_broadcast([P, R, S]), ALU.add).then_inc(lcap_done, 1)

            def add_heads(g, half, q):
                hold(pool, hs_done, g + 1, consts)
                pool.tensor_tensor(hs[:, q, :, :], hs[:, q, :, :],
                                   head_w[:, :].unsqueeze(1).to_broadcast([P, GT, D]), ALU.mult).then_inc(hsw_done, 1)
                hold(pool, hsw_done, g + 1, consts)
                pool.tensor_tensor(xgroup(g), xgroup(g), hs[:, q, :, :].rearrange("p t d -> p (t d)"),
                                   ALU.add).then_inc(x1_done, 1)

            def scatter(g, half, q):
                hold(pool, slot_done, g + 1, consts)
                if isinstance(g, int) and g == 0:
                    pool.wait_ge(filled, 16 * (NT * D // FILL))
                for t in range(GT):
                    pool.indirect_dma_start(out=slots_x, out_offset=bass.IndirectOffsetOnAxis(ap=sidx[:, q, t:t + 1], axis=0),
                                            in_=xn2[:, q, t, :], in_offset=None).then_inc(scattered[q], 16)

            def first_pass(at):
                _, two, three, _, five = at
                if five:
                    scatter(*five)
                if two:
                    exponents(*two)
                if three:
                    add_heads(*three)

            over_groups(pool, NG, 5, first_pass)

            for q in range(2):
                pool.wait_ge(y_out[q], 16 * NG // 2)

            def gather(g, half, q):
                if isinstance(g, int) and g == 0:
                    pool.wait_ge(read_done, 2 * NG)
                hold(pool, x2_done, g - 1, consts)
                pool.tensor_copy(gix[:, q, :], gidx[:, tiles(g)]).then_inc(gix_done, 1)
                hold(pool, gix_done, g + 1, consts)
                for t in range(GT):
                    pool.indirect_dma_start(out=yg[:, q, t, :], out_offset=None, in_=slots_y,
                                            in_offset=bass.IndirectOffsetOnAxis(ap=gix[:, q, t:t + 1], axis=0)
                                            ).then_inc(yg_in[q], 16)

            def add_bias(g, half, q):
                hold(pool, x3_done, g + 1, consts)
                hold(pool, xo_done, g - 1, consts)
                pool.tensor_tensor(xb[:, q, :, :], xgroup(g).rearrange("p (t d) -> p t d", t=GT),
                                   fbias[:, :].unsqueeze(1).to_broadcast([P, GT, D]), ALU.add).then_inc(xb_done, 1)

            def last_pass(at):
                one, _, _, _, five = at
                if one:
                    gather(*one)
                if five:
                    add_bias(*five)

            over_groups(pool, NG, 5, last_pass)

        @block.scalar
        def _(act):
            act.wait_ge(par_in, PARAMS)
            act.activation(tx[:, :], gx[:, :], ACT.Tanh).then_inc(act_setup, 1)
            act.activation(tf[:, :], gf[:, :], ACT.Tanh).then_inc(act_setup, 1)

            def keys(g, half, q):
                act.wait_ge(ct_done, g + 1)
                act.activation(kt[:, q, :], bank[1][:, :], ACT.Copy).then_inc(kt_done, 1)

            def projected_keys(g, half, q):
                hold(act, kp_done, g + 1, consts)
                act.activation(kpt[:, bass.ds(g * GW, GW)], bank[1][:, :], ACT.Identity,
                               bias=pc[:, 0:1]).then_inc(kpt_done, 1)

            def values(g, half, q):
                act.wait_ge(ctx_in[q], half * 16 + 16)
                need(act, pv_done, nth(g - 2, GT, GT))
                act.activation(vaug[:, q, :, :, 0:HD], ctxb[:, q, :, :].rearrange("p t (h d) -> p t h d", h=NH),
                               ACT.Copy).then_inc(vaug_done, 1)

            def queries(g, half, q):
                act.wait_ge(xt1_done, g + 1)
                act.activation(qt[:, :], bank[0][:, :], ACT.Copy).then_inc(qt_done, 1)

            def norm1(g, half, q):
                need(act, xt1_done, g)
                ln12.act_apply(act, g, 0, lambda t: xn1[:, t, :], xtile(g))

            def gates_out(g, half, q):
                act.wait_ge(gate_rows_ps, g + 1)
                act.activation(gate_rows[:, :], bank[1][0:2 * NH, :], ACT.Copy).then_inc(gate_rows_done, 1)

            def logits_out(g, half, q):
                act.wait_ge(logit_rows_ps, g + 1)
                act.activation(logit_rows[:, :], bank[7][0:E, :], ACT.Copy).then_inc(logit_rows_done, 1)

            def queries_by_head(g, half, q):
                for h in range(NH):
                    hp = slice(h * HD, (h + 1) * HD)
                    act.activation(qbd[hp, q, :].rearrange("p (b h i) -> p b h i", b=BG, h=NH)[:, :, h, :],
                                   bank[0][hp, :].rearrange("p (b i) -> p b i", b=BG), ACT.Copy).then_inc(qbd_done, 1)

            def soft_part(g, half, q):
                act.wait_ge(gate_steps, nth(g, 2, 3))
                act.activation(eneg[:, :], negabs[:, :], ACT.Exp).then_inc(gate_act, 1)
                act.wait_ge(gate_act, nth(g, 1, 2))
                act.activation(softp[:, :], eneg[:, :], ACT.Ln, bias=1.0).then_inc(gate_act, 1)

            def exp_m(g, half, q):
                act.wait_ge(mtok_done, g + 1)
                need(act, n_done, nth(g - 2, 1, 4))
                act.activation(em[:, q, :], mtok[:, :], ACT.Exp, scale=-1.0).then_inc(em_done, 1)

            def decays(g, half, q):
                act.wait_ge(lcap_done, g + 1)
                act.activation(ex[:, q, :], ex[:, q, :], ACT.Exp).then_inc(ex_done, 1)

            def squares(g, half, q):
                act.wait_ge(n_done, nth(g, 1, 4))
                act.activation(sq[:, :, :, :],
                               heads[:, :, NH * S:NH * (S + HA)].rearrange("p t (h d) -> p t h d", d=HA)[:, :, :, 0:HD],
                               ACT.Square).then_inc(sq_done, 1)

            def rms_guess(g, half, q):
                act.wait_ge(z_done, nth(g, 1, 4))
                act.activation(zz[:, 1, :], zz[:, 0, :], ACT.Ln).then_inc(z_act, 1)
                act.wait_ge(z_act, nth(g, 1, 2))
                act.activation(zz[:, 2, :], zz[:, 1, :], ACT.Exp, scale=-0.5).then_inc(z_act, 1)

            def routed_rows(g, half, q):
                act.wait_ge(xt2_ps, g + 1)
                act.activation(xt2[:, :], bank[7][:, :], ACT.Copy).then_inc(xt2_done, 1)

            def route_exp(g, half, q):
                act.wait_ge(route, nth(g, 2, 6))
                act.activation(rt[:, 1, :, :], rt[:, 0, :, :], ACT.Exp).then_inc(route_act, 1)

            def first_pass(at):
                one, two, three, four = at
                if one:
                    keys(*one)
                norms = [(i,) for i, here in enumerate((one, four)) if here]
                if norms:
                    ln12.act_guess(act, step_of(at), norms)
                if two:
                    exp_m(*two)
                if one:
                    norm1(*one)
                if three:
                    squares(*three)
                if four:
                    routed_rows(*four)
                if one:
                    projected_keys(*one)
                if three:
                    rms_guess(*three)
                if two:
                    values(*two)
                if four:
                    logits_out(*four)
                if one:
                    queries(*one)
                if four:
                    route_exp(*four)
                if one:
                    gates_out(*one)
                if two:
                    decays(*two)
                if one:
                    soft_part(*one)
                    queries_by_head(*one)

            act.preload_act_table_set("natural_log_exp_and_others")
            act.wait_ge(cleared, 2)
            over_groups(act, NG, 4, first_pass)

            def gelu(s, e):
                for c in range(FC):
                    hold(act, h_ps, nth(s, c + 1, FC), consts)
                    if c == 0:
                        hold(act, y_ps, s - 1, consts)
                    col = cols[:, bass.ds(e * FC + c, 1)]
                    act.activation(ht[:, s_par, c, :], heads[:, c, :], ACT.Gelu_apprx_tanh,
                                   bias=col).then_inc(h_done, 1)

            s_par = 0
            for s in range(2):
                s_par = s
                gelu(s, 0)
            with act.Fori(1, E) as e:
                for j in range(2):
                    s_par = j
                    gelu(e * 2 + j, e)

            def queries3(g, half, q):
                act.wait_ge(q3_ps, g + 1)
                need(act, qp_ps, g)
                act.activation(qt3[:, :], bank[0][:, :], ACT.Copy).then_inc(q3_done, 1)

            def projected_queries(g, half, q):
                act.wait_ge(qp_ps, g + 1)
                act.activation(qp[:, q, :], bank[1][:, :], ACT.Identity, bias=pc[:, 0:1]).then_inc(qp_done, 1)

            def probabilities(g, half, q):
                act.wait_ge(sm_steps, nth(g, 3, 3))
                need(act, prt_ps, g)
                act.activation(pr[:, :, :], sm[:, 1, :, :], ACT.Exp).then_inc(pr_done, 1)

            def turned_probabilities(g, half, q):
                act.wait_ge(prt_ps, g + 1)
                need(act, o3_ps, g)
                act.activation(prt[:, :, :].rearrange("p u n -> p (u n)"), heads[:, 1, 0:2 * P], ACT.Copy).then_inc(prt_done, 1)

            def rows4(g, half, q):
                act.wait_ge(xt4_ps, g + 1)
                need(act, f_out_ps, g)
                act.activation(xt4[:, :], bank[6][:, :], ACT.Copy).then_inc(xt4_done, 1)

            def last_pass(at):
                one, two, three, four, five = at
                norms = [(i,) for i, here in enumerate((two, five)) if here]
                if four:
                    turned_probabilities(*four)
                if norms:
                    k = step_of(at[1:])
                    ln34.act_guess(act, k, norms)
                if three:
                    projected_queries(*three)
                if five:
                    need(act, xt4_ps, five[0])
                    ln34.act_apply(act, k, 1, lambda t: xn4[:, t, :], xtile(five[0]))
                if two:
                    need(act, q3_ps, two[0])
                    ln34.act_apply(act, k, 0, lambda t: xn3[:, t, :], xtile(two[0]))
                if five:
                    rows4(*five)
                if three:
                    probabilities(*three)
                if two:
                    queries3(*two)

            act.preload_act_table_set("natural_log_exp_and_others")
            over_groups(act, NG, 5, last_pass)

        @block.tensor
        def _(pe):
            pe.wait_ge(consts, CONSTS)
            pe.wait_ge(par_in, PARAMS)
            pe.transpose(bank[0][:, 0:40], rows[0:40, :], ident[0:40, 0:40]).then_inc(pe_setup, 1)
            pe.transpose(bank[0][:, 128:256], pw2_sb[:, :], ident[:, :]).then_inc(pe_setup, 1)
            pe.wait_ge(dve_setup, 8)
            pe.matmul(bank[0][:, 256:384], pw1_sb[:, :], pw2t[:, :], start=True, stop=True).then_inc(pe_setup, 1)
            pe.matmul(bank[1][:, 0:1], pw2t[:, :], cols[:, PB1:PB1 + 1], start=True, stop=True).then_inc(pe_setup, 1)
            pe.transpose(bank[1][:, 128:256], cbs[:, :], ident[:, :]).then_inc(pe_setup, 1)
            pe.wait_ge(dve_setup, 11)

            def keep_clock(b, n):
                for _ in range(n):
                    pe.matmul(bank[b][:, :], ones_b[:, :], ones_b[:, :].unsqueeze(1).to_broadcast([P, GT, P]),
                              start=True, stop=True)

            def turn_context(g, half, q):
                pe.wait_ge(ctx_in[q], half * 16 + 16)
                need(pe, gate_rows_done, g)
                for t in range(GT):
                    last = pe.transpose(bank[1][:, t * P:(t + 1) * P], ctxb[:, q, t, :], ident[:, :])
                last.then_inc(ct_done, 1)

            def project_keys(g, half, q):
                pe.wait_ge(kt_done, g + 1)
                pe.matmul(bank[1][:, :], pa[:, :], kt[:, q, :], start=True, stop=True).then_inc(kp_done, 1)

            def turn_queries(g, half, q):
                pe.wait_ge(ln12.applied[0], g + 1)
                need(pe, qbd_done, NH * g)
                for t in range(GT):
                    last = pe.transpose(bank[0][:, t * P:(t + 1) * P], xn1[:, t, :], ident[:, :])
                last.then_inc(xt1_done, 1)

            def gate_products(g, half, q):
                need(pe, kpt_done, g + 1)
                pe.matmul(bank[1][0:2 * NH, :], kc[:, :], kt[:, q, :], start=True, stop=False)
                pe.wait_ge(qt_done, g + 1)
                pe.matmul(bank[1][0:2 * NH, :], kqkv[:, 0, :], qt[:, :], start=False, stop=True).then_inc(gate_rows_ps, 1)

            def turn_gates(g, half, q):
                hold(pe, mtok_done, g, consts)
                hold(pe, gate_rows_done, g + 1, consts)
                for t in range(GT):
                    last = pe.transpose(bank[6][:, t * 2 * NH:(t + 1) * 2 * NH], gate_rows[:, t * P:(t + 1) * P],
                                        ident[0:2 * NH, 0:2 * NH])
                last.then_inc(gates_ps, 1)

            def forget_sums(g, half, q):
                pe.wait_ge(gate_steps, nth(g, 3, 3))
                pe.matmul(bank[6][:, 64:64 + R], tri[:, :], logf[:, :], start=True, stop=True).then_inc(f_ps, 1)

            def turn_a(g, half, q):
                pe.wait_ge(a_done, g + 1)
                pe.transpose(bank[6][0:R, 128:256], am[:, q, :], ident[:, :]).then_inc(at_ps, 1)

            def turn_maxima(g, half, q):
                hold(pe, mrow_done, g + 1, consts)
                pe.transpose(bank[6][:, 256:256 + R], mrow[:, q, :], ident[0:R, 0:R]).then_inc(mt_ps, 1)

            def scores(g, q, tiles_of):
                for t in tiles_of:
                    if t == 0:
                        pe.wait_ge(qbd_done, nth(g, NH, NH))
                        need(pe, hs_done, g)
                    for b in range(2 * t, 2 * t + 2):
                        last = pe.matmul(heads[(b % 2) * S:(b % 2 + 1) * S, t, 0:NH * S], kt[:, q, b * S:(b + 1) * S],
                                         qbd[:, q, b * NH * S:(b + 1) * NH * S], start=True, stop=True)
                    last.then_inc(scores_done, 1)

            def head_values(g, q, tiles_of):
                for t in tiles_of:
                    hold(pe, cw_done, nth(g, t + 1, GT), consts)
                    if t == 0:
                        pe.wait_ge(vaug_done, g + 1)
                    for h in range(NH):
                        for b in range(2):
                            bp = slice(b * S, (b + 1) * S)
                            last = pe.matmul(heads[bp, t, NH * S + h * HA:NH * S + (h + 1) * HA],
                                             cw[bp, t, h, :], vaug[bp, q, t, h, :], start=True, stop=True)
                    last.then_inc(pv_done, 1)

            def turn_routed(g, half, q):
                pe.wait_ge(ln12.applied[1], g + 1)
                need(pe, cum_used, g)
                for t in range(GT):
                    last = pe.transpose(bank[7][:, t * P:(t + 1) * P], xn2[:, q, t, :], ident[:, :])
                last.then_inc(xt2_ps, 1)

            def logits(g, half, q):
                if isinstance(g, int) and g == 0:
                    pe.wait_ge(late_in, 16 * len(late_loads))
                pe.wait_ge(xt2_done, g + 1)
                pe.matmul(bank[7][0:E, :], wg_sb[:, :], xt2[:, :], start=True, stop=True).then_inc(logit_rows_ps, 1)

            def turn_logits(g, half, q):
                hold(pe, logit_rows_done, g + 1, consts)
                for t in range(GT):
                    last = pe.transpose(bank[7][:, t * E:(t + 1) * E], logit_rows[:, t * P:(t + 1) * P], ident[0:E, 0:E])
                last.then_inc(logits_ps, 1)

            def count_tokens(g, half, q):
                pe.wait_ge(onehot_done, g + 1)
                W = (GT + 1) * E
                cum = bank[7][:, 128:128 + W]
                pe.matmul(cum, tri_b[:, :], onehot[:, :, :].rearrange("p t e -> p (t e)"), start=True, stop=False)
                for t in range(GT):
                    last = pe.matmul(cum[:, (t + 1) * E:W], ones_b[:, :],
                                     onehot[:, t:t + 1, :].to_broadcast([P, GT - t, E]),
                                     start=False, stop=(t == GT - 1))
                last.then_inc(cum_ps, 1)

            def first_pass(at):
                one, two, three, four = at
                if three:
                    scores(three[0], three[2], (0, 1))
                if two:
                    pe.wait_ge(gate_rows_done, two[0] + 1)
                    keep_clock(1, 2)
                if two:
                    forget_sums(*two)
                if three:
                    scores(three[0], three[2], (2, 3))
                if one:
                    turn_context(*one)
                if two:
                    turn_a(*two)
                if three:
                    head_values(three[0], three[2], (0, 1))
                if two:
                    turn_maxima(*two)
                if three:
                    head_values(three[0], three[2], (2, 3))
                if one:
                    project_keys(*one)
                if four:
                    turn_routed(*four)
                    logits(*four)
                if one:
                    turn_queries(*one)
                if four:
                    turn_logits(*four)
                if one:
                    gate_products(*one)
                if four:
                    count_tokens(*four)
                if one:
                    turn_gates(*one)

            over_groups(pe, NG, 4, first_pass)

            def turn_slots(s, half, q):
                pe.wait_ge(xe_in[q], half * 16 + 16)
                need(pe, xet_done, s)
                for t in range(GT):
                    last = pe.transpose(bank[0][:, t * P:(t + 1) * P], xe[:, q, t, :], ident[:, :])
                last.then_inc(xet_ps, 1)

            def up(s, wq):
                pe.wait_ge(xet_done, s + 1)
                for c in range(FC):
                    need(pe, h_done, nth(s - 1, c + 1, FC))
                    pe.matmul(heads[:, c, :], w1_sb[:, wq, c * P:(c + 1) * P], xet[:, :], start=True, stop=True).then_inc(h_ps, 1)

            def down(s, q, wq):
                pe.wait_ge(h_done, nth(s, FC, FC))
                need(pe, y_done, s)
                for t in range(GT):
                    for c in range(FC):
                        last = pe.matmul(bank[6][:, t * D:(t + 1) * D], ht[:, q, c, t * P:(t + 1) * P], w2_sb[:, wq, c, :],
                                         start=(c == 0), stop=(c == FC - 1))
                last.then_inc(y_ps, 1)

            def expert_quad(quad, first=False, last=False):
                for j in range(4):
                    s = quad * 4 + j
                    if j % 2 == 0:
                        pe.wait_ge(w_in[j // 2], quad * 32 + 32)
                    up(s, j // 2)
                    if not (last and j == 3):
                        turn_slots(s + 1, quad * 2 + (j + 1) // 2, (j + 1) % 2)
                    if not (first and j == 0):
                        down(s - 1, (j - 1) % 2, ((j - 1) % 4) // 2)

            need(pe, hs_done, NG)
            turn_slots(0, 0, 0)
            expert_quad(0, first=True)
            with pe.Fori(1, E // 2 - 1) as quad:
                expert_quad(quad)
            expert_quad(E // 2 - 1, last=True)
            down(NG - 1, 1, 1)

            def turn_queries3(g, half, q):
                pe.wait_ge(ln34.applied[0], g + 1)
                need(pe, q3_done, g)
                for t in range(GT):
                    last = pe.transpose(bank[0][:, t * P:(t + 1) * P], xn3[:, t, :], ident[:, :])
                last.then_inc(q3_ps, 1)

            def project_queries(g, half, q):
                pe.wait_ge(q3_done, g + 1)
                need(pe, qp_done, g)
                pe.matmul(bank[1][:, :], pa[:, :], qt3[:, :], start=True, stop=True).then_inc(qp_ps, 1)

            def scores3(g, half, q):
                pe.wait_ge(qp_done, g + 1)
                pe.wait_ge(kpr_in[q], half * 16 + 16)
                need(pe, sm_steps, nth(g - 1, 1, 3))
                for b in range(BG):
                    u, p, c = b // 4, b // 2 % 2, b % 2
                    last = pe.matmul(heads[p * S:(p + 1) * S, 0, (2 * u + c) * S:(2 * u + c + 1) * S],
                                     qp[:, q, b * S:(b + 1) * S], kpr[:, q, b * S:(b + 1) * S], start=True, stop=True)
                last.then_inc(s3_ps, 1)

            def turn_probabilities(g, half, q):
                pe.wait_ge(pr_done, g + 1)
                need(pe, prt_done, g)
                for u in range(2):
                    last = pe.transpose(heads[:, 1, u * P:(u + 1) * P],
                                        pr[:, 2 * u:2 * u + 2, :].rearrange("p c k -> p (c k)"), ident[:, :])
                last.then_inc(prt_ps, 1)

            def values3(g, half, q):
                hold(pe, v_in[q], half * 16 + 16, consts)
                hold(pe, x3_done, g, consts)
                hold(pe, prt_done, g + 1, consts)
                for b in range(BG):
                    u, p, c = b // 4, b // 2 % 2, b % 2
                    t = b // 2
                    cp = slice(c * S, (c + 1) * S)
                    last = pe.matmul(heads[cp, 2 + t // 2, (t % 2) * (D + 1):(t % 2 + 1) * (D + 1)],
                                     prt[cp, u, p * S:(p + 1) * S], ctxv[cp, q, t, :], start=True, stop=True)
                last.then_inc(o3_ps, 1)

            def turn_rows4(g, half, q):
                need(pe, xt4_done, g)
                keep_clock(6, 3)
                pe.wait_ge(ln34.applied[1], g + 1)
                for t in range(GT):
                    last = pe.transpose(bank[6][:, t * P:(t + 1) * P], xn4[:, t, :], ident[:, :])
                last.then_inc(xt4_ps, 1)

            def product4(g, half, q):
                pe.wait_ge(xt4_done, g + 1)
                need(pe, xo_done, g)
                for t in range(GT):
                    last = pe.matmul(bank[7][:, t * D:(t + 1) * D], xt4[:, t * P:(t + 1) * P], cbt[:, :], start=True, stop=True)
                last.then_inc(f_out_ps, 1)

            def last_pass(at):
                one, two, three, four, five = at
                if four:
                    turn_probabilities(*four)
                if three:
                    project_queries(*three)
                if four:
                    values3(*four)
                if three:
                    scores3(*three)
                if five:
                    turn_rows4(*five)
                if two:
                    turn_queries3(*two)
                if five:
                    product4(*five)

            over_groups(pe, NG, 5, last_pass)

        @block.vector
        def _(dve):
            dve.memset(zeros, 0.0).then_inc(cleared, 1)
            dve.memset(qbd, 0.0).then_inc(cleared, 1)
            dve.wait_ge(par_in, PARAMS)
            dve.tensor_tensor(kc[:, :], kqkv[:, 1, :], kqkv[:, 2, :], ALU.add).then_inc(dve_setup, 1)
            dve.wait_ge(act_setup, 2)
            dve.tensor_scalar(rmsw[:, :], rmsb[:, :], 1.0, tx[:, 0:1], ALU.add, ALU.mult).then_inc(dve_setup, 1)
            dve.wait_ge(dve_setup, 2)
            dve.tensor_copy(head_w[:, :].rearrange("p (h d) -> p h d", h=NH),
                            rmsw[:, :].unsqueeze(1).to_broadcast([P, NH, HD])).then_inc(dve_setup, 1)
            dve.tensor_scalar(fbias[:, :], cbias_b[:, :], tf[:, 1:2], None, ALU.mult).then_inc(dve_setup, 1)
            dve.wait_ge(pe_setup, 2)
            dve.tensor_copy(cols[:, :], bank[0][:, 0:40]).then_inc(dve_setup, 1)
            dve.tensor_copy(pw2t[:, :], bank[0][:, 128:256]).then_inc(dve_setup, 1)
            dve.wait_ge(dve_setup, 5)
            dve.tensor_scalar(scb_t[:, :], cols[:, SCBC:SCBC + 1], 1.0 / 127.0, tf[:, 1:2], ALU.mult, ALU.mult).then_inc(dve_setup, 1)
            dve.wait_ge(dve_setup, 7)
            dve.tensor_scalar(cbs[:, :], cb_sb[:, :], scb_t[:, 0:1], None, ALU.mult).then_inc(dve_setup, 1)
            dve.wait_ge(pe_setup, 5)
            dve.tensor_copy(pa[:, :], bank[0][:, 256:384]).then_inc(dve_setup, 1)
            dve.tensor_tensor(pc[:, :], bank[1][:, 0:1], cols[:, PB2:PB2 + 1], ALU.add).then_inc(dve_setup, 1)
            dve.tensor_copy(cbt[:, :], bank[1][:, 128:256]).then_inc(dve_setup, 1)

            def gate_values(g, half, q):
                dve.wait_ge(gates_ps, g + 1)
                dve.tensor_tensor(gates[:, :, :].rearrange("p k (t h) -> p k t h", t=GT),
                                  bank[6][:, 0:2 * R].rearrange("p (t k h) -> p k t h", t=GT, k=2),
                                  gate_bias[:, :].rearrange("p (k h) -> p k h", k=2).unsqueeze(2).to_broadcast([P, 2, GT, NH]),
                                  ALU.add).then_inc(gate_steps, 1)
                dve.wait_ge(gate_steps, nth(g, 1, 3))
                dve.scalar_tensor_tensor(out=negabs[:, :], in0=gates[:, 1, :], scalar=-1.0, in1=gates[:, 1, :],
                                         op0=ALU.mult, op1=ALU.min).then_inc(gate_steps, 1)

            def log_forget(g, half, q):
                dve.wait_ge(gate_act, nth(g, 2, 2))
                dve.scalar_tensor_tensor(out=logf[:, :], in0=gates[:, 1, :], scalar=0.0, in1=softp[:, :],
                                         op0=ALU.min, op1=ALU.subtract).then_inc(gate_steps, 1)

            def a_values(g, half, q):
                dve.wait_ge(f_ps, g + 1)
                dve.tensor_copy(fcum[:, :], bank[6][:, 64:64 + R]).then_inc(gate_copy, 1)
                dve.wait_ge(gate_copy, g + 1)
                need(dve, l_done, g - 1)
                dve.tensor_tensor(am[:, q, :], gates[:, 0, :], fcum[:, :], ALU.subtract).then_inc(a_done, 1)

            def running_max(g, half, q):
                dve.wait_ge(at_ps, g + 1)
                if not isinstance(g, int) or g >= 2:
                    dve.wait_ge(m_out[q], half * 16)
                dve.tensor_tensor_scan(mrow[:, q, :], reset[:, :], bank[6][0:R, 128:256], 0.0, ALU.add, ALU.max).then_inc(mrow_done, 1)

            def max_by_token(g, half, q):
                dve.wait_ge(mt_ps, g + 1)
                dve.tensor_tensor(mtok[:, :], bank[6][:, 256:256 + R], fcum[:, :], ALU.add).then_inc(mtok_done, 1)

            def decayed_scores(g, q, tiles_of):
                for t in tiles_of:
                    if t == 0:
                        dve.wait_ge(ex_done, g + 1)
                    dve.wait_ge(scores_done, nth(g, t + 1, GT))
                    need(dve, pv_done, nth(g - 1, t + 1, GT))
                    dve.scalar_tensor_tensor(out=cw[:, t, :, :].rearrange("p h i -> p (h i)"), in0=heads[:, t, 0:NH * S],
                                             scalar=float(HD) ** -0.5, in1=ex[:, q, t * NH * S:(t + 1) * NH * S],
                                             op0=ALU.mult, op1=ALU.mult).then_inc(cw_done, 1)

            def normalisers(g, half, q):
                dve.wait_ge(pv_done, nth(g, GT, GT))
                dve.wait_ge(em_done, g + 1)
                o4 = heads[:, :, NH * S:NH * (S + HA)].rearrange("p t (h d) -> p t h d", d=HA)
                dve.tensor_tensor(nn[:, 0, :].rearrange("p (t h) -> p t h", t=GT), o4[:, :, :, HD],
                                  em[:, q, :].rearrange("p (t h) -> p t h", t=GT), ALU.max).then_inc(n_done, 1)
                dve.wait_ge(n_done, nth(g, 1, 4))
                dve.tensor_scalar(nn[:, 1, :], nn[:, 0, :], 1e-6, None, ALU.add).then_inc(n_done, 1)
                dve.wait_ge(n_done, nth(g, 2, 4))
                dve.scalar_tensor_tensor(out=nn[:, 2, :], in0=nn[:, 1, :], scalar=1e-6, in1=nn[:, 1, :],
                                         op0=ALU.mult, op1=ALU.mult).then_inc(n_done, 1)

            def mean_squares(g, half, q):
                dve.wait_ge(sq_done, g + 1)
                dve.tensor_reduce(ss[:, :].rearrange("p (t h) -> p t h", t=GT), sq[:, :, :, :], AX, ALU.add).then_inc(n_done, 1)
                dve.wait_ge(n_done, nth(g, 4, 4))
                dve.scalar_tensor_tensor(out=zz[:, 0, :], in0=ss[:, :], scalar=1.0 / HD, in1=nn[:, 2, :],
                                         op0=ALU.mult, op1=ALU.add).then_inc(z_done, 1)

            def rms_newton(g, step):
                if step == 1:
                    dve.wait_ge(z_act, nth(g, 2, 2))
                    dve.tensor_tensor(zz[:, 3, :], zz[:, 2, :], zz[:, 2, :], ALU.mult).then_inc(z_done, 1)
                    return
                dve.wait_ge(z_done, nth(g, step, 4))
                if step == 2:
                    dve.scalar_tensor_tensor(out=zz[:, 4, :], in0=zz[:, 3, :], scalar=-0.5, in1=zz[:, 0, :],
                                             op0=ALU.mult, op1=ALU.mult).then_inc(z_done, 1)
                else:
                    dve.scalar_tensor_tensor(out=zz[:, 5, :], in0=zz[:, 4, :], scalar=1.5, in1=zz[:, 2, :],
                                             op0=ALU.add, op1=ALU.mult).then_inc(z_done, 1)

            def scaled_heads(g, half, q):
                dve.wait_ge(z_done, nth(g, 4, 4))
                need(dve, x1_done, g - 1)
                for t in range(GT):
                    last = dve.tensor_tensor(hs[:, q, t, :].rearrange("p (h d) -> p h d", h=NH),
                                             heads[:, t, NH * S:NH * (S + HA)].rearrange("p (h d) -> p h d", d=HA)[:, :, 0:HD],
                                             zz[:, 5, t * NH:(t + 1) * NH].unsqueeze(2).to_broadcast([P, NH, HD]), ALU.mult)
                last.then_inc(hs_done, 1)

            def norm2(k, g, half, q):
                if not isinstance(g, int) or g >= 2:
                    dve.wait_ge(scattered[q], half * (16 * GT))
                ln12.dve_apply(dve, k, 1, lambda t: xn2[:, q, t, :], xtile(g))

            def choose(g, step):
                lg = bank[7][:, 0:GT * E].rearrange("p (t e) -> p t e", t=GT)
                if step == 1:
                    dve.wait_ge(logits_ps, g + 1)
                    dve.tensor_reduce(rs[:, 8, :], lg, AX, ALU.max).then_inc(route, 1)
                    return
                dve.wait_ge(route, nth(g, step - 1, 6))
                if step == 2:
                    dve.tensor_tensor(rt[:, 0, :, :], lg, rs[:, 8, :].unsqueeze(2).to_broadcast([P, GT, E]), ALU.subtract).then_inc(route, 1)
                elif step == 3:
                    dve.scalar_tensor_tensor(out=rt[:, 2, :, :], in0=rt[:, 0, :, :], scalar=0.0,
                                             in1=prio[:, :].unsqueeze(1).to_broadcast([P, GT, E]),
                                             op0=ALU.is_ge, op1=ALU.mult).then_inc(route, 1)
                elif step == 4:
                    dve.tensor_reduce(rs[:, 1, :], rt[:, 2, :, :], AX, ALU.max).then_inc(route, 1)
                else:
                    dve.tensor_tensor(onehot[:, 0:GT, :], rt[:, 2, :, :],
                                      rs[:, 1, :].unsqueeze(2).to_broadcast([P, GT, E]), ALU.is_equal).then_inc(onehot_done, 1)
                    dve.tensor_scalar(rs[:, 3, :], rs[:, 1, :], -float(CAP), float((E + 1) * CAP), ALU.mult, ALU.add).then_inc(limit_done, 1)

            def count(g, half, q):
                dve.wait_ge(cum_ps, g + 1)
                cum = bank[7][:, 128:128 + (GT + 1) * E].rearrange("p (t e) -> p t e", e=E)
                dve.tensor_tensor(rt[:, 3, :, :], cum[:, 0:GT, :], carry[:, q:q + 1, :].to_broadcast([P, GT, E]), ALU.add).then_inc(slot_steps, 1)
                dve.tensor_tensor(carry[:, 1 - q, :], cum[:, GT, :], carry[:, q, :], ALU.add).then_inc(cum_used, 1)

            def place(g, half, q):
                dve.wait_ge(route_act, g + 1)
                dve.tensor_reduce(rs[:, 9, :], rt[:, 1, :, :], AX, ALU.add).then_inc(route, 1)
                dve.wait_ge(slot_steps, nth(g, 1, 6))
                dve.tensor_tensor(rt[:, 4, :, :], rt[:, 3, :, :], onehot[:, 0:GT, :], ALU.mult).then_inc(slot_steps, 1)
                dve.wait_ge(route, nth(g, 5, 6))
                dve.reciprocal(rs[:, 2, :], rs[:, 9, :]).then_inc(route, 1)
                dve.wait_ge(slot_steps, nth(g, 2, 6))
                slot, limit, beyond = rs[:, 0, :], rs[:, 3, :], rs[:, 7, :]
                dve.tensor_reduce(slot, rt[:, 4, :, :], AX, ALU.add).then_inc(slot_steps, 1)
                dve.wait_ge(slot_steps, nth(g, 3, 6))
                dve.wait_ge(limit_done, g + 1)
                dve.tensor_tensor(beyond, slot, limit, ALU.subtract).then_inc(slot_steps, 1)
                dve.tensor_tensor(rs[:, 5, :], slot, trash[:, tiles(g)], ALU.subtract).then_inc(slot_steps, 1)
                dve.wait_ge(slot_steps, nth(g, 5, 6))
                dve.scalar_tensor_tensor(out=rs[:, 6, :], in0=beyond, scalar=0.0, in1=rs[:, 5, :],
                                         op0=ALU.is_lt, op1=ALU.mult).then_inc(slot_steps, 1)
                dve.scalar_tensor_tensor(out=gidx[:, tiles(g)], in0=beyond, scalar=-1.0, in1=limit,
                                         op0=ALU.min, op1=ALU.add).then_inc(read_done, 1)
                dve.wait_ge(route, nth(g, 6, 6))
                dve.scalar_tensor_tensor(out=gw[:, tiles(g)], in0=beyond, scalar=0.0, in1=rs[:, 2, :],
                                         op0=ALU.is_lt, op1=ALU.mult).then_inc(read_done, 1)
                dve.wait_ge(slot_steps, nth(g, 6, 6))
                dve.tensor_tensor(sidx[:, q, :], rs[:, 6, :], trash[:, tiles(g)], ALU.add).then_inc(slot_done, 1)

            def first_pass(at):
                one, two, three, four = at
                norms = []
                if one:
                    hold(dve, x_in[one[2]], one[1] * 16 + 16, consts)
                    ln12.dve_stats(dve, 0, xtile(one[0]))
                    norms.append((0, one[0]))
                if two:
                    log_forget(*two)
                if three:
                    decayed_scores(three[0], three[2], (0, 1))
                if two:
                    a_values(*two)
                if four:
                    hold(dve, x1_done, four[0] + 1, consts)
                    ln12.dve_stats(dve, 1, xtile(four[0]))
                    norms.append((1, four[0]))
                if norms:
                    ln12.dve_moments(dve, step_of(at), norms)
                if two:
                    running_max(*two)
                if three:
                    decayed_scores(three[0], three[2], (2, 3))
                if two:
                    max_by_token(*two)
                if norms:
                    ln12.dve_newton(dve, step_of(at), norms)
                if one:
                    ln12.dve_shift(dve, one[0], [(0, one[0])])
                if four:
                    norm2(step_of(at), *four)
                if three:
                    normalisers(*three)
                    mean_squares(*three)
                    for i in range(1, 4):
                        rms_newton(three[0], i)
                    scaled_heads(*three)
                if four:
                    for i in range(1, 6):
                        choose(four[0], i)
                    count(*four)
                if four:
                    place(*four)
                if one:
                    gate_values(*one)

            gate_copy = sem("gate_copy")
            slot_steps = sem("slot_steps")
            limit_done = sem("limit_done")
            dve.wait_ge(consts, CONSTS)
            over_groups(dve, NG, 4, first_pass)

            dve.wait_ge(par_in, PARAMS + 16 * E)

            def evac_x(s):
                dve.wait_ge(xet_ps, s + 1)
                need(dve, h_ps, nth(s - 1, FC, FC))
                dve.tensor_copy(xet[:, :], bank[0][:, :]).then_inc(xet_done, 1)

            def evac_y(s, q, e):
                dve.wait_ge(y_ps, s + 1)
                if not isinstance(e, int) or e >= 1:
                    dve.wait_ge(y_out[q], e * 16)
                dve.tensor_tensor(ye[:, q, :, :], bank[6][:, :].rearrange("p (t d) -> p t d", t=GT),
                                  b2b[:, bass.ds(e, 1), :].to_broadcast([P, GT, D]), ALU.add).then_inc(y_done, 1)

            evac_x(0)
            evac_x(1)
            for q in range(2):
                evac_x(2 + q)
                evac_y(q, q, 0)
            with dve.Fori(2, E) as e:
                for q in range(2):
                    evac_x(e * 2 + q)
                    evac_y(e * 2 - 2 + q, q, e - 1)
            for q in range(2):
                evac_y(NG - 2 + q, q, E - 1)

            o3 = heads[:, 2:4, 0:2 * (D + 1)].rearrange("p b (t d) -> p b t d", d=D + 1)
            dve.wait_ge(late_in, 16 * len(late_loads))
            dve.wait_ge(read_done, 2 * NG)
            dve.tensor_scalar(gwt[:, :], gw[:, :], tf[:, 0:1], None, ALU.mult).then_inc(gwt_done, 1)
            dve.wait_ge(gwt_done, 1)

            def add_experts(g, half, q):
                dve.wait_ge(yg_in[q], half * (16 * GT) + 16 * GT)
                for t in range(GT):
                    last = dve.scalar_tensor_tensor(out=xtile(g)(t), in0=yg[:, q, t, :], scalar=gwt[:, bass.ds(g * GT + t, 1)],
                                                    in1=xtile(g)(t), op0=ALU.mult, op1=ALU.add)
                last.then_inc(x2_done, 1)

            def exponents3(g, half, q):
                dve.wait_ge(s3_ps, g + 1)
                dve.scalar_tensor_tensor(out=sm[:, 0, :, :], in0=heads[:, 0, 0:GT * S].rearrange("p (c k) -> p c k", k=S),
                                         scalar=float(D) ** -0.5, in1=mask[:, :].unsqueeze(1).to_broadcast([P, GT, S]),
                                         op0=ALU.mult, op1=ALU.add).then_inc(sm_steps, 1)
                dve.wait_ge(sm_steps, nth(g, 1, 3))
                dve.tensor_reduce(smx[:, :], sm[:, 0, :, :], AX, ALU.max).then_inc(sm_steps, 1)
                dve.wait_ge(sm_steps, nth(g, 2, 3))
                need(dve, pr_done, g)
                dve.tensor_tensor(sm[:, 1, :, :], sm[:, 0, :, :], smx[:, :].unsqueeze(2).to_broadcast([P, GT, S]),
                                  ALU.subtract).then_inc(sm_steps, 1)

            def attention_sums(g, half, q):
                dve.wait_ge(o3_ps, g + 1)
                dve.reciprocal(rsum[:, 0, :].rearrange("p (b t) -> p b t", b=2), o3[:, :, :, D]).then_inc(o3_steps, 1)
                dve.wait_ge(o3_steps, nth(g, 1, 2))
                dve.tensor_scalar(rsum[:, 1, :], rsum[:, 0, :], tx[:, 1:2], None, ALU.mult).then_inc(o3_steps, 1)

            def add_attention(g, half, q):
                dve.wait_ge(o3_steps, nth(g, 2, 2))
                for t in range(GT):
                    last = dve.scalar_tensor_tensor(out=xtile(g)(t), in0=o3[:, t // 2, t % 2, 0:D], scalar=rsum[:, 1, t:t + 1],
                                                    in1=xtile(g)(t), op0=ALU.mult, op1=ALU.add)
                last.then_inc(x3_done, 1)

            def outputs(g, half, q):
                dve.wait_ge(f_out_ps, g + 1)
                dve.wait_ge(xb_done, g + 1)
                if not isinstance(g, int) or g >= 2:
                    dve.wait_ge(stored[q], half * 16)
                dve.tensor_tensor(xo[:, q, :, :], bank[7][:, :].rearrange("p (t d) -> p t d", t=GT), xb[:, q, :, :],
                                  ALU.add).then_inc(xo_done, 1)

            def last_pass(at):
                _, two, three, four, five, six = at
                norms = []
                if two:
                    add_experts(*two)
                if five:
                    hold(dve, x3_done, five[0] + 1, consts)
                    ln34.dve_stats(dve, 1, xtile(five[0]))
                if two:
                    hold(dve, x2_done, two[0] + 1, consts)
                    ln34.dve_stats(dve, 0, xtile(two[0]))
                    norms.append((0, two[0]))
                if five:
                    norms.append((1, five[0]))
                if norms:
                    k = step_of(at[1:5])
                    ln34.dve_moments(dve, k, norms)
                if six:
                    outputs(*six)
                if norms:
                    ln34.dve_newton(dve, k, norms)
                    ln34.dve_shift(dve, k, norms)
                if four:
                    attention_sums(*four)
                if three:
                    exponents3(*three)
                if four:
                    add_attention(*four)

            over_groups(dve, NG, 6, last_pass)


_INS = ['x', 'ctx_1024', 'fside_1xSxS2_0', 'g_xattn', 'g_ffn', 'L0_xattn_igate_kernel', 'L0_xattn_igate_bias',
        'L0_xattn_fgate_kernel', 'L0_xattn_fgate_bias', 'L0_xattn_rms_scale', 'L0_ffn_wg', 'L0_ffn_w1', 'L0_ffn_b1',
        'L0_ffn_w2', 'L0_ffn_b2', 'L1_xattn_W1', 'L1_xattn_b1', 'L1_xattn_W2', 'L1_xattn_b2', 'L1_ffn_CB',
        'L1_ffn_SCB', 'L1_ffn_bias']
_OUTS = [((128, 64, 128), 'float32')]


def kernel(**inputs):
    import numpy as _np
    import concourse.bacc as _bacc
    from concourse import mybir as _mybir
    from concourse.bass_utils import run_bass_kernel_spmd as _run

    nc = _bacc.Bacc("TRN2", target_bir_lowering=False, num_devices=1)
    arrays, args = {}, []
    for name in _INS:
        a = _np.ascontiguousarray(inputs[name])
        arrays[f"in_{name}_dram"] = a
        args.append(nc.dram_tensor(f"in_{name}_dram", a.shape, _mybir.dt.from_np(a.dtype), kind="ExternalInput").ap())
    for i, (shape, dtype) in enumerate(_OUTS):
        dt = _mybir.dt.from_np(_np.dtype(dtype))
        args.append(nc.dram_tensor(f"out_{i}_dram", shape, dt, kind="ExternalOutput").ap())
    flamingo(nc, *args)
    r = _run(nc, [arrays], core_ids=[0])
    return r.results[0]["out_0_dram"]
```
